# Optimizing a Trainium2 kernel written in Bass

```python
import numpy as np
import jax
import jax.numpy as jnp

def _softmax(x, axis=-1):
    return jax.nn.softmax(x, axis=axis)

def _gelu(x):
    return jax.nn.gelu(x, approximate=True)

def _silu(x):
    return jax.nn.silu(x)

def _sigmoid(x):
    return jax.nn.sigmoid(x)

def _layernorm(x, axis=-1, eps=1e-05):
    m = jnp.mean(x, axis=axis, keepdims=True)
    v = jnp.var(x, axis=axis, keepdims=True)
    return (x - m) / jnp.sqrt(v + eps)

def _scatter_add(tgt, idx, src, axis=0):
    return tgt.at[idx].add(src)

def _segment_sum(src, seg, n):
    return jax.ops.segment_sum(src, seg, n)
kernel_name = 'mk_macaron_d1_jaxref_r8_6e2d94'

def setup_inputs(seed: int=0):
    np.random.seed(seed)
    _w = jnp.asarray

    def _L0_attn_setup():
        import jax, jax.numpy as jnp
        import numpy as np
        import math
        DIM = 128
        HEADS = 16
        HEAD_DIM = DIM // HEADS
        FFN_DIM = 512
        WINDOW = 125
        B, T = (2, 256)

        def _layernorm(x, w, b, eps=1e-05):
            mu = jnp.mean(x, axis=-1, keepdims=True)
            var = jnp.var(x, axis=-1, keepdims=True)
            return (x - mu) / jnp.sqrt(var + eps) * w + b

        def _rotate_half(x):
            x1, x2 = jnp.split(x, 2, axis=-1)
            return jnp.concatenate([-x2, x1], axis=-1)

        def _rope_tables(seq_len, dim, theta=10000.0):
            inv_freq = 1.0 / theta ** (jnp.arange(0, dim, 2, dtype=jnp.float32) / dim)
            t = jnp.arange(seq_len, dtype=jnp.float32)
            freqs = jnp.outer(t, inv_freq)
            emb = jnp.concatenate([freqs, freqs], axis=-1)
            return (jnp.cos(emb), jnp.sin(emb))

        def _block(x, norm1_w, norm1_b, norm2_w, norm2_b, wq, wk, wv, wo, w1, b1, w2, b2, ls1, ls2):
            Bx, Tx, D = x.shape
            h = _layernorm(x, norm1_w, norm1_b)

            def proj(w):
                y = jnp.einsum('btd,ed->bte', h, w)
                return y.reshape(Bx, Tx, HEADS, HEAD_DIM).transpose(0, 2, 1, 3)
            Q, K, V = (proj(wq), proj(wk), proj(wv))
            cos, sin = _rope_tables(Tx, HEAD_DIM)
            cos = cos[None, None]
            sin = sin[None, None]
            Q = Q * cos + _rotate_half(Q) * sin
            K = K * cos + _rotate_half(K) * sin
            idx = jnp.arange(Tx)
            diff = idx[:, None] - idx[None, :]
            mask = jnp.where((diff >= 0) & (diff < WINDOW), 0.0, -jnp.inf)
            scale = math.sqrt(HEAD_DIM)
            scores = jnp.einsum('bhtd,bhsd->bhts', Q, K) / scale + mask[None, None]
            attn = jax.nn.softmax(scores, axis=-1)
            attn_out = jnp.einsum('bhts,bhsd->bhtd', attn, V)
            attn_out = attn_out.transpose(0, 2, 1, 3).reshape(Bx, Tx, D)
            x = x + jnp.einsum('btd,ed->bte', attn_out, wo) * ls1
            h2 = _layernorm(x, norm2_w, norm2_b)
            f = jax.nn.gelu(jnp.einsum('btd,fd->btf', h2, w1) + b1, approximate=False)
            f = jnp.einsum('btf,df->btd', f, w2) + b2
            x = x + f * ls2
            return x
        key = jax.random.key(seed)
        ks = jax.random.split(key, 12)
        s = 0.02
        return {'x': jax.random.normal(ks[0], (B, T, DIM), dtype=jnp.float32), 'norm1_w': jnp.ones((DIM,), jnp.float32), 'norm1_b': jnp.zeros((DIM,), jnp.float32), 'norm2_w': jnp.ones((DIM,), jnp.float32), 'norm2_b': jnp.zeros((DIM,), jnp.float32), 'wq': jax.random.normal(ks[1], (DIM, DIM), jnp.float32) * s, 'wk': jax.random.normal(ks[2], (DIM, DIM), jnp.float32) * s, 'wv': jax.random.normal(ks[3], (DIM, DIM), jnp.float32) * s, 'wo': jax.random.normal(ks[4], (DIM, DIM), jnp.float32) * s, 'w1': jax.random.normal(ks[5], (FFN_DIM, DIM), jnp.float32) * s, 'b1': jnp.zeros((FFN_DIM,), jnp.float32), 'w2': jax.random.normal(ks[6], (DIM, FFN_DIM), jnp.float32) * s, 'b2': jnp.zeros((DIM,), jnp.float32), 'ls1': jnp.full((DIM,), 0.01, jnp.float32), 'ls2': jnp.full((DIM,), 0.01, jnp.float32)}
    _L0_attn_in = _L0_attn_setup()

    def _L0_ffn_setup():
        import jax, jax.numpy as jnp
        import numpy as np
        DIM = 128
        HID = 512
        NUM_EXPERTS = 8
        TOP_K = 2
        ALPHA = 2.0
        B, S = (4, 256)

        def _swiglu(x, wu, wg, wd):
            up = x @ wu
            g = x @ wg
            gate = jax.nn.sigmoid(g) * g
            return up * gate @ wd
        key = jax.random.key(seed)
        ks = jax.random.split(key, 8)
        x = jax.random.normal(ks[0], (B, S, DIM), dtype=jnp.float32)
        Wr = jax.random.normal(ks[1], (DIM, NUM_EXPERTS), dtype=jnp.float32) * 0.02
        Wu = jax.random.normal(ks[2], (NUM_EXPERTS - 1, DIM, HID), dtype=jnp.float32) * 0.02
        Wg = jax.random.normal(ks[3], (NUM_EXPERTS - 1, DIM, HID), dtype=jnp.float32) * 0.02
        Wd = jax.random.normal(ks[4], (NUM_EXPERTS - 1, HID, DIM), dtype=jnp.float32) * 0.002
        Wu_s = jax.random.normal(ks[5], (DIM, HID), dtype=jnp.float32) * 0.02
        Wg_s = jax.random.normal(ks[6], (DIM, HID), dtype=jnp.float32) * 0.02
        Wd_s = jax.random.normal(ks[7], (HID, DIM), dtype=jnp.float32) * 0.002
        return {'x': x, 'Wr': Wr, 'Wu': Wu, 'Wg': Wg, 'Wd': Wd, 'Wu_s': Wu_s, 'Wg_s': Wg_s, 'Wd_s': Wd_s}
    _L0_ffn_in = _L0_ffn_setup()
    _d = {'L0_attn_x': _L0_attn_in['x'], 'L0_attn_norm1_w': _L0_attn_in['norm1_w'], 'L0_attn_norm1_b': _L0_attn_in['norm1_b'], 'L0_attn_norm2_w': _L0_attn_in['norm2_w'], 'L0_attn_norm2_b': _L0_attn_in['norm2_b'], 'L0_attn_wq': _L0_attn_in['wq'], 'L0_attn_wk': _L0_attn_in['wk'], 'L0_attn_wv': _L0_attn_in['wv'], 'L0_attn_wo': _L0_attn_in['wo'], 'L0_attn_w1': _L0_attn_in['w1'], 'L0_attn_b1': _L0_attn_in['b1'], 'L0_attn_w2': _L0_attn_in['w2'], 'L0_attn_b2': _L0_attn_in['b2'], 'L0_attn_ls1': _L0_attn_in['ls1'], 'L0_attn_ls2': _L0_attn_in['ls2'], 'L0_ffn_Wr': _L0_ffn_in['Wr'], 'L0_ffn_Wu': _L0_ffn_in['Wu'], 'L0_ffn_Wg': _L0_ffn_in['Wg'], 'L0_ffn_Wd': _L0_ffn_in['Wd'], 'L0_ffn_Wu_s': _L0_ffn_in['Wu_s'], 'L0_ffn_Wg_s': _L0_ffn_in['Wg_s'], 'L0_ffn_Wd_s': _L0_ffn_in['Wd_s']}
    _x0 = _d['L0_attn_x']
    _d['L0_attn_x'] = jax.random.normal(jax.random.fold_in(jax.random.key(seed), 1), (1, 2048, 128), dtype=_x0.dtype)
    del _x0
    return _d

def reference(L0_attn_x, L0_attn_norm1_w, L0_attn_norm1_b, L0_attn_norm2_w, L0_attn_norm2_b, L0_attn_wq, L0_attn_wk, L0_attn_wv, L0_attn_wo, L0_attn_w1, L0_attn_b1, L0_attn_w2, L0_attn_b2, L0_attn_ls1, L0_attn_ls2, L0_ffn_Wr, L0_ffn_Wu, L0_ffn_Wg, L0_ffn_Wd, L0_ffn_Wu_s, L0_ffn_Wg_s, L0_ffn_Wd_s):

    def _L0_attn_ref(x, norm1_w, norm1_b, norm2_w, norm2_b, wq, wk, wv, wo, w1, b1, w2, b2, ls1, ls2):
        import jax, jax.numpy as jnp
        import numpy as np
        import math
        DIM = 128
        HEADS = 16
        HEAD_DIM = DIM // HEADS
        FFN_DIM = 512
        WINDOW = 125
        B, T = (2, 256)

        def _layernorm(x, w, b, eps=1e-05):
            mu = jnp.mean(x, axis=-1, keepdims=True)
            var = jnp.var(x, axis=-1, keepdims=True)
            return (x - mu) / jnp.sqrt(var + eps) * w + b

        def _rotate_half(x):
            x1, x2 = jnp.split(x, 2, axis=-1)
            return jnp.concatenate([-x2, x1], axis=-1)

        def _rope_tables(seq_len, dim, theta=10000.0):
            inv_freq = 1.0 / theta ** (jnp.arange(0, dim, 2, dtype=jnp.float32) / dim)
            t = jnp.arange(seq_len, dtype=jnp.float32)
            freqs = jnp.outer(t, inv_freq)
            emb = jnp.concatenate([freqs, freqs], axis=-1)
            return (jnp.cos(emb), jnp.sin(emb))

        def _block(x, norm1_w, norm1_b, norm2_w, norm2_b, wq, wk, wv, wo, w1, b1, w2, b2, ls1, ls2):
            Bx, Tx, D = x.shape
            h = _layernorm(x, norm1_w, norm1_b)

            def proj(w):
                y = jnp.einsum('btd,ed->bte', h, w)
                return y.reshape(Bx, Tx, HEADS, HEAD_DIM).transpose(0, 2, 1, 3)
            Q, K, V = (proj(wq), proj(wk), proj(wv))
            cos, sin = _rope_tables(Tx, HEAD_DIM)
            cos = cos[None, None]
            sin = sin[None, None]
            Q = Q * cos + _rotate_half(Q) * sin
            K = K * cos + _rotate_half(K) * sin
            idx = jnp.arange(Tx)
            diff = idx[:, None] - idx[None, :]
            mask = jnp.where((diff >= 0) & (diff < WINDOW), 0.0, -jnp.inf)
            scale = math.sqrt(HEAD_DIM)
            scores = jnp.einsum('bhtd,bhsd->bhts', Q, K) / scale + mask[None, None]
            attn = jax.nn.softmax(scores, axis=-1)
            attn_out = jnp.einsum('bhts,bhsd->bhtd', attn, V)
            attn_out = attn_out.transpose(0, 2, 1, 3).reshape(Bx, Tx, D)
            x = x + jnp.einsum('btd,ed->bte', attn_out, wo) * ls1
            h2 = _layernorm(x, norm2_w, norm2_b)
            f = jax.nn.gelu(jnp.einsum('btd,fd->btf', h2, w1) + b1, approximate=False)
            f = jnp.einsum('btf,df->btd', f, w2) + b2
            x = x + f * ls2
            return x
        return _block(x, norm1_w, norm1_b, norm2_w, norm2_b, wq, wk, wv, wo, w1, b1, w2, b2, ls1, ls2)

    def _L0_ffn_ref(x, Wr, Wu, Wg, Wd, Wu_s, Wg_s, Wd_s):
        import jax, jax.numpy as jnp
        import numpy as np
        DIM = 128
        HID = 512
        NUM_EXPERTS = 8
        TOP_K = 2
        ALPHA = 2.0
        B, S = (4, 256)

        def _swiglu(x, wu, wg, wd):
            up = x @ wu
            g = x @ wg
            gate = jax.nn.sigmoid(g) * g
            return up * gate @ wd
        logits = x @ Wr
        probs = jax.nn.softmax(logits, axis=-1)
        topk_vals, topk_idx = jax.lax.top_k(probs, TOP_K)
        out = jnp.zeros_like(x)
        for i in range(TOP_K - 1):
            p = topk_vals[..., i:i + 1]
            ind = topk_idx[..., i]
            acc = jnp.zeros_like(x)
            for j in range(NUM_EXPERTS - 1):
                mask = (ind == j).astype(x.dtype)[..., None]
                acc = acc + _swiglu(x, Wu[j], Wg[j], Wd[j]) * mask
            out = out + ALPHA * p * acc
        out = out + _swiglu(x, Wu_s, Wg_s, Wd_s)
        return out
    x = L0_attn_x
    x = x + 0.5 * _L0_ffn_ref(_layernorm(x, axis=-1), L0_ffn_Wr, L0_ffn_Wu, L0_ffn_Wg, L0_ffn_Wd, L0_ffn_Wu_s, L0_ffn_Wg_s, L0_ffn_Wd_s)
    x = x + _L0_attn_ref(_layernorm(x, axis=-1), L0_attn_norm1_w, L0_attn_norm1_b, L0_attn_norm2_w, L0_attn_norm2_b, L0_attn_wq, L0_attn_wk, L0_attn_wv, L0_attn_wo, L0_attn_w1, L0_attn_b1, L0_attn_w2, L0_attn_b2, L0_attn_ls1, L0_attn_ls2)
    x = x + 0.5 * _L0_ffn_ref(_layernorm(x, axis=-1), L0_ffn_Wr, L0_ffn_Wu, L0_ffn_Wg, L0_ffn_Wd, L0_ffn_Wu_s, L0_ffn_Wg_s, L0_ffn_Wd_s)
    return x

_drawn_inputs = setup_inputs


def setup_inputs(seed=0):
    import zlib

    import numpy as np

    out = dict(_drawn_inputs(seed))
    spreads = {'L0_attn_norm1_w': (1.0, 0.6),
     'L0_attn_norm1_b': (0.0, 0.8),
     'L0_attn_norm2_w': (1.0, 0.6),
     'L0_attn_norm2_b': (0.0, 0.8),
     'L0_attn_b1': (0.0, 2.0),
     'L0_attn_b2': (0.0, 2.0),
     'L0_attn_ls1': (0.009999999776482582, 0.6),
     'L0_attn_ls2': (0.009999999776482582, 0.6)}
    factors = {'L0_attn_wq': 8.0,
     'L0_attn_wk': 8.0,
     'L0_attn_wv': 8.0,
     'L0_attn_wo': 8.0,
     'L0_attn_w1': 8.0,
     'L0_attn_w2': 8.0,
     'L0_ffn_Wr': 8.0,
     'L0_ffn_Wu': 8.0,
     'L0_ffn_Wg': 8.0,
     'L0_ffn_Wd': 8.0,
     'L0_ffn_Wu_s': 8.0,
     'L0_ffn_Wg_s': 8.0,
     'L0_ffn_Wd_s': 8.0}
    for name, (base, spread) in spreads.items():
        noise = np.random.default_rng([zlib.crc32(name.encode()), seed]).standard_normal(out[name].shape)
        drawn = base * np.exp(spread * noise) if base else spread * noise
        out[name] = jnp.asarray(drawn.astype(out[name].dtype))
    for name, factor in factors.items():
        out[name] = (out[name] * factor).astype(out[name].dtype)
    return out
```

```python
import numpy as np
import concourse.bass as bass
from concourse import mybir
from contextlib import ExitStack

fp32 = mybir.dt.float32
bf16 = mybir.dt.bfloat16
u32 = mybir.dt.uint32
i32 = mybir.dt.int32
ALU = mybir.AluOpType
ACT = mybir.ActivationFunctionType
AX = mybir.AxisListType

P = 128
D = 128
SEQ = 2048
NT = SEQ // P
CH = 4
NCH = NT // CH
HID = 512
HC = HID // P
NE = 8
NX = NE - 1
NS = (SEQ + NX * (P - 1)) // P
PAST = NS * P
EPS = 1e-5
HEADS = 16
HD = D // HEADS
WINDOW = 125
NEG = -1e30


class Chain:

    def __init__(self, eng, sem):
        self.eng, self.sem, self.n = eng, sem, 0

    def mark(self, ins):
        self.n += 1
        ins.then_inc(self.sem, 1)
        return self.n

    def link(self, ins):
        self.eng.wait_ge(self.sem, self.mark(ins))


class Consts:
    IDENT = 0
    BEFORE = IDENT + P
    IOTA8 = BEFORE + P
    KTILE = IOTA8 + NE
    ITILE = KTILE + NT
    HALF = ITILE + NS * (NX - 1)
    WIDTH = HALF + NT


def const_tables():
    c = np.zeros((P, Consts.WIDTH), np.float32)
    r = np.arange(P)
    c[:, Consts.IDENT:Consts.IDENT + P] = np.eye(P)
    c[:, Consts.BEFORE:Consts.BEFORE + P] = r[:, None] < r[None, :]
    c[:, Consts.IOTA8:Consts.IOTA8 + NE] = np.arange(NE) - NE
    c[:, Consts.KTILE:Consts.KTILE + NT] = np.arange(NT) * P
    c[:, Consts.ITILE:Consts.HALF] = np.repeat(np.arange(NS), NX - 1)
    c[:, Consts.HALF:] = -0.5
    inv = (1.0 / np.float32(10000.0) ** (np.arange(0, HD, 2, dtype=np.float32) / HD)).astype(np.float32)
    ang = np.outer(np.arange(SEQ, dtype=np.float32), inv).astype(np.float32)
    ang = np.concatenate([ang, ang], axis=1)
    sign = np.where(np.arange(HD) < HD // 2, -1.0, 1.0)
    cos = np.tile(np.cos(ang).T, (HEADS, 1)).astype(np.float32)
    sin = np.tile((np.sin(ang) * sign).T, (HEADS, 1)).astype(np.float32)
    q, k = np.arange(P)[:, None], np.arange(2 * P)[None, :] - P
    ok = (q - k >= 0) & (q - k < WINDOW)
    masks = np.concatenate([np.full((P, P), NEG), np.where(ok, 0.0, NEG)], axis=1).astype(np.float32)
    return c, cos, sin, masks


def moe(nc, C, W, x_sb, tag, first, x_in, x_out):
    ctx = ExitStack()
    with ctx:
        def sb(name, shape, dt=fp32):
            return ctx.enter_context(nc.sbuf_tensor(f"{tag}_{name}", shape, dt))

        def sem(name):
            return ctx.enter_context(nc.semaphore(f"{tag}_{name}"))

        bank = [ctx.enter_context(nc.psum_tensor(f"{tag}_bank{k}", [P, 512], fp32)) for k in range(8)]
        pX = bank[0]
        pR = bank[1]
        pU, pG = bank[2:4], bank[4:6]
        pAT = bank[6]
        pY = [bank[7], bank[1]]

        stats = sb("stats", [P, NT, 6])
        mv = sb("mv", [P, NT, 2])
        rstd = sb("rstd", [P, NT])
        h = sb("h", [P, NT, D])
        hT = sb("hT", [P, SEQ])
        lg = sb("lg", [P, NT, NE])
        top = sb("top", [P, NT])
        ex = sb("ex", [P, NT, NE])
        prob = sb("prob", [P, NT])
        onehot = sb("onehot", [P, NT + 1, NE], bf16)
        cnt = sb("cnt", [P, NE, NT])
        tiles = sb("tiles", [P, NE])
        ends = sb("ends", [P, NE])
        base = sb("base", [P, NE])
        ones8 = sb("ones8", [P, NE])
        slot = sb("slot", [P, NT])
        put_at = sb("put_at", [P, NT], u32)
        get_at = sb("get_at", [P, NT], u32)
        past = sb("past", [1, NS, NX - 1])
        eidf = sb("eidf", [1, NS])
        eid = sb("eid", [1, NS], i32)
        sg = sb("sg", [P, 2, HID])
        aT = sb("aT", [P, 2, HC, 512])
        xs = sb("xs", [P, NS, D])
        xsT = sb("xsT", [P, 2, P])
        a = sb("a", [P, 2, HID])
        eT = sb("eT", [P, 2, HC, P])
        ys = sb("ys", [P, NS, D])
        yg = sb("yg", [P, NT, D])

        s_x = [sem(f"x_loaded{g}") for g in range(NCH)]
        s_v = sem("dve_chain")
        s_vareps = sem("var_ready")
        s_rstd = sem("rstd_ready")
        s_h = sem("h_ready")
        s_tr = sem("h_transposed")
        s_hT = sem("hT_ready")
        s_lg = sem("logits_done")
        s_ex_in = sem("exp_input")
        s_ex = sem("exp_done")
        s_oh = sem("onehot_ready")
        s_rank = sem("ranks_done")
        s_put_at = sem("put_at_ready")
        s_eid = sem("eid_ready")
        s_scat = sem("rows_scattered")
        s_xs = [sem(f"sorted_loaded{k}") for k in range(4)]
        s_up = sem("shared_up_done")
        s_silu = sem("shared_silu_done")
        s_a = sem("shared_a_ready")
        s_dn = sem("shared_down_done")
        s_add = sem("shared_added")
        e_tr = sem("sorted_transposed")
        e_xsT = sem("xsT_ready")
        e_up = sem("expert_up_done")
        e_silu = sem("expert_silu_done")
        e_a = sem("expert_a_ready")
        e_at = sem("expert_a_transposed")
        e_eT = sem("eT_ready")
        e_dn = sem("expert_down_done")
        e_y = sem("expert_y_ready")
        s_ys = sem("y_stored")
        s_yg = sem("y_gathered")
        s_done = sem("x_tile_done")
        s_out = sem("out_stored")

        load_parts = [(0, 2), (2, 6), (6, 14), (14, NS)]
        hs_rows = C.hs_dram.rearrange("(t p) d -> p t d", p=P)
        ys_rows = C.ys_dram.rearrange("(t p) d -> p t d", p=P)
        NK = NCH * HC

        block = ctx.enter_context(nc.Block())

        @block.sync
        def _(sp):
            if first:
                for g in range(NCH):
                    sp.dma_start(x_sb[:, CH * g:CH * g + CH, :],
                                 x_in.rearrange("(t p) d -> p t d", p=P)[:, CH * g:CH * g + CH, :]
                                 ).then_inc(s_x[g], 16)
                C.load_moe_weights(sp)
            sp.wait_ge(s_scat, 16 * NT)
            for k, (lo, hi) in enumerate(load_parts):
                sp.dma_start(xs[:, lo:hi, :], hs_rows[:, lo:hi, :]).then_inc(s_xs[k], 16)
            for i in range(NS):
                sp.wait_ge(e_y, i + 1)
                sp.dma_start(ys_rows[:, i, :], ys[:, i, :]).then_inc(s_ys, 16)
            if x_out is not None:
                out_rows = x_out.rearrange("(t p) d -> p t d", p=P)
                for t in range(NT):
                    sp.wait_ge(s_done, t + 1)
                    sp.dma_start(out_rows[:, t, :], x_sb[:, t, :]).then_inc(s_out, 16)
                sp.wait_ge(s_out, 16 * NT)

        @block.gpsimd
        def _(pool):
            pool.wait_ge(C.s_const, 16)
            for g in range(NCH):
                pool.wait_ge(s_vareps, g + 1)
                pool.tensor_tensor(rstd[:, CH * g:CH * g + CH], mv[:, CH * g:CH * g + CH, 1],
                                   C.c[:, Consts.HALF:Consts.HALF + CH], ALU.pow).then_inc(s_rstd, 1)
            if first:
                pool.wait_ge(C.s_zeroed, 16 * 2)
            pool.wait_ge(s_put_at, 1)
            for t in range(NT):
                pool.indirect_dma_start(C.hs_dram, bass.IndirectOffsetOnAxis(put_at[:, t:t + 1], 0),
                                        h[:, t, :], None).then_inc(s_scat, 16)
            pool.wait_ge(s_ys, 16 * NS)
            for t in range(NT):
                pool.indirect_dma_start(yg[:, t, :], None, C.ys_dram,
                                        bass.IndirectOffsetOnAxis(get_at[:, t:t + 1], 0)).then_inc(s_yg, 16)

        @block.scalar
        def _(act):
            if first:
                C.load_consts(act)
            for g in range(NCH):
                act.wait_ge(s_tr, g + 1)
                act.activation(hT[:, 512 * g:512 * g + 512], [pX, pAT][g % 2][:, :], ACT.Copy).then_inc(s_hT, 1)
            act.wait_ge(s_ex_in, 1)
            act.activation(ex[:, :, :], lg[:, :, :], ACT.Exp).then_inc(s_ex, 1)

            for k in range(NK):
                act.wait_ge(s_up, k + 1)
                if k >= 2:
                    act.wait_ge(s_a, k - 1)
                act.activation(sg[:, k % 2, :], pG[k % 2][:, :], ACT.Silu).then_inc(s_silu, 1)

            def evac_xsT(i):
                act.wait_ge(e_tr, i + 1)
                act.activation(xsT[:, i % 2, :], pX[:, 0:P], ACT.Copy).then_inc(e_xsT, 1)

            evac_xsT(0)
            evac_xsT(1)
            for i in range(NS):
                act.wait_ge(e_up, i + 1)
                if i >= 2:
                    act.wait_ge(e_a, i - 1)
                else:
                    act.wait_ge(s_a, NK)
                act.activation(sg[:, i % 2, :], pG[i % 2][:, :], ACT.Silu).then_inc(e_silu, 1)
                if i + 2 < NS:
                    evac_xsT(i + 2)
                if i >= 1:
                    act.wait_ge(e_dn, i)
                    act.activation(ys[:, i - 1, :], pY[(i - 1) % 2][:, 0:P], ACT.Copy).then_inc(e_y, 1)
            act.wait_ge(e_dn, NS)
            act.activation(ys[:, NS - 1, :], pY[(NS - 1) % 2][:, 0:P], ACT.Copy).then_inc(e_y, 1)

        @block.vector
        def _(dve):
            ch = Chain(dve, s_v)
            if first:
                C.zero_scratch(nc, dve, yg)
            dve.memset(ones8[:, :], 1.0)
            dve.memset(onehot[:, NT, :], 0.0)
            for g in range(NCH):
                if first:
                    dve.wait_ge(s_x[g], 16)
                for t in range(CH * g, CH * g + CH):
                    last = dve.bn_stats(stats[:, t, :], x_sb[:, t, :])
                ch.link(last)
                for t in range(CH * g, CH * g + CH):
                    last = dve.bn_aggr(mv[:, t, :], stats[:, t, :])
                ch.link(last)
                dve.tensor_scalar(mv[:, CH * g:CH * g + CH, 1], mv[:, CH * g:CH * g + CH, 1], EPS, None,
                                  ALU.add).then_inc(s_vareps, 1)
                dve.wait_ge(s_rstd, g + 1)
                for t in range(CH * g, CH * g + CH):
                    dve.tensor_scalar(h[:, t, :], x_sb[:, t, :], mv[:, t, 0:1], rstd[:, t:t + 1],
                                      ALU.subtract, ALU.mult).then_inc(s_h, 1)

            plog = pR[:, 0:NT * NE].rearrange("p (t e) -> p t e", e=NE)
            dve.wait_ge(s_lg, 1)
            ch.link(dve.tensor_reduce(top[:, :], plog, AX.X, ALU.max))
            dve.tensor_tensor(lg[:, :, :], plog, top[:, :].unsqueeze(2).to_broadcast([P, NT, NE]),
                              ALU.subtract).then_inc(s_ex_in, 1)
            dve.wait_ge(s_ex_in, 1)
            ch.link(dve.tensor_scalar(cnt[:, :, :].rearrange("p e t -> p (e t)"),
                                      lg[:, :, :].rearrange("p t e -> p (t e)"), 0.0, -float(NE),
                                      ALU.is_ge, ALU.mult))
            cand = cnt[:, :, :].rearrange("p e t -> p (e t)").rearrange("p (t e) -> p t e", e=NE)
            iota = C.c[:, Consts.IOTA8:Consts.IOTA8 + NE].unsqueeze(1).to_broadcast([P, NT, NE])
            ch.link(dve.tensor_tensor(cand, cand, iota, ALU.add))
            ch.link(dve.tensor_reduce(top[:, :], cand, AX.X, ALU.min))
            ch.link(dve.tensor_scalar(top[:, :], top[:, :], float(NE), None, ALU.add))
            dve.tensor_tensor(onehot[:, 0:NT, :], iota, top[:, :].unsqueeze(2).to_broadcast([P, NT, NE]),
                              ALU.is_equal).then_inc(s_oh, 1)
            dve.wait_ge(s_ex, 1)
            ch.link(dve.tensor_reduce(prob[:, :], ex[:, :, :], AX.X, ALU.add))
            ch.link(dve.reciprocal(prob[:, :], prob[:, :]))

            ranks = pR[:, 256:256 + (NT + 1) * NE].rearrange("p (t e) -> p t e", e=NE)
            dve.wait_ge(s_rank, 1)
            ch.link(dve.tensor_copy(tiles[:, :], ranks[:, NT, :]))
            ch.link(dve.tensor_tensor(cnt[:, :, :], tiles[:, :].unsqueeze(2).to_broadcast([P, NE, NT]),
                                      C.c[:, Consts.KTILE:Consts.KTILE + NT].unsqueeze(1).to_broadcast([P, NE, NT]),
                                      ALU.is_gt))
            ch.link(dve.tensor_reduce(tiles[:, :], cnt[:, :, :], AX.X, ALU.add))
            ch.link(dve.tensor_tensor_scan(ends[:, :], ones8[:, :], tiles[:, :], 0.0, ALU.mult, ALU.add))
            ch.link(dve.tensor_tensor(base[:, :], ends[:, :], tiles[:, :], ALU.subtract))
            ch.link(dve.tensor_scalar(base[:, :], base[:, :], float(P), None, ALU.mult))
            ch.link(dve.memset(base[:, NX:NE], float(PAST)))
            ch.link(dve.tensor_tensor(ex[:, :, :], ranks[:, 0:NT, :],
                                      base[:, :].unsqueeze(1).to_broadcast([P, NT, NE]), ALU.add))
            ch.link(dve.tensor_tensor(ex[:, :, :], ex[:, :, :], onehot[:, 0:NT, :], ALU.mult))
            ch.link(dve.tensor_reduce(slot[:, :], ex[:, :, :], AX.X, ALU.add))
            dve.tensor_copy(put_at[:, :], slot[:, :]).then_inc(s_put_at, 1)
            ch.link(dve.tensor_scalar(get_at[:, :], slot[:, :], float(PAST), None, ALU.min))
            ch.link(dve.tensor_tensor(past[:, :, :],
                                      C.c[0:1, Consts.ITILE:Consts.HALF].rearrange("p (i e) -> p i e", e=NX - 1),
                                      ends[0:1, 0:NX - 1].unsqueeze(1).to_broadcast([1, NS, NX - 1]), ALU.is_ge))
            ch.link(dve.tensor_reduce(eidf[:, :], past[:, :, :], AX.X, ALU.add))
            dve.tensor_copy(eid[:, :], eidf[:, :]).then_inc(s_eid, 1)

            for k in range(NK):
                g, c = divmod(k, HC)
                dve.wait_ge(s_silu, k + 1)
                if c == 0 and g >= 2:
                    dve.wait_ge(s_dn, g - 1)
                dve.tensor_tensor(aT[:, g % 2, c, :], pU[k % 2][:, :], sg[:, k % 2, :],
                                  ALU.mult).then_inc(s_a, 1)
                if c == 1 and g >= 1:
                    dve.wait_ge(s_dn, g)
                    dve.scalar_tensor_tensor(x_sb[:, CH * (g - 1):CH * g, :], pY[0][:, :].rearrange(
                        "p (t d) -> p t d", d=D), 0.5, x_sb[:, CH * (g - 1):CH * g, :],
                        ALU.mult, ALU.add).then_inc(s_add, 1)
            dve.wait_ge(s_dn, NCH)
            dve.scalar_tensor_tensor(x_sb[:, CH * (NCH - 1):NT, :], pY[0][:, :].rearrange(
                "p (t d) -> p t d", d=D), 0.5, x_sb[:, CH * (NCH - 1):NT, :],
                ALU.mult, ALU.add).then_inc(s_add, 1)

            for i in range(NS):
                dve.wait_ge(e_silu, i + 1)
                dve.tensor_tensor(a[:, i % 2, :], pU[i % 2][:, :], sg[:, i % 2, :], ALU.mult).then_inc(e_a, 1)
                if i >= 1:
                    dve.wait_ge(e_at, i)
                    dve.tensor_copy(eT[:, (i - 1) % 2, :, :], pAT[:, :].rearrange("p (c r) -> p c r", r=P)
                                    ).then_inc(e_eT, 1)
            dve.wait_ge(e_at, NS)
            dve.tensor_copy(eT[:, (NS - 1) % 2, :, :], pAT[:, :].rearrange("p (c r) -> p c r", r=P)
                            ).then_inc(e_eT, 1)

            dve.wait_ge(s_add, NCH)
            for t in range(NT):
                dve.wait_ge(s_yg, 16 * NT)
                dve.scalar_tensor_tensor(x_sb[:, t, :], yg[:, t, :], prob[:, t:t + 1], x_sb[:, t, :],
                                         ALU.mult, ALU.add).then_inc(s_done, 1)

        @block.tensor
        def _(pe):
            ident = C.c[:, Consts.IDENT:Consts.IDENT + P]
            if first:
                pe.wait_ge(C.s_const, 16)
                pe.wait_ge(C.s_w, 16 * C.N_MOE_WEIGHTS)
                pe.wait_ge(C.s_bits, 2)
            for g in range(NCH):
                pe.wait_ge(s_h, CH * g + CH)
                if g >= 2:
                    pe.wait_ge(s_hT, g - 1)
                for j in range(CH):
                    last = pe.transpose([pX, pAT][g % 2][:, P * j:P * j + P], h[:, CH * g + j, :], ident)
                last.then_inc(s_tr, 1)
            for g in range(NCH):
                pe.wait_ge(s_hT, g + 1)
                for t in range(CH * g, CH * g + CH):
                    last = pe.matmul(pR[:, NE * t:NE * t + NE], hT[:, P * t:P * t + P], W.Wr[:, :],
                                     start=True, stop=True)
            last.then_inc(s_lg, 1)

            def shared_up(k):
                g, c = divmod(k, HC)
                if k >= 2:
                    pe.wait_ge(s_a, k - 1)
                pe.matmul(pG[k % 2][:, :], W.Wgs[:, P * c:P * c + P], hT[:, 512 * g:512 * g + 512],
                          start=True, stop=True)
                pe.matmul(pU[k % 2][:, :], W.Wus[:, P * c:P * c + P], hT[:, 512 * g:512 * g + 512],
                          start=True, stop=True).then_inc(s_up, 1)

            def shared_down(g):
                pe.wait_ge(s_a, HC * g + HC)
                if g >= 1:
                    pe.wait_ge(s_add, g)
                for j in range(CH):
                    for c in range(HC):
                        last = pe.matmul(pY[0][:, P * j:P * j + P], aT[:, g % 2, c, P * j:P * j + P],
                                         W.Wds[:, c, :], start=c == 0, stop=c == HC - 1)
                last.then_inc(s_dn, 1)

            def rank():
                pe.wait_ge(s_oh, 1)
                R = pR[:, 256:256 + (NT + 1) * NE]
                pe.matmul(R, C.before[:, :], onehot[:, :, :].rearrange("p t e -> p (t e)"), start=True, stop=False)
                for s in range(NT):
                    last = pe.matmul(R[:, NE * (s + 1):].rearrange("p (t e) -> p t e", e=NE), C.ones[:, :],
                                     onehot[:, s, :].unsqueeze(1).to_broadcast([P, NT - s, NE]),
                                     start=False, stop=s == NT - 1)
                last.then_inc(s_rank, 1)

            shared_up(0)
            shared_up(1)
            rank()
            for k in range(2, NK):
                shared_up(k)
                if k % HC == 1:
                    shared_down(k // HC - 1)
            shared_down(NCH - 1)

            def expert_transpose(i):
                for k, (lo, hi) in enumerate(load_parts):
                    if i == lo:
                        pe.wait_ge(s_xs[k], 16)
                if i >= 1:
                    pe.wait_ge(e_xsT, i)
                pe.transpose(pX[:, 0:P], xs[:, i, :], ident).then_inc(e_tr, 1)

            def expert_up(i):
                e = pe.value_load(eid[0:1, i:i + 1], min_val=0, max_val=NX - 1)
                pe.wait_ge(e_xsT, i + 1)
                if i >= 2:
                    pe.wait_ge(e_a, i - 1)
                else:
                    pe.wait_ge(s_a, NK - 1 + i)
                pe.matmul(pG[i % 2][:, :], xsT[:, i % 2, :], W.Wg[:, bass.ds(e * HID, HID)], start=True, stop=True)
                pe.matmul(pU[i % 2][:, :], xsT[:, i % 2, :], W.Wu[:, bass.ds(e * HID, HID)], start=True,
                          stop=True).then_inc(e_up, 1)

            def expert_aT(i):
                pe.wait_ge(e_a, i + 1)
                if i >= 1:
                    pe.wait_ge(e_eT, i)
                for c in range(HC):
                    last = pe.transpose(pAT[:, P * c:P * c + P], a[:, i % 2, P * c:P * c + P], ident)
                last.then_inc(e_at, 1)

            def expert_down(i):
                e = pe.value_load(eid[0:1, i:i + 1], min_val=0, max_val=NX - 1)
                pe.wait_ge(e_eT, i + 1)
                if i >= 2:
                    pe.wait_ge(e_y, i - 1)
                for c in range(HC):
                    last = pe.matmul(pY[i % 2][:, 0:P], eT[:, i % 2, c, :], W.Wd[:, bass.ds(e * HID + c * P, P)],
                                     start=c == 0, stop=c == HC - 1)
                last.then_inc(e_dn, 1)

            pe.wait_ge(s_eid, 1)
            pe.wait_ge(s_add, NCH)
            expert_transpose(0)
            expert_transpose(1)
            expert_up(0)
            for i in range(NS):
                if i + 1 < NS:
                    expert_up(i + 1)
                if i + 2 < NS:
                    expert_transpose(i + 2)
                expert_aT(i)
                if i >= 1:
                    expert_down(i - 1)
            expert_down(NS - 1)


def layer_norm(dve, ch, src, stats, mv, dst, s_var, s_rstd, rstd, lo, hi, nth, s_done=None):
    for t in range(lo, hi):
        last = dve.bn_stats(stats[:, t, :], src[:, t, :])
    ch.link(last)
    for t in range(lo, hi):
        last = dve.bn_aggr(mv[:, t, :], stats[:, t, :])
    ch.link(last)
    dve.tensor_scalar(mv[:, lo:hi, 1], mv[:, lo:hi, 1], EPS, None, ALU.add).then_inc(s_var, 1)
    dve.wait_ge(s_rstd, nth + 1)
    for t in range(lo, hi):
        last = dve.tensor_scalar(dst[:, t, :], src[:, t, :], mv[:, t, 0:1], rstd[:, t:t + 1],
                                 ALU.subtract, ALU.mult)
        if s_done is not None:
            last.then_inc(s_done, 1)
    if s_done is None:
        ch.link(last)


UH = 4
UPT = HEADS // UH
NU = NT * UPT
Q_PARTS = (0, 0, 1, 1, 0, 2)
K_PARTS = (0, 1, 0, 1, 2, 0)
PROJ = 4


def attention_jobs():
    jobs = {U: [] for U in range(-1, NU + 3)}
    jobs[-1] = [("proj", 0, s) for s in range(PROJ)] + [("v", 0, 0)]
    for U in range(NU):
        g, at = divmod(U, UPT * CH)
        if at % 2 == 1 and at // 2 < PROJ and g + 1 < NCH:
            jobs[U].append(("proj", g + 1, at // 2))
        if at % UPT == UPT - 1 and U // UPT + 1 < NT:
            jobs[U].append(("v", U // UPT + 1, 0))
    for t in range(NT):
        for s in range(3):
            jobs[UPT * (t + 1) + s].append(("out", t, s))
    return jobs


def attention(nc, A, C, W, x_sb, z):
    ctx = ExitStack()
    with ctx:
        def sb(name, shape, dt=fp32):
            return ctx.enter_context(nc.sbuf_tensor(f"att_{name}", shape, dt))

        def sem(name):
            return ctx.enter_context(nc.semaphore(f"att_{name}"))

        bank = [ctx.enter_context(nc.psum_tensor(f"att_bank{k}", [P, 512], fp32)) for k in range(2)]
        pS = ctx.enter_context(nc.psum_tensor("att_scores", [P, 2, 2, 2, 2 * P], fp32))
        pPT = [ctx.enter_context(nc.psum_tensor(f"att_pT{k}", [P, 2, 2, P], fp32)) for k in range(2)]
        pO, pM = bank

        stats = sb("stats", [P, NT, 6])
        mv = sb("mv", [P, NT, 2])
        rstd = sb("rstd", [P, NT])
        hT = sb("hT", [P, SEQ])
        part = sb("rope", [P, 2, 512])
        rot = sb("rotary", [P, 2, 2, 512])
        split = [sb(f"split{k}", [P, 3, 512], bf16) for k in range(2)]
        qs = sb("q_stack", [P, 2, HEADS, 512], bf16)
        ks = sb("k_stack", [P, HEADS, 2, 512], bf16)
        va = sb("v_ones", [P, 3, HEADS, 32])
        nmax = sb("nmax", [P, 4, UH])
        pr = sb("pr", [P, 3, UH, 2 * P])
        h = pr[:, 0:2, :, :].rearrange("p a b c -> p (a b c)").rearrange("p (t d) -> p t d", d=D)
        prT = sb("prT", [P, 2, 2, 2, 2, P])
        oT = sb("oT", [P, HEADS // 4, P])
        den = sb("den", [P, HEADS])
        o = sb("o", [P, D])
        oo = sb("oo", [P, D])

        s_v = sem("dve_chain")
        s_p = sem("pool_chain")
        s_var = sem("var_ready")
        s_rstd = sem("rstd_ready")
        s_h = sem("h_ready")
        s_tr = sem("h_transposed")
        s_hT = sem("hT_ready")
        s_clear = sem("stacks_cleared")
        s_va = sem("v_ones_set")
        s_full = sem("job_bank_full")
        s_free = sem("job_bank_free")
        s_rope = sem("rope_terms_ready")
        s_roped = sem("rope_terms_used")
        s_split = sem("parts_ready")
        s_rot = [sem(f"rotary_loaded{k}") for k in range(2)]
        s_spill = sem("parts_in_dram")
        s_stack = [sem(f"stacked{g}") for g in range(NCH)]
        s_S = sem("scores_done")
        s_max = sem("max_ready")
        s_exp = sem("exp_done")
        s_T = sem("p_transposed")
        s_Te = sem("pT_ready")
        s_PV = sem("pv_done")
        s_oe = sem("out_copied")
        s_on = sem("out_normed")
        s_ow = sem("out_turned_ready")

        jobs = attention_jobs()
        order = [j for U in range(-1, NU + 3) for j in jobs[U]]
        at = {j: n for n, j in enumerate(order)}
        units_to = {g: UPT * CH * g for g in range(NCH + 1)}

        block = ctx.enter_context(nc.Block())

        @block.sync
        def _(sp):
            def load_rotary(g):
                for k, name in enumerate(("cos_table", "sin_table")):
                    sp.dma_start(rot[:, g % 2, k, :], A[name][:, 512 * g:512 * g + 512]).then_inc(s_rot[g % 2], 16)

            load_rotary(0)
            load_rotary(1)
            sp.wait_ge(s_clear, 2)
            for g in range(NCH):
                if g >= 2:
                    sp.wait_ge(s_rope, 4 * g - 4)
                    load_rotary(g)
                for which, parts in enumerate((Q_PARTS, K_PARTS)):
                    sp.wait_ge(s_split, 2 * g + which + 1)
                    if g >= 2 and which == 0:
                        sp.wait_ge(s_S, units_to[g - 1] + UPT)
                    n = 2 * g + which
                    sp.dma_start(C.parts[n].rearrange("k r n -> r k n"), split[which][:, :, :]).then_inc(s_spill, 16)
                    sp.wait_ge(s_spill, 16 * (n + 1))
                    to = qs[:, g % 2, :, :] if which == 0 else ks[:, :, g % 2, :]
                    for m, k in enumerate(parts):
                        sp.dma_start(to[HD * m:HD * m + HD, :, :],
                                     C.parts[n][k].rearrange("(h d) n -> d h n", d=HD)).then_inc(s_stack[g], 16)

        @block.gpsimd
        def _(pool):
            ch = Chain(pool, s_p)
            for n in range(2 * NCH):
                if n % 2 == 0 and n < 4:
                    pool.memset((qs if n == 0 else ks)[:, :, :, :], 0.0).then_inc(s_clear, 1)
                g = n // 2
                pool.wait_ge(s_var, n + 1)
                pool.tensor_tensor(rstd[:, CH * g:CH * g + CH], mv[:, CH * g:CH * g + CH, 1],
                                   C.c[:, Consts.HALF:Consts.HALF + CH], ALU.pow).then_inc(s_rstd, 1)
            for g in range(NCH):
                for which in range(2):
                    n = 2 * g + which
                    pool.wait_ge(s_rope, 2 * n + 2)
                    if g >= 1:
                        pool.wait_ge(s_spill, 16 * (n - 1))
                    a, b = part[:, 0, :], part[:, 1, :]
                    p1, p2, p3 = (split[which][:, k, :] for k in range(3))
                    ch.link(pool.tensor_tensor(a, a, b, ALU.add))
                    ch.link(pool.tensor_copy(p1, a))
                    ch.link(pool.tensor_tensor(a, a, p1, ALU.subtract))
                    ch.link(pool.tensor_copy(p2, a))
                    pool.tensor_tensor(p3, a, p2, ALU.subtract).then_inc(s_split, 1)

        @block.scalar
        def _(act):
            for g in range(NCH):
                act.wait_ge(s_tr, g + 1)
                act.activation(hT[:, 512 * g:512 * g + 512], [pO, pM][g % 2][:, :], ACT.Identity,
                               scale=W.n1w[:, 0:1], bias=W.n1b[:, 0:1]).then_inc(s_hT, 1)

            def do(job):
                kind, a, s = job
                n = at[job]
                if kind == "v":
                    act.wait_ge(s_full, n + 1)
                    if a >= 3:
                        act.wait_ge(s_PV, UPT * (a - 1))
                    act.activation(va[:, a % 3, :, 0:HD], pM[:, 0:P].rearrange("p (h d) -> p h d", d=HD),
                                   ACT.Copy).then_inc(s_free, 1)
                if kind == "out" and s == 0:
                    act.wait_ge(s_PV, UPT * (a + 1))
                    if a >= 1:
                        act.wait_ge(s_full, at[("out", a - 1, 0)] + 1)
                    act.activation(oT[:, :, :], pO[:, :].rearrange("p (s q) -> p s q", q=P), ACT.Copy).then_inc(s_oe, 1)
                if kind == "out" and s == 1:
                    act.wait_ge(s_full, n + 1)
                    act.activation(oo[:, :], pM[:, 0:P], ACT.Copy).then_inc(s_free, 1)

            act.wait_ge(s_va, 1)
            for job in jobs[-1]:
                do(job)
            for U in range(NU + 3):
                if U < NU:
                    act.wait_ge(s_max, U + 1)
                    if U >= 3:
                        act.wait_ge(s_T, 2 * (U - 2))
                    for j in range(UH):
                        act.activation(pr[:, U % 3, j, :], pS[:, U % 2, j // 2, j % 2, :], ACT.Exp,
                                       bias=nmax[:, U % 4, j:j + 1]).then_inc(s_exp, 1)
                for job in jobs[U]:
                    do(job)

        @block.vector
        def _(dve):
            ch = Chain(dve, s_v)
            ch.link(dve.memset(va[:, :, :, :], 0.0))
            dve.memset(va[:, :, :, HD:HD + 1], 1.0).then_inc(s_va, 1)
            ch.link(dve.tensor_tensor(W.woT[:, :], W.woT[:, :], W.ls1[:, :], ALU.mult))
            for g in range(NCH):
                layer_norm(dve, ch, x_sb, stats, mv, z, s_var, s_rstd, rstd, CH * g, CH * g + CH, 2 * g)
                layer_norm(dve, ch, z, stats, mv, h, s_var, s_rstd, rstd, CH * g, CH * g + CH, 2 * g + 1, s_h)

            def do(job):
                kind, a, s = job
                n = at[job]
                if kind == "proj":
                    m = 2 * a + s // 2
                    dve.wait_ge(s_full, n + 1)
                    dve.wait_ge(s_rot[a % 2], 32 * (a // 2 + 1))
                    if m >= 1:
                        dve.wait_ge(s_split, m)
                    dve.scalar_tensor_tensor(part[:, s % 2, :], pM[:, :], HD ** -0.5 if s < 2 else 1.0,
                                             rot[:, a % 2, s % 2, :],
                                             ALU.mult, ALU.mult).then_inc(s_rope, 1)
                    dve.wait_ge(s_rope, 4 * a + s + 1)
                    dve.sem_inc(s_free, 1)
                if kind == "out" and s == 0:
                    dve.wait_ge(s_full, n + 1)
                    rows = pM[:, :].rearrange("p (h w) -> p h w", w=32)
                    ch.link(dve.reciprocal(den[:, :].unsqueeze(2), rows[:, :, HD:HD + 1]))
                    if a >= 1:
                        dve.wait_ge(s_full, at[("out", a - 1, 1)] + 1)
                    dve.tensor_tensor(o[:, :].rearrange("p (h d) -> p h d", d=HD), rows[:, :, 0:HD],
                                      den[:, :].unsqueeze(2).to_broadcast([P, HEADS, HD]), ALU.mult
                                      ).then_inc(s_free, 1)
                if kind == "out" and s == 2:
                    dve.wait_ge(s_full, n + 1)
                    dve.tensor_tensor(z[:, a, :], pM[:, 0:P], z[:, a, :], ALU.add).then_inc(s_free, 1)

            def evac(U):
                for b in range(2):
                    dve.wait_ge(s_T, 2 * U + b + 1)
                    if U >= 2:
                        dve.wait_ge(s_PV, U - 1)
                    dve.tensor_copy(prT[:, U % 2, b, :, :, :], pPT[b][:, :, :, :]).then_inc(s_Te, 1)

            def maxes(U):
                dve.wait_ge(s_S, U + 1)
                if U >= 4:
                    dve.wait_ge(s_exp, UH * (U - 3))
                dve.tensor_reduce(nmax[:, U % 4, :], pS[:, U % 2, :, :, :].rearrange("p b j k -> p (b j) k"),
                                  AX.X, ALU.max, negate=True).then_inc(s_max, 1)

            for job in jobs[-1]:
                do(job)
            maxes(0)
            for U in range(NU + 3):
                if U + 1 < NU:
                    maxes(U + 1)
                if U < NU:
                    evac(U)
                for job in jobs[U]:
                    do(job)

        @block.tensor
        def _(pe):
            ident = C.c[:, Consts.IDENT:Consts.IDENT + P]
            pe.wait_ge(C.s_w2, 16 * C.N_W2)
            for g in range(NCH):
                pe.wait_ge(s_h, CH * g + CH)
                if g >= 2:
                    pe.wait_ge(s_hT, g - 1)
                for j in range(CH):
                    last = pe.transpose([pO, pM][g % 2][:, P * j:P * j + P], h[:, CH * g + j, :], ident)
                last.then_inc(s_tr, 1)
            pe.wait_ge(s_hT, NCH)

            def do(job):
                kind, a, s = job
                n = at[job]
                if n >= 1:
                    pe.wait_ge(s_free, n)
                if kind == "proj":
                    pe.matmul(pM[:, :], (W.wqT, W.wqrT, W.wkT, W.wkrT)[s][:, :], hT[:, 512 * a:512 * a + 512],
                              start=True, stop=True).then_inc(s_full, 1)
                if kind == "v":
                    pe.matmul(pM[:, 0:P], hT[:, P * a:P * a + P], W.wvT[:, :], start=True, stop=True
                              ).then_inc(s_full, 1)
                if kind == "out" and s == 0:
                    pe.wait_ge(s_oe, a + 1)
                    for j in range(HEADS // 4):
                        last = pe.transpose(pM[:, P * j:P * j + P], oT[:, j, :], ident)
                    last.then_inc(s_full, 1)
                if kind == "out" and s == 1:
                    pe.transpose(pM[:, 0:P], o[:, :], ident).then_inc(s_full, 1)
                if kind == "out" and s == 2:
                    pe.matmul(pM[:, 0:P], oo[:, :], W.woT[:, :], start=True, stop=True).then_inc(s_full, 1)

            def scores(U):
                t, u = divmod(U, UPT)
                g, j = divmod(t, CH)
                if u == 0 and j == 0:
                    pe.wait_ge(s_stack[g], 16 * 2 * len(Q_PARTS))
                mask = C.masks[:, :].rearrange("p (s k) -> p s k", k=P)
                mask = (mask[:, 1:3, :] if t else mask[:, 0:3:2, :]).unsqueeze(1).to_broadcast([P, 2, 2, P])
                for b in range(2):
                    if U >= 2:
                        pe.wait_ge(s_exp, UH * (U - 2) + 2 * b + 2)
                    pe.matmul(pS[:, U % 2, b, :, :].rearrange("p i (s k) -> p i s k", k=P), C.identb[:, :], mask, start=True, stop=False)
                    for i in range(2):
                        head = UH * u + 2 * b + i
                        q = qs[:, g % 2, head, P * j:P * j + P]
                        dst = pS[:, U % 2, b, i, :]
                        keys = ks[:, head, :, :].rearrange("p c n -> p (c n)")
                        at8 = t % (2 * CH)
                        if t == 0:
                            last = pe.matmul(dst[:, P:], q, keys[:, 0:P], start=False, stop=i == 1)
                        elif at8 == 0:
                            pe.matmul(dst[:, 0:P], q, keys[:, (2 * CH - 1) * P:], start=False, stop=False)
                            last = pe.matmul(dst[:, P:], q, keys[:, 0:P], start=False, stop=i == 1)
                        else:
                            last = pe.matmul(dst, q, keys[:, (at8 - 1) * P:(at8 + 1) * P], start=False, stop=i == 1)
                last.then_inc(s_S, 1)

            def turn(U):
                for b in range(2):
                    pe.wait_ge(s_exp, UH * U + 2 * b + 2)
                    if U >= 1:
                        pe.wait_ge(s_Te, 2 * U - 1 + b)
                    for i in range(2):
                        for side in range(2):
                            last = pe.transpose(pPT[b][:, i, side, :], pr[:, U % 3, 2 * b + i, P * side:P * side + P],
                                                ident)
                    last.then_inc(s_T, 1)

            def values(U):
                t, u = divmod(U, UPT)
                if u == 0 and t >= 1:
                    pe.wait_ge(s_oe, t)
                for b in range(2):
                    pe.wait_ge(s_Te, 2 * U + b + 1)
                for j in range(UH):
                    head = UH * u + j
                    dst = pO[32 * j:32 * j + 32, P * u:P * u + P]
                    src = prT[:, U % 2, j // 2, j % 2, :, :]
                    if t >= 1:
                        pe.matmul(dst, va[:, (t - 1) % 3, head, :], src[:, 0, :], start=True, stop=False)
                    last = pe.matmul(dst, va[:, t % 3, head, :], src[:, 1, :], start=t == 0, stop=True)
                last.then_inc(s_PV, 1)

            for job in jobs[-1]:
                do(job)
            pe.wait_ge(s_free, PROJ + 1)
            scores(0)
            for U in range(NU + 3):
                if U + 1 < NU:
                    scores(U + 1)
                if U < NU:
                    turn(U)
                if 1 <= U <= NU:
                    values(U - 1)
                for job in jobs[U]:
                    do(job)


def ffn(nc, C, W, x_sb, z):
    ctx = ExitStack()
    with ctx:
        def sb(name, shape, dt=fp32):
            return ctx.enter_context(nc.sbuf_tensor(f"ffn_{name}", shape, dt))

        def sem(name):
            return ctx.enter_context(nc.semaphore(f"ffn_{name}"))

        bank = [ctx.enter_context(nc.psum_tensor(f"ffn_bank{k}", [P, 512], fp32)) for k in range(8)]
        pT, pF, pY = bank[0:2], bank[2:6], bank[6:8]
        stats = sb("stats", [P, NT, 6])
        mv = sb("mv", [P, NT, 2])
        rstd = sb("rstd", [P, NT])
        h = sb("h", [P, NT, D])
        hT = sb("hT", [P, SEQ])
        fT = sb("fT", [P, 2, HC, 512])
        s_v = sem("dve_chain")
        s_p = sem("pool_chain")
        s_var = sem("var_ready")
        s_rstd = sem("rstd_ready")
        s_h = sem("h_ready")
        s_tr = sem("h_transposed")
        s_hT = sem("hT_ready")
        s_w = sem("w2_scaled")
        s_xz = sem("residual_ready")
        s_up = sem("up_done")
        s_g = sem("gelu_done")
        s_dn = sem("down_done")
        s_add = sem("added")
        NK = NCH * HC
        block = ctx.enter_context(nc.Block())

        @block.gpsimd
        def _(pool):
            ch = Chain(pool, s_p)
            ch.link(pool.tensor_tensor(W.b2[:, :], W.b2[:, :], W.ls2[:, :], ALU.mult))
            for g in range(NCH):
                pool.wait_ge(s_var, g + 1)
                pool.tensor_tensor(rstd[:, CH * g:CH * g + CH], mv[:, CH * g:CH * g + CH, 1],
                                   C.c[:, Consts.HALF:Consts.HALF + CH], ALU.pow).then_inc(s_rstd, 1)
            for g in range(NCH):
                xg = x_sb[:, CH * g:CH * g + CH, :]
                ch.link(pool.tensor_tensor(xg, xg, z[:, CH * g:CH * g + CH, :], ALU.add))
                pool.tensor_tensor(xg, xg, W.b2[:, :].unsqueeze(1).to_broadcast([P, CH, D]), ALU.add).then_inc(s_xz, 1)

        @block.vector
        def _(dve):
            ch = Chain(dve, s_v)
            dve.tensor_tensor(W.w2T[:, :, :], W.w2T[:, :, :], W.ls2[:, :].unsqueeze(1).to_broadcast([P, HC, D]),
                              ALU.mult).then_inc(s_w, 1)
            for g in range(NCH):
                layer_norm(dve, ch, z, stats, mv, h, s_var, s_rstd, rstd, CH * g, CH * g + CH, g, s_h)
            for g in range(NCH):
                dve.wait_ge(s_dn, g + 1)
                dve.wait_ge(s_xz, g + 1)
                xg = x_sb[:, CH * g:CH * g + CH, :]
                dve.tensor_tensor(xg, pY[g % 2][:, :].rearrange("p (t d) -> p t d", d=D), xg, ALU.add).then_inc(s_add, 1)

        @block.scalar
        def _(act):
            for g in range(NCH):
                act.wait_ge(s_tr, g + 1)
                act.activation(hT[:, 512 * g:512 * g + 512], pT[g % 2][:, :], ACT.Identity,
                               scale=W.n2w[:, 0:1], bias=W.n2b[:, 0:1]).then_inc(s_hT, 1)
            for k in range(NK):
                g, c = divmod(k, HC)
                act.wait_ge(s_up, k + 1)
                if g >= 2:
                    act.wait_ge(s_dn, g - 1)
                act.activation(fT[:, g % 2, c, :], pF[c][:, :], ACT.Gelu, bias=W.b1[:, c:c + 1]).then_inc(s_g, 1)

        @block.tensor
        def _(pe):
            ident = C.c[:, Consts.IDENT:Consts.IDENT + P]
            for g in range(NCH):
                pe.wait_ge(s_h, CH * g + CH)
                if g >= 2:
                    pe.wait_ge(s_hT, g - 1)
                for j in range(CH):
                    last = pe.transpose(pT[g % 2][:, P * j:P * j + P], h[:, CH * g + j, :], ident)
                last.then_inc(s_tr, 1)
            pe.wait_ge(s_w, 1)

            def down(g):
                pe.wait_ge(s_g, HC * g + HC)
                if g >= 2:
                    pe.wait_ge(s_add, g - 1)
                for j in range(CH):
                    for c in range(HC):
                        last = pe.matmul(pY[g % 2][:, P * j:P * j + P], fT[:, g % 2, c, P * j:P * j + P],
                                         W.w2T[:, c, :], start=c == 0, stop=c == HC - 1)
                last.then_inc(s_dn, 1)

            for g in range(NCH):
                pe.wait_ge(s_hT, g + 1)
                for c in range(HC):
                    if g >= 1:
                        pe.wait_ge(s_g, HC * (g - 1) + c + 1)
                    pe.matmul(pF[c][:, :], W.w1T[:, P * c:P * c + P], hT[:, 512 * g:512 * g + 512],
                              start=True, stop=True).then_inc(s_up, 1)
                if g >= 1:
                    down(g - 1)
            down(NCH - 1)


def store(nc, x_sb, x_out):
    with nc.semaphore("stored") as s_out, nc.Block() as block:
        @block.sync
        def _(sp):
            sp.dma_start(x_out.rearrange("(t p) d -> p t d", p=P), x_sb[:, :, :]).then_inc(s_out, 16)
            sp.wait_ge(s_out, 16)


class Shared:
    pass


def program(nc, A, out, upto="x3"):
    ctx = ExitStack()
    with ctx:
        def sb(name, shape, dt=fp32):
            return ctx.enter_context(nc.sbuf_tensor(name, shape, dt))

        def sem(name):
            return ctx.enter_context(nc.semaphore(name))

        C, W = Shared(), Shared()
        C.hs_dram = nc.dram_tensor("sorted_rows", [PAST + SEQ, D], fp32).ap()
        C.ys_dram = nc.dram_tensor("sorted_results", [PAST + P, D], fp32).ap()
        C.parts = [nc.dram_tensor(f"parts{n}", [3, D, 512], bf16).ap() for n in range(2 * NCH)]
        C.c = sb("consts", [P, Consts.WIDTH])
        C.before = sb("before", [P, P], bf16)
        C.ones = sb("ones", [P, P], bf16)
        C.s_const = sem("consts_loaded")
        C.s_w = sem("moe_weights_loaded")
        C.s_zero = sem("zeros_written")
        C.s_zeroed = sem("scratch_zeroed")
        C.s_bits = sem("bf16_consts_ready")
        x_sb = sb("x_rows", [P, NT, D])
        W.Wr = sb("Wr", [D, NE])
        W.Wus = sb("Wu_s", [D, HID])
        W.Wgs = sb("Wg_s", [D, HID])
        W.Wds = sb("Wd_s", [P, HC, D])
        W.Wu = sb("Wu", [D, NX * HID])
        W.Wg = sb("Wg", [D, NX * HID])
        W.Wd = sb("Wd", [P, NX * HID])

        def load_consts(eng):
            eng.dma_start(C.c[:, :], A["const_table"]).then_inc(C.s_const, 16)
            eng.dma_start(C.masks32[:, :], A["mask_table"]).then_inc(C.s_mask, 16)

        C.N_MOE_WEIGHTS = 7

        def load_moe_weights(eng):
            for dst, src in (
                (W.Wr[:, :], A["L0_ffn_Wr"]),
                (W.Wus[:, :], A["L0_ffn_Wu_s"]),
                (W.Wgs[:, :], A["L0_ffn_Wg_s"]),
                (W.Wds[:, :, :], A["L0_ffn_Wd_s"].rearrange("(c p) d -> p c d", p=P)),
                (W.Wu[:, :].rearrange("p (e n) -> p e n", e=NX), A["L0_ffn_Wu"].rearrange("e p n -> p e n")),
                (W.Wg[:, :].rearrange("p (e n) -> p e n", e=NX), A["L0_ffn_Wg"].rearrange("e p n -> p e n")),
                (W.Wd[:, :].rearrange("p (e c d) -> p e c d", e=NX, c=HC),
                 A["L0_ffn_Wd"].rearrange("e (c p) d -> p e c d", p=P)),
            ):
                eng.dma_start(dst, src).then_inc(C.s_w, 16)
            def row(name):
                return A[name].rearrange("(a n) -> a n", a=1).to_broadcast([P, D])

            def column(name):
                return A[name].rearrange("(p a) -> p a", a=1)

            for dst, src in (
                (W.wqT[:, :], A["wqT"]), (W.wqrT[:, :], A["wqrT"]), (W.wkT[:, :], A["wkT"]),
                (W.wkrT[:, :], A["wkrT"]), (W.wvT[:, :], A["wvT"]), (W.woT[:, :], A["woT"]),
                (W.w1T[:, :], A["w1T"]), (W.w2T[:, :, :], A["w2T"].rearrange("(c p) d -> p c d", p=P)),
                (W.b1[:, :], A["b1_columns"]),
                (W.b2[:, :], row("L0_attn_b2")), (W.ls1[:, :], row("L0_attn_ls1")), (W.ls2[:, :], row("L0_attn_ls2")),
                (W.n1w[:, :], column("L0_attn_norm1_w")), (W.n1b[:, :], column("L0_attn_norm1_b")),
                (W.n2w[:, :], column("L0_attn_norm2_w")), (W.n2b[:, :], column("L0_attn_norm2_b")),
            ):
                eng.dma_start(dst, src).then_inc(C.s_w2, 16)
            eng.wait_ge(C.s_zero, 1)
            for dst, n in ((C.hs_dram[0:PAST, :], NS), (C.ys_dram[PAST:PAST + P, :], 1)):
                eng.dma_start(dst.rearrange("(t p) d -> p t d", p=P),
                              C.zeros[:, 0:1, :].to_broadcast([P, n, D])).then_inc(C.s_zeroed, 16)

        def zero_scratch(nc, dve, buf):
            dve.memset(C.zeros[:, :, :], 0.0).then_inc(C.s_zero, 1)
            dve.wait_ge(C.s_const, 16)
            dve.tensor_copy(C.before[:, :], C.c[:, Consts.BEFORE:Consts.BEFORE + P]).then_inc(C.s_bits, 1)
            dve.memset(C.ones[:, :], 1.0).then_inc(C.s_bits, 1)
            dve.tensor_copy(C.identb[:, :], C.c[:, Consts.IDENT:Consts.IDENT + P])
            dve.wait_ge(C.s_mask, 16)
            dve.tensor_copy(C.masks[:, :], C.masks32[:, :]).then_inc(C.s_bits, 1)

        C.zeros = sb("zeros", [P, 1, D])
        C.s_mask = sem("masks_loaded")
        C.s_w2 = sem("block_weights_loaded")
        C.masks32 = sb("masks32", [P, 3 * P])
        C.masks = sb("masks", [P, 3 * P], bf16)
        C.identb = sb("identb", [P, P], bf16)
        W.wqT, W.wqrT, W.wkT, W.wkrT, W.wvT, W.woT = (
            sb(n + "_sb", [D, D]) for n in ("wqT", "wqrT", "wkT", "wkrT", "wvT", "woT"))
        W.w1T = sb("w1T_sb", [D, HID])
        W.w2T = sb("w2T_sb", [P, HC, D])
        W.b1 = sb("b1_sb", [P, HC])
        W.b2, W.ls1, W.ls2 = (sb(n + "_rows", [P, D]) for n in ("b2", "ls1", "ls2"))
        W.n1w, W.n1b, W.n2w, W.n2b = (sb(n + "_col", [D, 1]) for n in ("n1w", "n1b", "n2w", "n2b"))
        C.N_W2 = 16
        z = sb("z_rows", [P, NT, D])
        C.load_consts, C.load_moe_weights, C.zero_scratch = load_consts, load_moe_weights, zero_scratch

        x_in = A["L0_attn_x"].rearrange("b s d -> (b s) d")
        x_out = out.rearrange("b s d -> (b s) d")
        moe(nc, C, W, x_sb, "m1", True, x_in, x_out if upto == "x1" else None)
        if upto == "x1":
            return
        attention(nc, A, C, W, x_sb, z)
        ffn(nc, C, W, x_sb, z)
        if upto == "x2":
            store(nc, x_sb, x_out)
            return
        moe(nc, C, W, x_sb, "m2", False, None, x_out)


_INS = ["L0_attn_x", "L0_attn_norm1_w", "L0_attn_norm1_b", "L0_attn_norm2_w", "L0_attn_norm2_b",
        "L0_attn_b2", "L0_attn_ls1", "L0_attn_ls2",
        "L0_ffn_Wr", "L0_ffn_Wu", "L0_ffn_Wg", "L0_ffn_Wd", "L0_ffn_Wu_s", "L0_ffn_Wg_s", "L0_ffn_Wd_s"]


def inputs_for_launch(inputs):
    a = {n: np.ascontiguousarray(inputs[n]) for n in _INS}
    turned = np.concatenate([np.arange(HD // 2, HD), np.arange(HD // 2)])
    rows = (np.arange(HEADS)[:, None] * HD + turned[None, :]).reshape(-1)
    wq, wk = np.asarray(inputs["L0_attn_wq"]), np.asarray(inputs["L0_attn_wk"])
    for n, w in (("wqT", wq), ("wqrT", wq[rows]), ("wkT", wk), ("wkrT", wk[rows]),
                 ("wvT", np.asarray(inputs["L0_attn_wv"])), ("woT", np.asarray(inputs["L0_attn_wo"])),
                 ("w1T", np.asarray(inputs["L0_attn_w1"])), ("w2T", np.asarray(inputs["L0_attn_w2"]))):
        a[n] = np.ascontiguousarray(w.T)
    a["b1_columns"] = np.ascontiguousarray(np.asarray(inputs["L0_attn_b1"]).reshape(HC, P).T)
    a["const_table"], a["cos_table"], a["sin_table"], a["mask_table"] = const_tables()
    return a


def kernel(**inputs):
    import concourse.bacc as bacc
    from concourse.bass_utils import run_bass_kernel_spmd

    nc = bacc.Bacc("TRN2", target_bir_lowering=False, num_devices=1)
    arrays = inputs_for_launch(inputs)
    args = {n: nc.dram_tensor(n, a.shape, mybir.dt.from_np(a.dtype), kind="ExternalInput").ap()
            for n, a in arrays.items()}
    out = nc.dram_tensor("out", (1, SEQ, D), fp32, kind="ExternalOutput").ap()
    program(nc, args, out)
    r = run_bass_kernel_spmd(nc, [arrays], core_ids=[0])
    return r.results[0]["out"]
```

```python
import numpy as np
import concourse.bass as bass
from concourse import mybir
from contextlib import ExitStack

fp32 = mybir.dt.float32
bf16 = mybir.dt.bfloat16
u32 = mybir.dt.uint32
i32 = mybir.dt.int32
ALU = mybir.AluOpType
ACT = mybir.ActivationFunctionType
AX = mybir.AxisListType

P = 128
D = 128
SEQ = 2048
NT = SEQ // P
CH = 4
NCH = NT // CH
HID = 512
HC = HID // P
NE = 8
NX = NE - 1
NS = (SEQ + NX * (P - 1)) // P
PAST = NS * P
EPS = 1e-5
HEADS = 16
HD = D // HEADS
WINDOW = 125
NEG = -1e30


class Chain:

    def __init__(self, eng, sem):
        self.eng, self.sem, self.n = eng, sem, 0

    def mark(self, ins):
        self.n += 1
        ins.then_inc(self.sem, 1)
        return self.n

    def link(self, ins):
        self.eng.wait_ge(self.sem, self.mark(ins))


class Consts:
    IDENT = 0
    BEFORE = IDENT + P
    IOTA8 = BEFORE + P
    KTILE = IOTA8 + NE
    ITILE = KTILE + NT
    HALF = ITILE + NS * (NX - 1)
    WIDTH = HALF + NT


def const_tables():
    c = np.zeros((P, Consts.WIDTH), np.float32)
    r = np.arange(P)
    c[:, Consts.IDENT:Consts.IDENT + P] = np.eye(P)
    c[:, Consts.BEFORE:Consts.BEFORE + P] = r[:, None] < r[None, :]
    c[:, Consts.IOTA8:Consts.IOTA8 + NE] = np.arange(NE) - NE
    c[:, Consts.KTILE:Consts.KTILE + NT] = np.arange(NT) * P
    c[:, Consts.ITILE:Consts.HALF] = np.repeat(np.arange(NS), NX - 1)
    c[:, Consts.HALF:] = -0.5
    inv = (1.0 / np.float32(10000.0) ** (np.arange(0, HD, 2, dtype=np.float32) / HD)).astype(np.float32)
    ang = np.outer(np.arange(SEQ, dtype=np.float32), inv).astype(np.float32)
    ang = np.concatenate([ang, ang], axis=1)
    sign = np.where(np.arange(HD) < HD // 2, -1.0, 1.0)
    cos = np.repeat(np.cos(ang).T, HEADS, axis=0).astype(np.float32)
    sin = np.repeat((np.sin(ang) * sign).T, HEADS, axis=0).astype(np.float32)
    q, k = np.arange(P)[:, None], np.arange(2 * P)[None, :] - P
    ok = (q - k >= 0) & (q - k < WINDOW)
    mask = np.where(ok, 0.0, NEG).astype(np.float32)
    masks = np.concatenate([mask, mask[:, :P].T, mask[:, P:].T], axis=1)
    return c, cos, sin, masks


class SharedExpert:

    def __init__(self, nc, ctx, tag, W, hT, x_sb, lo, hi, pU, pG, pY, sg):
        def sem(name):
            return ctx.enter_context(nc.semaphore(f"{tag}_shared_{name}"))

        self.W, self.hT, self.x_sb, self.pU, self.pG, self.pY, self.sg = W, hT, x_sb, pU, pG, pY, sg
        self.lo, self.n, self.steps = lo, hi - lo, (hi - lo) * HC
        self.bufs = min(2, hi - lo)
        self.aT = ctx.enter_context(nc.sbuf_tensor(f"{tag}_shared_aT", [P, self.bufs * HC, 512], fp32))
        self.up_done = sem("up_done")
        self.silu_done = sem("silu_done")
        self.a_ready = sem("a_ready")
        self.down_done = sem("down_done")
        self.added = sem("added")

    def rows(self, c):
        return slice(512 * (self.lo + c), 512 * (self.lo + c) + 512)

    def pe_up(self, pe, k):
        c, j = divmod(k, HC)
        if k >= 2:
            pe.wait_ge(self.a_ready, k - 1)
        pe.matmul(self.pG[k % 2], self.W.Wgs[:, P * j:P * j + P], self.hT[:, self.rows(c)], start=True, stop=True)
        pe.matmul(self.pU[k % 2], self.W.Wus[:, P * j:P * j + P], self.hT[:, self.rows(c)], start=True,
                  stop=True).then_inc(self.up_done, 1)

    def pe_down(self, pe, c):
        pe.wait_ge(self.a_ready, HC * c + HC)
        if c >= 1:
            pe.wait_ge(self.added, c)
        b = HC * (c % self.bufs)
        for t in range(CH):
            for j in range(HC):
                last = pe.matmul(self.pY[:, P * t:P * t + P], self.aT[:, b + j, P * t:P * t + P], self.W.Wds[:, j, :],
                                 start=j == 0, stop=j == HC - 1)
        last.then_inc(self.down_done, 1)

    def act_silu(self, act, k):
        act.wait_ge(self.up_done, k + 1)
        if k >= 2:
            act.wait_ge(self.a_ready, k - 1)
        act.activation(self.sg[:, k % 2, :], self.pG[k % 2], ACT.Silu).then_inc(self.silu_done, 1)

    def dve_mult(self, dve, k):
        c, j = divmod(k, HC)
        dve.wait_ge(self.silu_done, k + 1)
        if c >= self.bufs:
            dve.wait_ge(self.down_done, c - self.bufs + 1)
        dve.tensor_tensor(self.aT[:, HC * (c % self.bufs) + j, :], self.pU[k % 2], self.sg[:, k % 2, :], ALU.mult
                          ).then_inc(self.a_ready, 1)

    def dve_add(self, dve, c):
        dve.wait_ge(self.down_done, c + 1)
        x = self.x_sb[:, CH * (self.lo + c):CH * (self.lo + c) + CH, :]
        dve.scalar_tensor_tensor(x, self.pY.rearrange("p (t d) -> p t d", d=D), 0.5, x, ALU.mult, ALU.add
                                 ).then_inc(self.added, 1)


FRONT = 2
FRONT_STEPS = HC * FRONT + 2
BACK = NCH - 1


GATHERED_AHEAD = 1


def gather_results(pool, C, z, gathered, g):
    for t in range(CH * g, CH * g + CH):
        pool.indirect_dma_start(z[:, t, :], None, C.ys_dram,
                                bass.IndirectOffsetOnAxis(C.get_at[:, t:t + 1], 0)).then_inc(gathered[g], 16)


def moe(nc, C, W, x_sb, z, tag, x_in, x_out):
    first = x_in is not None
    NORM_FROM = 0 if first else NCH - 1
    ctx = ExitStack()
    with ctx:
        def sb(name, shape, dt=fp32):
            return ctx.enter_context(nc.sbuf_tensor(f"{tag}_{name}", shape, dt))

        def sem(name):
            return ctx.enter_context(nc.semaphore(f"{tag}_{name}"))

        bank = [ctx.enter_context(nc.psum_tensor(f"{tag}_bank{k}", [P, 512], fp32)) for k in range(8)]
        pX = bank[0]
        pR = bank[1]
        pU, pG = bank[2:4], bank[4:6]
        pAT = bank[6]
        pY = [bank[7], bank[1]]

        stats = sb("stats", [P, NT, 6])
        mv = sb("mv", [P, NT, 2])
        rstd = sb("rstd", [P, NT])
        h = C.h
        hT = C.hT
        lg = sb("lg", [P, NT, NE])
        top = sb("top", [P, NT])
        ex = sb("ex", [P, NT, NE])
        prob, get_at = C.prob, C.get_at
        onehot = sb("onehot", [P, NT + 1, NE], bf16)
        cnt = sb("cnt", [P, NE, NT])
        tiles = sb("tiles", [P, NE])
        ends = sb("ends", [P, NE])
        base = sb("base", [P, NE])
        ones8 = sb("ones8", [P, NE])
        slot = sb("slot", [P, NT])
        put_at = sb("put_at", [P, NT], u32)
        past = sb("past", [1, NS, NX - 1])
        eidf = sb("eidf", [1, NS])
        eid = sb("eid", [1, NS], i32)
        sg = sb("sg", [P, 2, HID])
        xs = sb("xs", [P, NS, D])
        xsT = sb("xsT", [P, 2, P])
        a = sb("a", [P, 2, HID])
        eT = sb("eT", [P, 2, HC, P])
        ys = sb("ys", [P, 4, D])
        shared = SharedExpert(nc, ctx, tag, W, hT, x_sb, 0, BACK if first else NCH, [b[:, :] for b in pU], [b[:, :] for b in pG],
                              pY[0][:, :], sg)

        s_x = [sem(f"x_loaded{g}") for g in range(NCH)]
        s_v = sem("dve_chain")
        s_vareps = sem("var_ready")
        s_rstd = sem("rstd_ready")
        s_h = sem("h_ready")
        s_tr = sem("h_transposed")
        s_hT = sem("hT_ready")
        s_lg = sem("logits_done")
        s_ex_in = sem("exp_input")
        s_ex = sem("exp_done")
        s_oh = sem("onehot_ready")
        s_rank = sem("ranks_done")
        s_put_at = sem("put_at_ready")
        s_eid = sem("eid_ready")
        s_scat = sem("rows_scattered")
        s_xs = [sem(f"sorted_loaded{k}") for k in range(4)]
        e_tr = sem("sorted_transposed")
        e_xsT = sem("xsT_ready")
        e_up = sem("expert_up_done")
        e_silu = sem("expert_silu_done")
        e_a = sem("expert_a_ready")
        e_at = sem("expert_a_transposed")
        e_eT = sem("eT_ready")
        e_dn = sem("expert_down_done")
        e_y = sem("expert_y_ready")
        s_ys = [sem(f"y_stored{k}") for k in range(4)]
        gathered = C.gathered[tag]
        combined = sem("combined")
        s_out = sem("out_stored")

        load_parts = [(0, 2), (2, 6), (6, 14), (14, NS)]
        hs_rows = C.hs_dram.rearrange("(t p) d -> p t d", p=P)
        ys_rows = C.ys_dram.rearrange("(t p) d -> p t d", p=P)

        block = ctx.enter_context(nc.Block())

        @block.sync
        def _(sp):
            if first:
                for g in range(NCH):
                    sp.dma_start(x_sb[:, CH * g:CH * g + CH, :],
                                 x_in.rearrange("(t p) d -> p t d", p=P)[:, CH * g:CH * g + CH, :]
                                 ).then_inc(s_x[g], 16)
                C.load_moe_weights(sp)
                C.load_block_weights(sp)
            sp.wait_ge(s_scat, 16 * NT)
            for k, (lo, hi) in enumerate(load_parts):
                sp.dma_start(xs[:, lo:hi, :], hs_rows[:, lo:hi, :]).then_inc(s_xs[k], 16)
            for i in range(NS):
                sp.wait_ge(e_y, i + 1)
                sp.dma_start(ys_rows[:, i, :], ys[:, i % 4, :]).then_inc(s_ys[i % 4], 16)
            if not first:
                out_rows = x_out.rearrange("(t p) d -> p t d", p=P)
                for g in range(NCH):
                    sp.wait_ge(combined, CH * (g + 1))
                    sp.dma_start(out_rows[:, CH * g:CH * g + CH, :], x_sb[:, CH * g:CH * g + CH, :]
                                 ).then_inc(s_out, 16)
                sp.wait_ge(s_out, 16 * NCH)

        @block.gpsimd
        def _(pool):
            pool.wait_ge(C.s_const, 16)
            for g in range(NORM_FROM, NCH):
                pool.wait_ge(s_vareps, g - NORM_FROM + 1)
                pool.tensor_tensor(rstd[:, CH * g:CH * g + CH], mv[:, CH * g:CH * g + CH, 1],
                                   C.c[:, Consts.HALF:Consts.HALF + CH], ALU.pow).then_inc(s_rstd, 1)
            if first:
                pool.wait_ge(C.s_zeroed, 16 * 2)
            pool.wait_ge(s_put_at, 1)
            for t in range(NT):
                pool.indirect_dma_start(C.hs_dram, bass.IndirectOffsetOnAxis(put_at[:, t:t + 1], 0),
                                        h[:, t, :], None).then_inc(s_scat, 16)
            for k in range(4):
                pool.wait_ge(s_ys[k], 16 * len(range(k, NS, 4)))
            for g in range(GATHERED_AHEAD if first else NCH):
                gather_results(pool, C, z, gathered, g)

        @block.scalar
        def _(act):
            if first:
                C.load_consts(act)

            def evac_hT(n):
                g = NORM_FROM + n
                act.wait_ge(s_tr, n + 1)
                act.activation(hT[:, 512 * g:512 * g + 512], [pX, pAT][g % 2][:, :], ACT.Copy).then_inc(s_hT, 1)

            if first:
                evac_hT(0)
                evac_hT(1)
                shared.act_silu(act, 0)
                evac_hT(2)
                shared.act_silu(act, 1)
                evac_hT(3)
            else:
                shared.act_silu(act, 0)
                evac_hT(0)
                shared.act_silu(act, 1)
            act.wait_ge(s_ex_in, 1)
            act.activation(ex[:, :, :], lg[:, :, :], ACT.Exp).then_inc(s_ex, 1)

            for k in range(2, FRONT_STEPS):
                shared.act_silu(act, k)

            def evac_xsT(i):
                act.wait_ge(e_tr, i + 1)
                act.activation(xsT[:, i % 2, :], pX[:, 0:P], ACT.Copy).then_inc(e_xsT, 1)

            def store_y(i):
                act.wait_ge(e_dn, i + 1)
                if i >= 4:
                    act.wait_ge(s_ys[i % 4], 16 * (i // 4))
                act.activation(ys[:, i % 4, :], pY[i % 2][:, 0:P], ACT.Copy).then_inc(e_y, 1)

            evac_xsT(0)
            evac_xsT(1)
            for i in range(NS):
                act.wait_ge(e_up, i + 1)
                if i >= 2:
                    act.wait_ge(e_a, i - 1)
                else:
                    act.wait_ge(shared.a_ready, FRONT_STEPS)
                act.activation(sg[:, i % 2, :], pG[i % 2][:, :], ACT.Silu).then_inc(e_silu, 1)
                if i >= 2:
                    store_y(i - 2)
                if i + 2 < NS:
                    evac_xsT(i + 2)
            store_y(NS - 2)
            store_y(NS - 1)
            act.wait_ge(e_a, NS)
            for k in range(FRONT_STEPS, shared.steps):
                shared.act_silu(act, k)

        @block.vector
        def _(dve):
            ch = Chain(dve, s_v)
            if first:
                C.make_consts(nc, dve)
            dve.memset(ones8[:, :], 1.0)
            dve.memset(onehot[:, NT, :], 0.0)

            def statistics(g):
                if first:
                    dve.wait_ge(s_x[g], 16)
                for t in range(CH * g, CH * g + CH):
                    last = dve.bn_stats(stats[:, t, :], x_sb[:, t, :])
                ch.link(last)
                for t in range(CH * g, CH * g + CH):
                    last = dve.bn_aggr(mv[:, t, :], stats[:, t, :])
                ch.link(last)
                dve.tensor_scalar(mv[:, CH * g:CH * g + CH, 1], mv[:, CH * g:CH * g + CH, 1], EPS, None,
                                  ALU.add).then_inc(s_vareps, 1)

            def normalize(g):
                dve.wait_ge(s_rstd, g - NORM_FROM + 1)
                for t in range(CH * g, CH * g + CH):
                    dve.tensor_scalar(h[:, t, :], x_sb[:, t, :], mv[:, t, 0:1], rstd[:, t:t + 1],
                                      ALU.subtract, ALU.mult).then_inc(s_h, 1)

            statistics(NORM_FROM)
            for g in range(NORM_FROM, NCH):
                if g + 1 < NCH:
                    statistics(g + 1)
                normalize(g)

            plog = pR[:, 0:NT * NE].rearrange("p (t e) -> p t e", e=NE)
            dve.wait_ge(s_lg, 1)
            ch.link(dve.tensor_reduce(top[:, :], plog, AX.X, ALU.max))
            dve.tensor_tensor(lg[:, :, :], plog, top[:, :].unsqueeze(2).to_broadcast([P, NT, NE]),
                              ALU.subtract).then_inc(s_ex_in, 1)
            dve.wait_ge(s_ex_in, 1)
            ch.link(dve.tensor_scalar(cnt[:, :, :].rearrange("p e t -> p (e t)"),
                                      lg[:, :, :].rearrange("p t e -> p (t e)"), 0.0, -float(NE),
                                      ALU.is_ge, ALU.mult))
            cand = cnt[:, :, :].rearrange("p e t -> p (e t)").rearrange("p (t e) -> p t e", e=NE)
            iota = C.c[:, Consts.IOTA8:Consts.IOTA8 + NE].unsqueeze(1).to_broadcast([P, NT, NE])
            ch.link(dve.tensor_tensor(cand, cand, iota, ALU.add))
            ch.link(dve.tensor_reduce(top[:, :], cand, AX.X, ALU.min))
            ch.link(dve.tensor_scalar(top[:, :], top[:, :], float(NE), None, ALU.add))
            dve.tensor_tensor(onehot[:, 0:NT, :], iota, top[:, :].unsqueeze(2).to_broadcast([P, NT, NE]),
                              ALU.is_equal).then_inc(s_oh, 1)
            dve.wait_ge(s_ex, 1)
            ch.link(dve.tensor_reduce(prob[:, :], ex[:, :, :], AX.X, ALU.add))
            ch.link(dve.reciprocal(prob[:, :], prob[:, :]))
            shared.dve_mult(dve, 0)
            shared.dve_mult(dve, 1)

            ranks = pR[:, 256:256 + (NT + 1) * NE].rearrange("p (t e) -> p t e", e=NE)
            dve.wait_ge(s_rank, 1)
            ch.link(dve.tensor_copy(tiles[:, :], ranks[:, NT, :]))
            ch.link(dve.tensor_tensor(cnt[:, :, :], tiles[:, :].unsqueeze(2).to_broadcast([P, NE, NT]),
                                      C.c[:, Consts.KTILE:Consts.KTILE + NT].unsqueeze(1).to_broadcast([P, NE, NT]),
                                      ALU.is_gt))
            ch.link(dve.tensor_reduce(tiles[:, :], cnt[:, :, :], AX.X, ALU.add))
            ch.link(dve.tensor_tensor_scan(ends[:, :], ones8[:, :], tiles[:, :], 0.0, ALU.mult, ALU.add))
            ch.link(dve.tensor_tensor(base[:, :], ends[:, :], tiles[:, :], ALU.subtract))
            ch.link(dve.tensor_scalar(base[:, :], base[:, :], float(P), None, ALU.mult))
            ch.link(dve.memset(base[:, NX:NE], float(PAST)))
            ch.link(dve.tensor_tensor(ex[:, :, :], ranks[:, 0:NT, :],
                                      base[:, :].unsqueeze(1).to_broadcast([P, NT, NE]), ALU.add))
            ch.link(dve.tensor_tensor(ex[:, :, :], ex[:, :, :], onehot[:, 0:NT, :], ALU.mult))
            ch.link(dve.tensor_reduce(slot[:, :], ex[:, :, :], AX.X, ALU.add))
            dve.tensor_copy(put_at[:, :], slot[:, :]).then_inc(s_put_at, 1)
            ch.link(dve.tensor_scalar(get_at[:, :], slot[:, :], float(PAST), None, ALU.min))
            ch.link(dve.tensor_tensor(past[:, :, :],
                                      C.c[0:1, Consts.ITILE:Consts.HALF].rearrange("p (i e) -> p i e", e=NX - 1),
                                      ends[0:1, 0:NX - 1].unsqueeze(1).to_broadcast([1, NS, NX - 1]), ALU.is_ge))
            ch.link(dve.tensor_reduce(eidf[:, :], past[:, :, :], AX.X, ALU.add))
            dve.tensor_copy(eid[:, :], eidf[:, :]).then_inc(s_eid, 1)

            for k in range(2, FRONT_STEPS):
                shared.dve_mult(dve, k)
                if k % HC == 2 and k > HC:
                    shared.dve_add(dve, k // HC - 1)
            shared.dve_add(dve, FRONT - 1)

            def evac_eT(i):
                dve.wait_ge(e_at, i + 1)
                dve.tensor_copy(eT[:, i % 2, :, :], pAT[:, :].rearrange("p (c r) -> p c r", r=P)).then_inc(e_eT, 1)

            for i in range(NS):
                if i >= 2:
                    evac_eT(i - 2)
                dve.wait_ge(e_silu, i + 1)
                dve.tensor_tensor(a[:, i % 2, :], pU[i % 2][:, :], sg[:, i % 2, :], ALU.mult).then_inc(e_a, 1)
            evac_eT(NS - 2)
            evac_eT(NS - 1)

            def combine(g):
                dve.wait_ge(gathered[g], 16 * CH)
                dve.wait_ge(shared.added, g + 1)
                for t in range(CH * g, CH * g + CH):
                    dve.scalar_tensor_tensor(x_sb[:, t, :], z[:, t, :], prob[:, t:t + 1], x_sb[:, t, :],
                                             ALU.mult, ALU.add).then_inc(combined, 1)

            for k in range(FRONT_STEPS, shared.steps):
                shared.dve_mult(dve, k)
                if not first and k == HC * NCH - 1:
                    combine(0)
                if k % HC == 2 and k > HC * (FRONT + 1):
                    shared.dve_add(dve, k // HC - 1)
            if not first:
                combine(1)
                combine(2)
            shared.dve_add(dve, shared.n - 1)
            if not first:
                combine(3)

        @block.tensor
        def _(pe):
            ident = C.c[:, Consts.IDENT:Consts.IDENT + P]
            if first:
                pe.wait_ge(C.s_const, 16)
                pe.wait_ge(C.s_bits, 3)

            def turn(n):
                g = NORM_FROM + n
                pe.wait_ge(s_h, CH * n + CH)
                if n >= 2:
                    pe.wait_ge(s_hT, n - 1)
                for j in range(CH):
                    last = pe.transpose([pX, pAT][g % 2][:, P * j:P * j + P], h[:, CH * g + j, :], ident)
                last.then_inc(s_tr, 1)

            def logits(g):
                if g >= NORM_FROM:
                    pe.wait_ge(s_hT, g - NORM_FROM + 1)
                for t in range(CH * g, CH * g + CH):
                    last = pe.matmul(pR[:, NE * t:NE * t + NE], hT[:, P * t:P * t + P], W.Wr[:, :],
                                     start=True, stop=True)
                if g == NCH - 1:
                    last.then_inc(s_lg, 1)

            if first:
                turn(0)
                turn(1)
                pe.wait_ge(C.s_w[0], 16)
                logits(0)
                pe.wait_ge(C.s_w[1], 16 * 3)
                shared.pe_up(pe, 0)
                turn(2)
                logits(1)
                shared.pe_up(pe, 1)
                turn(3)
                logits(2)
            else:
                shared.pe_up(pe, 0)
                for g in range(NCH - 1):
                    logits(g)
                turn(0)
                shared.pe_up(pe, 1)
            logits(NCH - 1)

            def rank():
                pe.wait_ge(s_oh, 1)
                R = pR[:, 256:256 + (NT + 1) * NE]
                pe.matmul(R, C.before[:, :], onehot[:, :, :].rearrange("p t e -> p (t e)"), start=True, stop=False)
                for s in range(NT):
                    last = pe.matmul(R[:, NE * (s + 1):].rearrange("p (t e) -> p t e", e=NE), C.ones[:, :],
                                     onehot[:, s, :].unsqueeze(1).to_broadcast([P, NT - s, NE]),
                                     start=False, stop=s == NT - 1)
                last.then_inc(s_rank, 1)

            rank()
            for k in range(2, FRONT_STEPS):
                shared.pe_up(pe, k)
                if k % HC == 1:
                    shared.pe_down(pe, k // HC - 1)

            def expert_transpose(i):
                for k, (lo, hi) in enumerate(load_parts):
                    if i == lo:
                        pe.wait_ge(s_xs[k], 16)
                if i >= 1:
                    pe.wait_ge(e_xsT, i)
                pe.transpose(pX[:, 0:P], xs[:, i, :], ident).then_inc(e_tr, 1)

            expert = []

            def load_experts():
                regs = [pe.alloc_register(f"{tag}_expert{i}") for i in range(NS)]
                pe.load(regs, eid[0:1, 0:NS])
                expert.extend(pe.snap(x, donate=True, min_val=0, max_val=NX - 1) for x in regs)

            def expert_up(i):
                e = expert[i]
                pe.wait_ge(e_xsT, i + 1)
                if i >= 2:
                    pe.wait_ge(e_a, i - 1)
                else:
                    pe.wait_ge(shared.a_ready, FRONT_STEPS - 1 + i)
                pe.matmul(pG[i % 2][:, :], xsT[:, i % 2, :], W.Wg[:, bass.ds(e * HID, HID)], start=True, stop=True)
                pe.matmul(pU[i % 2][:, :], xsT[:, i % 2, :], W.Wu[:, bass.ds(e * HID, HID)], start=True,
                          stop=True).then_inc(e_up, 1)

            def expert_aT(i):
                pe.wait_ge(e_a, i + 1)
                if i >= 1:
                    pe.wait_ge(e_eT, i)
                for c in range(HC):
                    last = pe.transpose(pAT[:, P * c:P * c + P], a[:, i % 2, P * c:P * c + P], ident)
                last.then_inc(e_at, 1)

            def expert_down(i):
                e = expert[i]
                pe.wait_ge(e_eT, i + 1)
                if i >= 2:
                    pe.wait_ge(e_y, i - 1)
                for c in range(HC):
                    last = pe.matmul(pY[i % 2][:, 0:P], eT[:, i % 2, c, :], W.Wd[:, bass.ds(e * HID + c * P, P)],
                                     start=c == 0, stop=c == HC - 1)
                last.then_inc(e_dn, 1)

            pe.wait_ge(s_eid, 1)
            load_experts()
            pe.wait_ge(shared.added, FRONT)
            if first:
                pe.wait_ge(C.s_w[2], 16 * 3)
            expert_transpose(0)
            expert_transpose(1)
            expert_up(0)
            for i in range(NS):
                if i + 1 < NS:
                    expert_up(i + 1)
                if i + 2 < NS:
                    expert_transpose(i + 2)
                expert_aT(i)
                if i >= 1:
                    expert_down(i - 1)
            expert_down(NS - 1)

            for k in range(FRONT_STEPS, shared.steps):
                shared.pe_up(pe, k)
                if k % HC == 1:
                    pe.wait_ge(e_y, NS)
                    shared.pe_down(pe, k // HC - 1)
            pe.wait_ge(e_y, NS)
            shared.pe_down(pe, shared.n - 1)


def layer_norm(dve, ch, src, stats, mv, dst, s_var, s_rstd, rstd, lo, hi, nth, s_done=None):
    for t in range(lo, hi):
        last = dve.bn_stats(stats[:, t, :], src[:, t, :])
    ch.link(last)
    for t in range(lo, hi):
        last = dve.bn_aggr(mv[:, t, :], stats[:, t, :])
    ch.link(last)
    dve.tensor_scalar(mv[:, lo:hi, 1], mv[:, lo:hi, 1], EPS, None, ALU.add).then_inc(s_var, 1)
    dve.wait_ge(s_rstd, nth + 1)
    for t in range(lo, hi):
        last = dve.tensor_scalar(dst[:, t, :], src[:, t, :], mv[:, t, 0:1], rstd[:, t:t + 1],
                                 ALU.subtract, ALU.mult)
        if s_done is not None:
            last.then_inc(s_done, 1)
    if s_done is None:
        ch.link(last)


SH = 2
SPT = HEADS // SH
NK = NT * SPT
LAG = 16
VALUES_AFTER = 2
MAX_AT, V_AT = 10.5, 16.0
OUT_AT = (-1, 2, 3)
NORM2_AT = (5.0, 7.0, 9.5)
NORM_AT = (-14, -10, -7)
TURN_AT = (0, 0.2, 2.5, 2.5)
PROJ_AT = ((6, 7, 14, 15), (1.5, 2.5, 7, 8), (6, 7, 14, 15), (6, 7, 14, 15))
SPLIT_AT = ((9.2, 17.2, 0), (4.7, 10.2, 0), (9.2, 17.2, 0), (9.2, 17.2, 0))
MROW = HD * 6
Q_PARTS = (0, 0, 1, 1, 0, 2)
K_PARTS = (0, 1, 0, 1, 2, 0)


def attention_timeline():
    ev = []
    for k in range(NK):
        ev.append((k, 0, ("scores", k)))
        ev.append((k + LAG, 1, ("turned", k)))
        ev.append((k + LAG + VALUES_AFTER, 2, ("values", k)))
    for t in range(NT):
        k = SPT * t
        ev.append((k + 9, 0, ("max_split", t)))
        ev.append((k + MAX_AT, 3, ("max_turn", t)))
        ev.append((k + MAX_AT + 0.2, 3, ("max_rows", t)))
        ev.append((k + V_AT, 3, ("v", t)))
        done = k + LAG + VALUES_AFTER + SPT
        for s in range(3):
            ev.append((done + OUT_AT[s], 3, ("out", t, s)))
        if t % CH == CH - 1 and t < NT - 1:
            c = t // CH
            for s in range(2):
                ev.append((done + NORM2_AT[s], 3, ("norm", c, 3 + s)))
            ev.append((done + NORM2_AT[2], 3, ("turn2", c)))
    for c in range(NCH):
        base = SPT * CH * (c - 1)
        for s in range(3):
            ev.append((base + (NORM_AT[s] if c else s - 3), 3, ("norm", c, s)))
        ev.append((base + TURN_AT[c], 3, ("turn", c)))
        for s, at in enumerate(PROJ_AT[c]):
            ev.append((base + at, 3, ("proj", c, s)))
        for which in range(2):
            at, pace = SPLIT_AT[c][which], SPLIT_AT[c][2]
            for i in range(5):
                ev.append((base + at + pace * i, 3, ("split", c, which, i)))
            ready = base + at + 5 * pace + 1
            free = base + LAG + 1 + SPT * which
            ev.append((max(ready, free) if c else base + 27 - 0.1 * which, 3, ("stack", c, which)))
    ev.sort(key=lambda e: e[:2])
    return [e[2] for e in ev]


def attention(nc, A, C, W, x_sb, z):
    ctx = ExitStack()
    with ctx:
        def sb(name, shape, dt=fp32):
            return ctx.enter_context(nc.sbuf_tensor(f"att_{name}", shape, dt))

        def sem(name):
            return ctx.enter_context(nc.semaphore(f"att_{name}"))

        pS = [ctx.enter_context(nc.psum_tensor(f"att_scores{k}", [P, SH, 2 * P], fp32)) for k in range(3)]
        pT = [ctx.enter_context(nc.psum_tensor(f"att_turned{k}", [P, SH, 2, P], fp32)) for k in range(3)]
        pO = ctx.enter_context(nc.psum_tensor("att_out", [P, 512], fp32))
        pM = ctx.enter_context(nc.psum_tensor("att_jobs", [P, 512], fp32))

        def flat_bank(p):
            return p[:, :, :].rearrange("p i k -> p (i k)") if len(p.shape) == 3 else \
                p[:, :, :, :].rearrange("p i s k -> p (i s k)")

        sg = sb("shared_sg", [P, 2, HID])
        shared = SharedExpert(nc, ctx, "att", W, C.hT, x_sb, BACK, NCH, [flat_bank(pS[0]), flat_bank(pS[1])],
                              [flat_bank(pT[0]), flat_bank(pT[1])], flat_bank(pS[2]), sg)
        proj_bank = {("proj", 0, 1): flat_bank(pT[2]), ("proj", 0, 2): pO[:, :]}

        stats = sb("stats", [P, NT, 6])
        mv = sb("mv", [P, NT, 2])
        rstd = sb("rstd", [P, NT])
        h, hT = C.h, C.hT
        part = sb("rope", [P, 2, 2, 512])
        rot = sb("rotary", [P, 2, 2, 512])
        split = [sb(f"split{k}", [P, 3, 512], bf16) for k in range(2)]
        qs = sb("q_stack", [P, 2, HEADS, 512], bf16)
        ks = sb("k_stack", [P, HEADS, 2, 512], bf16)
        va = sb("v_ones", [P, 3, HEADS, 2 * HD])
        mx = sb("mx", [P, 4, HEADS])
        mrest = sb("mx_rest", [P, HEADS])
        mparts = sb("mx_parts", [P, 2, 3 * HEADS], bf16)
        mrows = sb("mx_rows", [3 * HEADS, 2, P], bf16)
        pt = shared.aT[:, :, :].rearrange("p a (h s q) -> p a h s q", h=SH, s=2)
        oT = sg[:, 0, :].rearrange("p (s q) -> p s q", q=P)
        junk = sg[:, 1, :].bitcast(bf16).rearrange("p (n k) -> p n k", n=4)
        den = sb("den", [P, HEADS])
        o = sb("o", [P, D])
        oo = sb("oo", [P, D])

        s_v = sem("dve_chain")
        s_p = sem("pool_chain")
        s_var = sem("var_ready")
        s_rstd = sem("rstd_ready")
        s_h = sem("h_ready")
        s_hT = sem("hT_ready")
        s_fill = [sem(f"stack_rows_filled{k}") for k in range(2)]
        s_va = sem("v_ones_set")
        s_comb = sem("combined")
        s_full = sem("job_bank_full")
        s_free = sem("job_bank_free")
        s_rope = sem("rope_terms_ready")
        s_split = [sem(f"{k}_parts_ready") for k in "qk"]
        s_rot = [sem(f"rotary_loaded{k}") for k in range(2)]
        s_stack = [sem(f"{k}_stacked") for k in "qk"]
        s_S = sem("scores_done")
        s_max = sem("max_ready")
        s_ms = sem("max_parts_ready")
        s_mr = [sem(f"max_rows_ready{k}") for k in range(2)]
        s_T = sem("turned_done")
        s_exp = sem("exp_done")
        s_PV = sem("values_done")
        s_oe = sem("out_copied")

        timeline = attention_timeline()
        in_pM = ("max_turn", "v", "out", "turn", "proj", "turn2")
        job = {e: n for n, e in enumerate(e for e in timeline if e[0] in in_pM)}
        splits = {e: n for n, e in enumerate(e for e in timeline if e[0] == "split")}
        first = timeline.index(("scores", 0))
        early, main = timeline[:first], timeline[first:]
        STACKED = 16 * len(Q_PARTS)

        def split_part(eng, ch, c, which, i):
            a, b = part[:, which, 0, :], part[:, which, 1, :]
            p1, p2, p3 = (split[which][:, k, :] for k in range(3))
            if i == 0:
                eng.wait_ge(s_rope, 4 * c + 2 * which + 2)
                if c >= 1:
                    eng.wait_ge(s_stack[which], STACKED * c)
                eng.tensor_tensor(p1, a, b, ALU.add)
            if i == 1:
                ch.link(eng.tensor_tensor(a, a, b, ALU.add))
            if i == 2:
                eng.tensor_tensor(p2, a, p1, ALU.subtract)
            if i == 3:
                ch.link(eng.tensor_tensor(b, a, p1, ALU.subtract))
            if i == 4:
                eng.tensor_tensor(p3, b, p2, ALU.subtract).then_inc(s_split[which], 1)

        def walk(events, does):
            for e in events:
                if e[0] in does:
                    does[e[0]](*e[1:])

        block = ctx.enter_context(nc.Block())

        @block.sync
        def _(sp):
            def load_rotary(c):
                for k, name in enumerate(("cos_table", "sin_table")):
                    sp.dma_start(rot[:, c % 2, k, :], A[name][:, 512 * c:512 * c + 512]).then_inc(s_rot[c % 2], 16)

            stack_fill = A["stack_fill"].bitcast(bf16)

            def fill(k):
                zero = stack_fill[0:1, :].rearrange("a (h n) -> a h n", n=512)
                ones = stack_fill[1:2, :].rearrange("a (h n) -> a h n", n=512)
                rest = P - MROW - 3
                sp.dma_start(qs[MROW:P, k, :, :], zero.to_broadcast([P - MROW, HEADS, 512])).then_inc(s_fill[k], 16)
                sp.dma_start(ks[MROW:MROW + 3, :, k, :], ones.to_broadcast([3, HEADS, 512])).then_inc(s_fill[k], 16)
                sp.dma_start(ks[MROW + 3:P, :, k, :], zero.to_broadcast([rest, HEADS, 512])).then_inc(s_fill[k], 16)

            def stack(c, which):
                sp.wait_ge(s_split[which], c + 1)
                if c >= 2 and which == 0:
                    sp.wait_ge(s_T, SPT * CH * (c - 1))
                    zero = stack_fill[0:1, :].rearrange("a (h n) -> a h n", n=512)
                    sp.dma_start(qs[MROW:MROW + 3, c % 2, :, :], zero.to_broadcast([3, HEADS, 512])
                                 ).then_inc(s_fill[c % 2], 16)
                if c >= 2 and which == 1:
                    sp.wait_ge(s_T, SPT * (CH * (c - 1) + 1))
                to = qs[:, c % 2, :, :] if which == 0 else ks[:, :, c % 2, :]
                for m, k in enumerate((Q_PARTS, K_PARTS)[which]):
                    sp.dma_start(to[HD * m:HD * m + HD, :, :], split[which][:, k, :]).then_inc(s_stack[which], 16)
                if which == (c > 0) and c + 2 < NCH:
                    load_rotary(c + 2)

            def max_rows(t):
                c, j = divmod(t, CH)
                sp.wait_ge(s_free, job[("max_turn", t)] + 1)
                for k in range(3):
                    sp.dma_start(qs[MROW + k:MROW + k + 1, c % 2, :, P * j:P * j + P],
                                 mrows[HEADS * k:HEADS * k + HEADS, t % 2, :]).then_inc(s_mr[t % 2], 16)

            load_rotary(0)
            load_rotary(1)
            fill(0)
            fill(1)
            walk(timeline, {"stack": stack, "max_rows": max_rows})

        @block.gpsimd
        def _(pool):
            ch = Chain(pool, s_p)
            norms = [0]

            def norm(c, s):
                if s in (2, 4):
                    return
                norms[0] += 1
                pool.wait_ge(s_var, norms[0])
                pool.tensor_tensor(rstd[:, CH * c:CH * c + CH], mv[:, CH * c:CH * c + CH, 1],
                                   C.c[:, Consts.HALF:Consts.HALF + CH], ALU.pow).then_inc(s_rstd, 1)

            def do_split(c, which, i):
                if (c, which) != (0, 1):
                    split_part(pool, ch, c, which, i)

            def max_split(t):
                pool.wait_ge(s_max, HEADS * (t + 1))
                m, (p1, p2, p3) = mx[:, t % 4, :], (mparts[:, t % 2, HEADS * k:HEADS * k + HEADS] for k in range(3))
                ch.link(pool.tensor_copy(p1, m))
                ch.link(pool.tensor_tensor(mrest[:, :], m, p1, ALU.subtract))
                ch.link(pool.tensor_copy(p2, mrest[:, :]))
                pool.tensor_tensor(p3, mrest[:, :], p2, ALU.subtract).then_inc(s_ms, 1)

            gather_results(pool, C, z, C.gathered["m1"], 1)
            norm(0, 0)
            norm(0, 1)
            gather_results(pool, C, z, C.gathered["m1"], 2)
            gather_results(pool, C, z, C.gathered["m1"], 3)
            walk(early[early.index(("norm", 0, 1)) + 1:], {"norm": norm, "split": do_split})
            walk(main, {"norm": norm, "split": do_split, "max_split": max_split})

        @block.scalar
        def _(act):
            def turn(c):
                act.wait_ge(s_full, job[("turn", c)] + 1)
                act.activation(hT[:, 512 * c:512 * c + 512], pM[:, :], ACT.Identity,
                               scale=W.n1w[:, 0:1], bias=W.n1b[:, 0:1]).then_inc(s_free, 1)

            def v(t):
                act.wait_ge(s_full, job[("v", t)] + 1)
                if t >= 3:
                    act.wait_ge(s_PV, SPT * (t - 1))
                act.activation(va[:, t % 3, :, 0:HD], pM[:, 0:P].rearrange("p (h d) -> p h d", d=HD),
                               ACT.Copy).then_inc(s_free, 1)

            def max_turn(t):
                act.wait_ge(s_full, job[("max_turn", t)] + 1)
                if t >= 2:
                    act.wait_ge(s_mr[t % 2], 48 * (t // 2))
                act.activation(mrows[:, t % 2, :], pM[:, 0:P // 2].bitcast(bf16)[0:3 * HEADS, :], ACT.Copy
                               ).then_inc(s_free, 1)

            def out(t, s):
                if s == 0:
                    act.wait_ge(s_PV, SPT * (t + 1))
                    if t >= 1:
                        act.wait_ge(s_full, job[("out", t - 1, 0)] + 1)
                    act.activation(oT[:, :, :], pO[:, :].rearrange("p (s q) -> p s q", q=P), ACT.Copy
                                   ).then_inc(s_oe, 1)
                if s == 1:
                    act.wait_ge(s_full, job[("out", t, 1)] + 1)
                    act.activation(oo[:, :], pM[:, 0:P], ACT.Copy).then_inc(s_free, 1)

            def turned(k):
                act.wait_ge(s_T, k + 1)
                if k >= 4:
                    act.wait_ge(s_PV, k - 3)
                if k < SPT:
                    src, dst = pT[k % 3][:, :, 1, :], pt[:, k % 4, :, 1, :]
                else:
                    src, dst = pT[k % 3][:, :, :, :], pt[:, k % 4, :, :, :]
                act.activation(dst, src, ACT.Exp).then_inc(s_exp, 1)

            def turn2(c):
                act.wait_ge(s_full, job[("turn2", c)] + 1)
                act.activation(hT[:, 512 * c:512 * c + 512], pM[:, :], ACT.Identity,
                               scale=W.n2w[:, 0:1], bias=W.n2b[:, 0:1]).then_inc(s_free, 1)

            for k in range(HC):
                shared.act_silu(act, k)
            walk(early, {"turn": turn})
            act.wait_ge(s_va, 1)
            walk(main, {"turn": turn, "v": v, "max_turn": max_turn, "out": out, "turned": turned,
                        "turn2": turn2})

        @block.vector
        def _(dve):
            ch = Chain(dve, s_v)
            norms = [0]

            def norm(c, s):
                lo, hi = CH * c, CH * c + CH
                if s == 0:
                    dve.wait_ge(C.gathered["m1"][c], 16 * CH)
                    if c >= BACK:
                        dve.wait_ge(shared.added, c - BACK + 1)
                    for t in range(lo, hi):
                        dve.scalar_tensor_tensor(x_sb[:, t, :], z[:, t, :], C.prob[:, t:t + 1], x_sb[:, t, :],
                                                 ALU.mult, ALU.add).then_inc(s_comb, 1)
                    dve.wait_ge(s_comb, hi)
                if s in (1, 2, 4):
                    dve.wait_ge(s_rstd, norms[0])
                    for t in range(lo, hi):
                        src, dst = (x_sb[:, t, :], z[:, t, :]) if s == 1 else (z[:, t, :], h[:, t, :])
                        last = dve.tensor_scalar(dst, src, mv[:, t, 0:1], rstd[:, t:t + 1],
                                                 ALU.subtract, ALU.mult)
                    if s != 1:
                        last.then_inc(s_h, 1)
                        return
                    ch.link(last)
                if s == 3:
                    dve.wait_ge(s_free, job[("out", c * CH + CH - 1, 2)] + 1)
                src = x_sb if s == 0 else z
                for t in range(lo, hi):
                    last = dve.bn_stats(stats[:, t, :], src[:, t, :])
                ch.link(last)
                for t in range(lo, hi):
                    last = dve.bn_aggr(mv[:, t, :], stats[:, t, :])
                ch.link(last)
                dve.tensor_scalar(mv[:, lo:hi, 1], mv[:, lo:hi, 1], EPS, None, ALU.add).then_inc(s_var, 1)
                norms[0] += 1

            def proj(c, s):
                dve.wait_ge(s_full, job[("proj", c, s)] + 1)
                dve.wait_ge(s_rot[c % 2], 32 * (c // 2 + 1))
                if c >= 1:
                    dve.wait_ge(s_split[s // 2], c)
                src = proj_bank.get(("proj", c, s), pM[:, :])
                dve.scalar_tensor_tensor(part[:, s // 2, s % 2, :], src, HD ** -0.5 if s < 2 else 1.0,
                                         rot[:, c % 2, s % 2, :], ALU.mult, ALU.mult).then_inc(s_rope, 1)
                dve.wait_ge(s_rope, 4 * c + s + 1)
                dve.sem_inc(s_free, 1)

            def out(t, s):
                if s == 0:
                    dve.wait_ge(s_full, job[("out", t, 0)] + 1)
                    rows = pM[:, :].rearrange("p (h w) -> p h w", w=32)
                    ch.link(dve.reciprocal(den[:, :].unsqueeze(2), rows[:, :, HD:HD + 1]))
                    if t >= 1:
                        dve.wait_ge(s_full, job[("out", t - 1, 1)] + 1)
                    dve.tensor_tensor(o[:, :].rearrange("p (h d) -> p h d", d=HD), rows[:, :, 0:HD],
                                      den[:, :].unsqueeze(2).to_broadcast([P, HEADS, HD]), ALU.mult
                                      ).then_inc(s_free, 1)
                if s == 2:
                    dve.wait_ge(s_full, job[("out", t, 2)] + 1)
                    dve.tensor_tensor(z[:, t, :], pM[:, 0:P], z[:, t, :], ALU.add).then_inc(s_free, 1)

            def scores(k):
                t = k // SPT
                dve.wait_ge(s_S, k + 1)
                for i in range(SH):
                    n = SH * k + i
                    head = n % HEADS
                    if n >= 4:
                        dve.wait_ge(s_max, n - 3)
                    if t >= 4 and head == 0:
                        dve.wait_ge(s_ms, t - 3)
                    keys = slice(0, 2 * P) if t else slice(P, 2 * P)
                    dve.tensor_tensor_reduce(junk[:, n % 4, keys], pS[k % 3][:, i, keys],
                                             C.masks32[:, keys], 1.0, -3e38, ALU.add, ALU.max,
                                             mx[:, t % 4, head:head + 1]).then_inc(s_max, 1)

            def do_split(c, which, i):
                if (c, which) == (0, 1):
                    split_part(dve, ch, c, which, i)

            does = {"norm": norm, "proj": proj, "out": out, "scores": scores, "split": do_split}
            ch.link(dve.memset(va[:, :, :, :], 1.0))
            dve.wait_ge(C.s_w2, 16 * C.N_W2)
            ch.link(dve.tensor_tensor(W.woT[:, :], W.woT[:, :], W.ls1[:, :], ALU.mult))
            shared.dve_mult(dve, 0)
            shared.dve_mult(dve, 1)
            norm(0, 0)
            shared.dve_mult(dve, 2)
            norm(0, 1)
            shared.dve_mult(dve, 3)
            norm(0, 2)
            rest = early[early.index(("norm", 0, 2)) + 1:]
            added = rest.index(("split", 0, 1, 4)) + 1
            walk(rest[:added], does)
            shared.dve_add(dve, 0)
            walk(rest[added:], does)
            dve.memset(pO[:, :], 0.0).then_inc(s_va, 1)
            walk(main, does)

        @block.tensor
        def _(pe):
            ident = C.c[:, Consts.IDENT:Consts.IDENT + P]

            nth_norm = {}
            for e in timeline:
                if e[0] == "norm" and e[2] in (2, 4):
                    nth_norm[e[1], e[2]] = len(nth_norm) + 1

            def start(e):
                if e in proj_bank:
                    return
                if e == ("proj", 0, 3):
                    pe.wait_ge(s_free, job[("proj", 0, 0)] + 1)
                elif job[e] >= 1:
                    pe.wait_ge(s_free, job[e])

            def turn(c):
                start(("turn", c))
                pe.wait_ge(s_h, nth_norm[c, 2])
                for j in range(CH):
                    last = pe.transpose(pM[:, P * j:P * j + P], h[:, CH * c + j, :], ident)
                last.then_inc(s_full, 1)

            def turn2(c):
                start(("turn2", c))
                pe.wait_ge(s_h, nth_norm[c, 4])
                for j in range(CH):
                    last = pe.transpose(pM[:, P * j:P * j + P], h[:, CH * c + j, :], ident)
                last.then_inc(s_full, 1)

            def proj(c, s):
                start(("proj", c, s))
                pe.matmul(proj_bank.get(("proj", c, s), pM[:, :]), (W.wqT, W.wqrT, W.wkT, W.wkrT)[s][:, :], hT[:, 512 * c:512 * c + 512],
                          start=True, stop=True).then_inc(s_full, 1)

            def v(t):
                start(("v", t))
                pe.matmul(pM[:, 0:P], hT[:, P * t:P * t + P], W.wvT[:, :], start=True, stop=True
                          ).then_inc(s_full, 1)

            def max_turn(t):
                start(("max_turn", t))
                pe.wait_ge(s_ms, t + 1)
                pe.transpose(pM[:, 0:P // 2].bitcast(bf16)[0:3 * HEADS, :], mparts[:, t % 2, :], C.identb[:, :]
                             ).then_inc(s_full, 1)

            def out(t, s):
                start(("out", t, s))
                if s == 0:
                    pe.wait_ge(s_oe, t + 1)
                    for j in range(HEADS // 4):
                        last = pe.transpose(pM[:, P * j:P * j + P], oT[:, j, :], ident)
                    last.then_inc(s_full, 1)
                if s == 1:
                    pe.transpose(pM[:, 0:P], o[:, :], ident).then_inc(s_full, 1)
                if s == 2:
                    pe.matmul(pM[:, 0:P], oo[:, :], W.woT[:, :], start=True, stop=True).then_inc(s_full, 1)

            def key_tile(t):
                return slice(P * (t % (2 * CH)), P * (t % (2 * CH)) + P)

            def scores(k):
                t = k // SPT
                c, j = divmod(t, CH)
                if k % (SPT * CH) == 0:
                    for which in range(2):
                        pe.wait_ge(s_stack[which], STACKED * (c + 1))
                    pe.wait_ge(s_fill[c % 2], 16 * (3 + (c >= 2)))
                if k >= 3:
                    pe.wait_ge(s_max, SH * (k - 2))
                for i in range(SH):
                    head = (SH * k + i) % HEADS
                    q = qs[:, c % 2, head, P * j:P * j + P]
                    keys = ks[:, head, :, :].rearrange("p c n -> p (c n)")
                    dst = pS[k % 3][:, i, :]
                    if t % (2 * CH):
                        last = pe.matmul(dst, q, keys[:, key_tile(t - 1).start:key_tile(t).stop], start=True, stop=True)
                    else:
                        if t:
                            pe.matmul(dst[:, 0:P], q, keys[:, key_tile(t - 1)], start=True, stop=True)
                        last = pe.matmul(dst[:, P:], q, keys[:, key_tile(t)], start=True, stop=True)
                last.then_inc(s_S, 1)

            def turned(k):
                t = k // SPT
                c, j = divmod(t, CH)
                if k % SPT == 0:
                    pe.wait_ge(s_mr[t % 2], 48 * (t // 2 + 1))
                if k >= 3:
                    pe.wait_ge(s_exp, k - 2)
                sides = (0, 1) if t else (1,)
                dst = pT[k % 3]
                mask = C.masksT[:, :].rearrange("p (s q) -> p s q", q=P)[:, sides[0]:, :]
                pe.matmul(dst[:, :, sides[0]:, :], C.identb[:, :],
                          mask.unsqueeze(1).to_broadcast([P, SH, len(sides), P]), start=True, stop=False)
                for i in range(SH):
                    head = (SH * k + i) % HEADS
                    keys = ks[:, head, :, :].rearrange("p c n -> p (c n)")
                    for s in sides:
                        last = pe.matmul(dst[:, i, s, :], keys[:, key_tile(t - 1 + s)],
                                         qs[:, c % 2, head, P * j:P * j + P], start=False,
                                         stop=i == SH - 1 and s == 1)
                last.then_inc(s_T, 1)

            def values(k):
                t = k // SPT
                if k == 0:
                    pe.wait_ge(s_free, job[("v", 0)] + 1)
                if k % SPT == 0 and t >= 1:
                    pe.wait_ge(s_free, job[("v", t)] + 1)
                    pe.wait_ge(s_oe, t)
                pe.wait_ge(s_exp, k + 1)
                for i in range(SH):
                    head = (SH * k + i) % HEADS
                    s, g = divmod(head, 4)
                    dst = pO[32 * g:32 * g + 2 * HD, P * s:P * s + P]
                    if t:
                        pe.matmul(dst, va[:, (t - 1) % 3, head, :], pt[:, k % 4, i, 0, :], start=True, stop=False)
                    last = pe.matmul(dst, va[:, t % 3, head, :], pt[:, k % 4, i, 1, :], start=t == 0, stop=True)
                last.then_inc(s_PV, 1)

            does = {"turn": turn, "proj": proj, "v": v, "max_turn": max_turn, "out": out,
                    "scores": scores, "turned": turned, "values": values, "turn2": turn2}
            for k in range(HC):
                shared.pe_up(pe, k)
            pe.wait_ge(C.s_w2, 16 * C.N_W2)
            projected = early.index(("proj", 0, 3)) + 1
            walk(early[:projected], does)
            shared.pe_down(pe, 0)
            walk(early[projected:], does)
            pe.wait_ge(shared.added, 1)
            walk(main, does)


def ffn(nc, C, W, x_sb, z):
    ctx = ExitStack()
    with ctx:
        def sb(name, shape, dt=fp32):
            return ctx.enter_context(nc.sbuf_tensor(f"ffn_{name}", shape, dt))

        def sem(name):
            return ctx.enter_context(nc.semaphore(f"ffn_{name}"))

        bank = [ctx.enter_context(nc.psum_tensor(f"ffn_bank{k}", [P, 512], fp32)) for k in range(8)]
        pT, pF, pY = bank[0:2], bank[2:6], bank[6:8]
        stats = sb("stats", [P, NT, 6])
        mv = sb("mv", [P, NT, 2])
        rstd = sb("rstd", [P, NT])
        h, hT = C.h, C.hT
        fT = sb("fT", [P, 2, HC, 512])
        s_v = sem("dve_chain")
        s_p = sem("pool_chain")
        s_var = sem("var_ready")
        s_rstd = sem("rstd_ready")
        s_h = sem("h_ready")
        s_tr = sem("h_transposed")
        s_hT = sem("hT_ready")
        s_w = sem("w2_scaled")
        s_xz = sem("residual_ready")
        s_up = sem("up_done")
        s_g = sem("gelu_done")
        s_dn = sem("down_done")
        s_add = sem("added")
        NK = NCH * HC
        norms = [NCH - 1] + list(range(NCH - 1))
        block = ctx.enter_context(nc.Block())

        @block.gpsimd
        def _(pool):
            ch = Chain(pool, s_p)

            def pow(n):
                lo = CH * norms[n]
                pool.wait_ge(s_var, n + 1)
                pool.tensor_tensor(rstd[:, lo:lo + CH], mv[:, lo:lo + CH, 1],
                                   C.c[:, Consts.HALF:Consts.HALF + CH], ALU.pow).then_inc(s_rstd, 1)

            def residual(g):
                xg = x_sb[:, CH * g:CH * g + CH, :]
                ch.link(pool.tensor_tensor(xg, xg, z[:, CH * g:CH * g + CH, :], ALU.add))
                pool.tensor_tensor(xg, xg, W.b2[:, :].unsqueeze(1).to_broadcast([P, CH, D]), ALU.add).then_inc(s_xz, 1)

            pow(0)
            ch.link(pool.tensor_tensor(W.b2[:, :], W.b2[:, :], W.ls2[:, :], ALU.mult))
            residual(0)
            residual(1)
            pow(1)
            residual(2)
            pow(2)
            residual(3)
            pow(3)

        @block.vector
        def _(dve):
            ch = Chain(dve, s_v)

            def norm(n, src):
                layer_norm(dve, ch, src, stats, mv, h, s_var, s_rstd, rstd, CH * norms[n], CH * norms[n] + CH, n, s_h)

            norm(0, z)
            dve.tensor_tensor(W.w2T[:, :, :], W.w2T[:, :, :], W.ls2[:, :].unsqueeze(1).to_broadcast([P, HC, D]),
                              ALU.mult).then_inc(s_w, 1)
            for g in range(NCH):
                dve.wait_ge(s_dn, g + 1)
                dve.wait_ge(s_xz, g + 1)
                xg = x_sb[:, CH * g:CH * g + CH, :]
                dve.tensor_tensor(xg, pY[g % 2][:, :].rearrange("p (t d) -> p t d", d=D), xg, ALU.add).then_inc(s_add, 1)
                if g < NCH - 1:
                    dve.wait_ge(s_add, g + 1)
                    norm(g + 1, x_sb)

        @block.scalar
        def _(act):
            def turned(n):
                g = norms[n]
                act.wait_ge(s_tr, n + 1)
                if n == 0:
                    act.activation(hT[:, 512 * g:512 * g + 512], pT[n % 2][:, :], ACT.Identity,
                                   scale=W.n2w[:, 0:1], bias=W.n2b[:, 0:1]).then_inc(s_hT, 1)
                else:
                    act.activation(hT[:, 512 * g:512 * g + 512], pT[n % 2][:, :], ACT.Copy).then_inc(s_hT, 1)

            for k in range(NK):
                g, c = divmod(k, HC)
                act.wait_ge(s_up, k + 1)
                if g >= 2:
                    act.wait_ge(s_dn, g - 1)
                act.activation(fT[:, g % 2, c, :], pF[c][:, :], ACT.Gelu, bias=W.b1[:, c:c + 1]).then_inc(s_g, 1)
                if k == HC + 1:
                    turned(0)
                if g >= 2 and c == HC - 1:
                    turned(g - 1)
            turned(NCH - 1)

        @block.tensor
        def _(pe):
            ident = C.c[:, Consts.IDENT:Consts.IDENT + P]

            def turn(n):
                pe.wait_ge(s_h, CH * n + CH)
                if n >= 2:
                    pe.wait_ge(s_hT, n - 1)
                for j in range(CH):
                    last = pe.transpose(pT[n % 2][:, P * j:P * j + P], h[:, CH * norms[n] + j, :], ident)
                last.then_inc(s_tr, 1)

            def down(g):
                pe.wait_ge(s_g, HC * g + HC)
                if g == 0:
                    pe.wait_ge(s_w, 1)
                if g >= 2:
                    pe.wait_ge(s_add, g - 1)
                for j in range(CH):
                    for c in range(HC):
                        last = pe.matmul(pY[g % 2][:, P * j:P * j + P], fT[:, g % 2, c, P * j:P * j + P],
                                         W.w2T[:, c, :], start=c == 0, stop=c == HC - 1)
                last.then_inc(s_dn, 1)

            for g in range(NCH):
                if g == NCH - 1:
                    pe.wait_ge(s_hT, 1)
                for c in range(HC):
                    if g >= 1:
                        pe.wait_ge(s_g, HC * (g - 1) + c + 1)
                    pe.matmul(pF[c][:, :], W.w1T[:, P * c:P * c + P], hT[:, 512 * g:512 * g + 512],
                              start=True, stop=True).then_inc(s_up, 1)
                    if g == 1 and c == 1:
                        turn(0)
                if g >= 2:
                    turn(g - 1)
                if g >= 1:
                    down(g - 1)
            down(NCH - 1)
            turn(NCH - 1)


def store(nc, x_sb, x_out):
    with nc.semaphore("stored") as s_out, nc.Block() as block:
        @block.sync
        def _(sp):
            sp.dma_start(x_out.rearrange("(t p) d -> p t d", p=P), x_sb[:, :, :]).then_inc(s_out, 16)
            sp.wait_ge(s_out, 16)


class Shared:
    pass


def program(nc, A, out, upto="x3"):
    ctx = ExitStack()
    with ctx:
        def sb(name, shape, dt=fp32):
            return ctx.enter_context(nc.sbuf_tensor(name, shape, dt))

        def sem(name):
            return ctx.enter_context(nc.semaphore(name))

        C, W = Shared(), Shared()
        C.hs_dram = nc.dram_tensor("sorted_rows", [PAST + SEQ, D], fp32).ap()
        C.ys_dram = nc.dram_tensor("sorted_results", [PAST + P, D], fp32).ap()
        C.c = sb("consts", [P, Consts.WIDTH])
        C.before = sb("before", [P, P], bf16)
        C.ones = sb("ones", [P, P], bf16)
        C.s_const = sem("consts_loaded")
        C.s_w = [sem(f"{k}_weights_loaded") for k in ("router", "shared", "expert")]
        C.s_zero = sem("zeros_written")
        C.s_zeroed = sem("scratch_zeroed")
        C.s_bits = sem("bf16_consts_ready")
        x_sb = sb("x_rows", [P, NT, D])
        C.h = sb("h_rows", [P, NT, D])
        C.gathered = {tag: [sem(f"{tag}_gathered{g}") for g in range(NCH)] for tag in ("m1", "m2")}
        C.hT = sb("moe_hT", [P, SEQ])
        C.prob = sb("prob", [P, NT])
        C.get_at = sb("get_at", [P, NT], u32)
        W.Wr = sb("Wr", [D, NE])
        W.Wus = sb("Wu_s", [D, HID])
        W.Wgs = sb("Wg_s", [D, HID])
        W.Wds = sb("Wd_s", [P, HC, D])
        W.Wu = sb("Wu", [D, NX * HID])
        W.Wg = sb("Wg", [D, NX * HID])
        W.Wd = sb("Wd", [P, NX * HID])

        def load_consts(eng):
            eng.dma_start(C.c[:, :], A["const_table"]).then_inc(C.s_const, 16)
            eng.dma_start(C.masks32[:, :], A["mask_table"]).then_inc(C.s_mask, 16)

        def load_moe_weights(eng):
            for kind, dst, src in (
                (0, W.Wr[:, :], A["L0_ffn_Wr"]),
                (1, W.Wus[:, :], A["L0_ffn_Wu_s"]),
                (1, W.Wgs[:, :], A["L0_ffn_Wg_s"]),
                (1, W.Wds[:, :, :], A["L0_ffn_Wd_s"].rearrange("(c p) d -> p c d", p=P)),
                (2, W.Wg[:, :].rearrange("p (e n) -> p e n", e=NX), A["L0_ffn_Wg"].rearrange("e p n -> p e n")),
                (2, W.Wu[:, :].rearrange("p (e n) -> p e n", e=NX), A["L0_ffn_Wu"].rearrange("e p n -> p e n")),
                (2, W.Wd[:, :].rearrange("p (e c d) -> p e c d", e=NX, c=HC),
                 A["L0_ffn_Wd"].rearrange("e (c p) d -> p e c d", p=P)),
            ):
                eng.dma_start(dst, src).then_inc(C.s_w[kind], 16)
            eng.wait_ge(C.s_zero, 1)
            for dst, n in ((C.hs_dram[0:PAST, :], NS), (C.ys_dram[PAST:PAST + P, :], 1)):
                eng.dma_start(dst.rearrange("(t p) d -> p t d", p=P),
                              C.zeros[:, 0:1, :].to_broadcast([P, n, D])).then_inc(C.s_zeroed, 16)

        def load_block_weights(eng):
            def row(name):
                return A[name].rearrange("(a n) -> a n", a=1).to_broadcast([P, D])

            def column(name):
                return A[name].rearrange("(p a) -> p a", a=1)

            for dst, src in (
                (W.wqT[:, :], A["wqT"]), (W.wqrT[:, :], A["wqrT"]), (W.wkT[:, :], A["wkT"]),
                (W.wkrT[:, :], A["wkrT"]), (W.wvT[:, :], A["wvT"]), (W.woT[:, :], A["woT"]),
                (W.w1T[:, :], A["w1T"]), (W.w2T[:, :, :], A["w2T"].rearrange("(c p) d -> p c d", p=P)),
                (W.b1[:, :], A["b1_columns"]),
                (W.b2[:, :], row("L0_attn_b2")), (W.ls1[:, :], row("L0_attn_ls1")), (W.ls2[:, :], row("L0_attn_ls2")),
                (W.n1w[:, :], column("L0_attn_norm1_w")), (W.n1b[:, :], column("L0_attn_norm1_b")),
                (W.n2w[:, :], column("L0_attn_norm2_w")), (W.n2b[:, :], column("L0_attn_norm2_b")),
            ):
                eng.dma_start(dst, src).then_inc(C.s_w2, 16)
        def make_consts(nc, dve):
            dve.memset(C.zeros[:, :, :], 0.0).then_inc(C.s_zero, 1)
            dve.wait_ge(C.s_const, 16)
            dve.tensor_copy(C.before[:, :], C.c[:, Consts.BEFORE:Consts.BEFORE + P]).then_inc(C.s_bits, 1)
            dve.memset(C.ones[:, :], 1.0).then_inc(C.s_bits, 1)
            dve.tensor_copy(C.identb[:, :], C.c[:, Consts.IDENT:Consts.IDENT + P])
            dve.wait_ge(C.s_mask, 16)
            dve.tensor_copy(C.masksT[:, :], C.masks32[:, 2 * P:4 * P]).then_inc(C.s_bits, 1)

        C.zeros = sb("zeros", [P, 1, D])
        C.s_mask = sem("masks_loaded")
        C.s_w2 = sem("block_weights_loaded")
        C.masks32 = sb("masks32", [P, 4 * P])
        C.masksT = sb("masksT", [P, 2 * P], bf16)
        C.identb = sb("identb", [P, P], bf16)
        W.wqT, W.wqrT, W.wkT, W.wkrT, W.wvT, W.woT = (
            sb(n + "_sb", [D, D]) for n in ("wqT", "wqrT", "wkT", "wkrT", "wvT", "woT"))
        W.w1T = sb("w1T_sb", [D, HID])
        W.w2T = sb("w2T_sb", [P, HC, D])
        W.b1 = sb("b1_sb", [P, HC])
        W.b2, W.ls1, W.ls2 = (sb(n + "_rows", [P, D]) for n in ("b2", "ls1", "ls2"))
        W.n1w, W.n1b, W.n2w, W.n2b = (sb(n + "_col", [D, 1]) for n in ("n1w", "n1b", "n2w", "n2b"))
        C.N_W2 = 16
        z = sb("z_rows", [P, NT, D])
        C.load_consts, C.load_moe_weights, C.load_block_weights, C.make_consts = (
            load_consts, load_moe_weights, load_block_weights, make_consts)

        x_in = A["L0_attn_x"].rearrange("b s d -> (b s) d")
        x_out = out.rearrange("b s d -> (b s) d")
        moe(nc, C, W, x_sb, z, "m1", x_in, None)
        attention(nc, A, C, W, x_sb, z)
        ffn(nc, C, W, x_sb, z)
        if upto == "x2":
            store(nc, x_sb, x_out)
            return
        moe(nc, C, W, x_sb, z, "m2", None, x_out)


_INS = ["L0_attn_x", "L0_attn_norm1_w", "L0_attn_norm1_b", "L0_attn_norm2_w", "L0_attn_norm2_b",
        "L0_attn_b2", "L0_attn_ls1", "L0_attn_ls2",
        "L0_ffn_Wr", "L0_ffn_Wu", "L0_ffn_Wg", "L0_ffn_Wd", "L0_ffn_Wu_s", "L0_ffn_Wg_s", "L0_ffn_Wd_s"]


def inputs_for_launch(inputs):
    a = {n: np.ascontiguousarray(inputs[n]) for n in _INS}
    turned = np.concatenate([np.arange(HD // 2, HD), np.arange(HD // 2)])
    plain = (np.arange(HEADS)[None, :] * HD + np.arange(HD)[:, None]).reshape(-1)
    rows = (np.arange(HEADS)[None, :] * HD + turned[:, None]).reshape(-1)
    wq, wk = np.asarray(inputs["L0_attn_wq"]), np.asarray(inputs["L0_attn_wk"])
    for n, w in (("wqT", wq[plain]), ("wqrT", wq[rows]), ("wkT", wk[plain]), ("wkrT", wk[rows]),
                 ("wvT", np.asarray(inputs["L0_attn_wv"])), ("woT", np.asarray(inputs["L0_attn_wo"])),
                 ("w1T", np.asarray(inputs["L0_attn_w1"])), ("w2T", np.asarray(inputs["L0_attn_w2"]))):
        a[n] = np.ascontiguousarray(w.T)
    a["b1_columns"] = np.ascontiguousarray(np.asarray(inputs["L0_attn_b1"]).reshape(HC, P).T)
    a["stack_fill"] = np.repeat(np.array([[0x0000], [0xBF80]], np.uint16), HEADS * 512, axis=1)
    a["const_table"], a["cos_table"], a["sin_table"], a["mask_table"] = const_tables()
    return a


def kernel(**inputs):
    import concourse.bacc as bacc
    from concourse.bass_utils import run_bass_kernel_spmd

    nc = bacc.Bacc("TRN2", target_bir_lowering=False, num_devices=1)
    arrays = inputs_for_launch(inputs)
    args = {n: nc.dram_tensor(n, a.shape, mybir.dt.from_np(a.dtype), kind="ExternalInput").ap()
            for n, a in arrays.items()}
    out = nc.dram_tensor("out", (1, SEQ, D), fp32, kind="ExternalOutput").ap()
    program(nc, args, out)
    r = run_bass_kernel_spmd(nc, [arrays], core_ids=[0])
    return r.results[0]["out"]
```

```python
import numpy as np
import concourse.bass as bass
from concourse import mybir
from contextlib import ExitStack

fp32 = mybir.dt.float32
bf16 = mybir.dt.bfloat16
u32 = mybir.dt.uint32
i32 = mybir.dt.int32
ALU = mybir.AluOpType
ACT = mybir.ActivationFunctionType
AX = mybir.AxisListType

P = 128
D = 128
SEQ = 2048
NT = SEQ // P
CH = 4
NCH = NT // CH
HID = 512
HC = HID // P
NE = 8
NX = NE - 1
NS = (SEQ + NX * (P - 1)) // P
PAST = NS * P
EPS = 1e-5
HEADS = 16
HD = D // HEADS
WINDOW = 125
NEG = -1e30


class Chain:

    def __init__(self, eng, sem):
        self.eng, self.sem, self.n = eng, sem, 0

    def mark(self, ins):
        self.n += 1
        ins.then_inc(self.sem, 1)
        return self.n

    def link(self, ins):
        self.eng.wait_ge(self.sem, self.mark(ins))


class Consts:
    IDENT = 0
    BEFORE = IDENT + P
    IOTA8 = BEFORE + P
    KTILE = IOTA8 + NE
    ITILE = KTILE + NT
    HALF = ITILE + NS * (NX - 1)
    ROW = HALF + NT
    NO_ROW = ROW + NT
    WIDTH = NO_ROW + NS


def const_tables():
    c = np.zeros((P, Consts.WIDTH), np.float32)
    r = np.arange(P)
    c[:, Consts.IDENT:Consts.IDENT + P] = np.eye(P)
    c[:, Consts.BEFORE:Consts.BEFORE + P] = r[:, None] < r[None, :]
    c[:, Consts.IOTA8:Consts.IOTA8 + NE] = np.arange(NE) - NE
    c[:, Consts.KTILE:Consts.KTILE + NT] = np.arange(NT) * P
    c[:, Consts.ITILE:Consts.HALF] = np.repeat(np.arange(NS), NX - 1)
    c[:, Consts.HALF:Consts.ROW] = -0.5
    c[:, Consts.ROW:Consts.NO_ROW] = np.arange(NT) * P + r[:, None]
    c[:, Consts.NO_ROW:] = SEQ + np.arange(NS) * P + r[:, None]
    inv = (1.0 / np.float32(10000.0) ** (np.arange(0, HD, 2, dtype=np.float32) / HD)).astype(np.float32)
    ang = np.outer(np.arange(SEQ, dtype=np.float32), inv).astype(np.float32)
    ang = np.concatenate([ang, ang], axis=1)
    sign = np.where(np.arange(HD) < HD // 2, -1.0, 1.0)
    cos = np.repeat(np.cos(ang).T, HEADS, axis=0).astype(np.float32)
    sin = np.repeat((np.sin(ang) * sign).T, HEADS, axis=0).astype(np.float32)
    q, k = np.arange(P)[:, None], np.arange(2 * P)[None, :] - P
    ok = (q - k >= 0) & (q - k < WINDOW)
    mask = np.where(ok, 0.0, NEG).astype(np.float32)
    masks = np.concatenate([mask, mask[:, :P].T, mask[:, P:].T], axis=1)
    return c, cos, sin, masks


class SharedExpert:

    def __init__(self, nc, ctx, tag, W, hT, x_sb, lo, hi, pU, pG, pY, sg):
        def sem(name):
            return ctx.enter_context(nc.semaphore(f"{tag}_shared_{name}"))

        self.W, self.hT, self.x_sb, self.pU, self.pG, self.pY, self.sg = W, hT, x_sb, pU, pG, pY, sg
        self.lo, self.n, self.steps = lo, hi - lo, (hi - lo) * HC
        self.bufs = min(2, hi - lo)
        self.aT = ctx.enter_context(nc.sbuf_tensor(f"{tag}_shared_aT", [P, self.bufs * HC, 512], fp32))
        self.up_done = sem("up_done")
        self.silu_done = sem("silu_done")
        self.a_ready = sem("a_ready")
        self.down_done = sem("down_done")
        self.added = sem("added")

    def rows(self, c):
        return slice(512 * (self.lo + c), 512 * (self.lo + c) + 512)

    def pe_up(self, pe, k):
        c, j = divmod(k, HC)
        if k >= 2:
            pe.wait_ge(self.a_ready, k - 1)
        pe.matmul(self.pG[k % 2], self.W.Wgs[:, P * j:P * j + P], self.hT[:, self.rows(c)], start=True, stop=True)
        pe.matmul(self.pU[k % 2], self.W.Wus[:, P * j:P * j + P], self.hT[:, self.rows(c)], start=True,
                  stop=True).then_inc(self.up_done, 1)

    def pe_down(self, pe, c):
        pe.wait_ge(self.a_ready, HC * c + HC)
        if c >= 1:
            pe.wait_ge(self.added, c)
        b = HC * (c % self.bufs)
        for t in range(CH):
            for j in range(HC):
                last = pe.matmul(self.pY[:, P * t:P * t + P], self.aT[:, b + j, P * t:P * t + P], self.W.Wds[:, j, :],
                                 start=j == 0, stop=j == HC - 1)
        last.then_inc(self.down_done, 1)

    def act_silu(self, act, k):
        act.wait_ge(self.up_done, k + 1)
        if k >= 2:
            act.wait_ge(self.a_ready, k - 1)
        act.activation(self.sg[:, k % 2, :], self.pG[k % 2], ACT.Silu).then_inc(self.silu_done, 1)

    def dve_mult(self, dve, k):
        c, j = divmod(k, HC)
        dve.wait_ge(self.silu_done, k + 1)
        if c >= self.bufs:
            dve.wait_ge(self.down_done, c - self.bufs + 1)
        dve.tensor_tensor(self.aT[:, HC * (c % self.bufs) + j, :], self.pU[k % 2], self.sg[:, k % 2, :], ALU.mult
                          ).then_inc(self.a_ready, 1)

    def dve_add(self, dve, c):
        dve.wait_ge(self.down_done, c + 1)
        x = self.x_sb[:, CH * (self.lo + c):CH * (self.lo + c) + CH, :]
        dve.scalar_tensor_tensor(x, self.pY.rearrange("p (t d) -> p t d", d=D), 0.5, x, ALU.mult, ALU.add
                                 ).then_inc(self.added, 1)


FRONT = 2
FRONT_STEPS = HC * FRONT + 4
BACK = FRONT


LEFT = 2


def scatter_result(pool, C, tag, i):
    pool.wait_ge(C.y_ready[tag], i + 1)
    pool.indirect_dma_start(C.y_dram[tag], bass.IndirectOffsetOnAxis(C.row_of[:, i:i + 1], 0),
                            C.ys[:, i % 4, :], None).then_inc(C.y_stored[tag][i % 4], 16)


def load_results(sp, C, z, tag):
    for k in range(4):
        sp.wait_ge(C.y_stored[tag][k], 16 * len(range(k, NS, 4)))
    for g in range(NCH):
        sp.dma_start(z[:, CH * g:CH * g + CH, :],
                     C.y_dram[tag][512 * g:512 * g + 512, :].rearrange("(t p) d -> p t d", p=P)
                     ).then_inc(C.gathered[tag][g], 16)


def moe(nc, C, W, x_sb, z, tag, x_in, x_out):
    first = x_in is not None
    NORM_FROM = 0 if first else NCH - 1
    front_steps = HC * FRONT if first else FRONT_STEPS
    ctx = ExitStack()
    with ctx:
        def sb(name, shape, dt=fp32):
            return ctx.enter_context(nc.sbuf_tensor(f"{tag}_{name}", shape, dt))

        def sem(name):
            return ctx.enter_context(nc.semaphore(f"{tag}_{name}"))

        bank = [ctx.enter_context(nc.psum_tensor(f"{tag}_bank{k}", [P, 512], fp32)) for k in range(8)]
        pX = bank[0]
        pR = bank[1]
        pU, pG = bank[2:4], bank[4:6]
        pAT = bank[6]
        pY = [bank[7], bank[1]]

        stats = sb("stats", [P, NT, 6])
        mv = sb("mv", [P, NT, 2])
        rstd = sb("rstd", [P, NT])
        h = C.h
        hT = C.hT
        lg = sb("lg", [P, NT, NE])
        top = sb("top", [P, NT])
        ex = sb("ex", [P, NT, NE])
        prob = C.prob
        onehot = sb("onehot", [P, NT + 1, NE], bf16)
        cnt = sb("cnt", [P, NE, NT])
        tiles = sb("tiles", [P, NE])
        ends = sb("ends", [P, NE])
        base = sb("base", [P, NE])
        ones8 = sb("ones8", [P, NE])
        slot = sb("slot", [P, NT])
        put_at = sb("put_at", [P, NT], u32)
        past = sb("past", [1, NS, NX - 1])
        eidf = sb("eidf", [1, NS])
        eid = sb("eid", [1, NS], i32)
        sg = sb("sg", [P, 2, HID])
        xs = sb("xs", [P, NS, D + 1])
        xsT = sb("xsT", [P, 2, P])
        a = sb("a", [P, 2, HID])
        eT = sb("eT", [P, 2, HC, P])
        ys = C.ys
        shared = SharedExpert(nc, ctx, tag, W, hT, x_sb, 0, BACK if first else NCH, [b[:, :] for b in pU],
                              [b[:, :] for b in pG], pY[0][:, :], sg)

        s_x = [sem(f"x_loaded{g}") for g in range(NCH)]
        s_v = sem("dve_chain")
        s_vareps = sem("var_ready")
        s_rstd = sem("rstd_ready")
        s_h = sem("h_ready")
        s_tr = sem("h_transposed")
        s_hT = sem("hT_ready")
        s_lg = sem("logits_done")
        s_ex_in = sem("exp_input")
        s_ex = sem("exp_done")
        s_oh = sem("onehot_ready")
        s_rank = sem("ranks_done")
        s_put_at = sem("put_at_ready")
        s_eid = sem("eid_ready")
        s_scat = sem("rows_scattered")
        s_xs = [sem(f"sorted_loaded{k}") for k in range(4)]
        e_tr = sem("sorted_transposed")
        e_xsT = sem("xsT_ready")
        e_up = sem("expert_up_done")
        e_silu = sem("expert_silu_done")
        e_a = sem("expert_a_ready")
        e_at = sem("expert_a_transposed")
        e_eT = sem("eT_ready")
        e_dn = sem("expert_down_done")
        e_y = C.y_ready[tag]
        s_blank = sem("blank_slots_ready")
        s_ys = C.y_stored[tag]
        gathered = C.gathered[tag]
        combined = sem("combined")
        s_out = sem("out_stored")
        s_rows = sem("pool_chain")

        load_parts = [(0, 2), (2, 6), (6, 14), (14, NS)]
        hs_rows = C.hs_dram[tag].rearrange("(t p) d -> p t d", p=P)

        block = ctx.enter_context(nc.Block())

        @block.sync
        def _(sp):
            if first:
                for g in range(NCH):
                    sp.dma_start(x_sb[:, CH * g:CH * g + CH, :],
                                 x_in.rearrange("(t p) d -> p t d", p=P)[:, CH * g:CH * g + CH, :]
                                 ).then_inc(s_x[g], 16)
                C.load_moe_weights(sp, 2)
                sp.wait_ge(s_blank, 1)
                for each in ("m1", "m2"):
                    sp.dma_start(C.hs_dram[each][0:PAST, :].rearrange("(t p) d -> p t d", p=P), xs[:, :, :]
                                 ).then_inc(C.s_blanked, 16)
                C.load_moe_weights(sp, 3)
            sp.wait_ge(s_scat, 16 * NT)
            for k, (lo, hi) in enumerate(load_parts):
                sp.dma_start(xs[:, lo:hi, :], hs_rows[:, lo:hi, :]).then_inc(s_xs[k], 16)
            if first:
                sp.wait_ge(C.s_zero, 1)
                for each in ("m1", "m2"):
                    sp.dma_start(C.y_dram[each][0:SEQ, :].rearrange("(t p) d -> p t d", p=P),
                                 C.zeros[:, 0:1, :].to_broadcast([P, NT, D])).then_inc(C.s_zeroed[each], 16)
                C.load_block_weights(sp)
            else:
                load_results(sp, C, z, tag)
                out_rows = x_out.rearrange("(t p) d -> p t d", p=P)
                for g, combined_tiles in enumerate((CH, 2 * CH, 3 * CH, NT)):
                    sp.wait_ge(combined, combined_tiles)
                    sp.wait_ge(shared.added, g + 1)
                    sp.dma_start(out_rows[:, CH * g:CH * g + CH, :], x_sb[:, CH * g:CH * g + CH, :]
                                 ).then_inc(s_out, 16)
                sp.wait_ge(s_out, 16 * NCH)

        @block.gpsimd
        def _(pool):
            pool.wait_ge(C.s_const, 16)
            if first:
                ch = Chain(pool, s_rows)
                ch.link(pool.memset(xs[:, :, :], 0.0))
                pool.tensor_copy(xs[:, :, D:D + 1].bitcast(u32),
                                 C.c[:, Consts.NO_ROW:Consts.NO_ROW + NS].unsqueeze(2)).then_inc(s_blank, 1)
            for g in range(NORM_FROM, NCH):
                pool.wait_ge(s_vareps, g - NORM_FROM + 1)
                pool.tensor_tensor(rstd[:, CH * g:CH * g + CH], mv[:, CH * g:CH * g + CH, 1],
                                   C.c[:, Consts.HALF:Consts.HALF + CH], ALU.pow).then_inc(s_rstd, 1)
            if first:
                pool.wait_ge(C.s_blanked, 16 * 2)
            pool.wait_ge(s_put_at, 1)
            for t in range(NT):
                pool.indirect_dma_start(C.hs_dram[tag], bass.IndirectOffsetOnAxis(put_at[:, t:t + 1], 0),
                                        C.h_numbered[:, t, :], None).then_inc(s_scat, 16)
            for k, (lo, hi) in enumerate(load_parts):
                pool.wait_ge(s_xs[k], 16)
                copied = pool.tensor_copy(C.row_of[:, lo:hi].unsqueeze(2), xs[:, lo:hi, D:D + 1].bitcast(u32))
                copied.then_inc(s_rows, 1)
            pool.wait_ge(s_rows, len(load_parts) + (1 if first else 0))
            pool.wait_ge(C.s_zeroed[tag], 16)
            for i in range(NS - LEFT if first else NS):
                scatter_result(pool, C, tag, i)

        @block.scalar
        def _(act):
            if first:
                C.load_consts(act)

            def evac_hT(n):
                g = NORM_FROM + n
                act.wait_ge(s_tr, n + 1)
                act.activation(hT[:, 512 * g:512 * g + 512], [pX, pAT][g % 2][:, :], ACT.Copy).then_inc(s_hT, 1)

            for n in range(NCH - NORM_FROM):
                evac_hT(n)
            act.wait_ge(s_ex_in, 1)
            act.activation(ex[:, :, :], lg[:, :, :], ACT.Exp).then_inc(s_ex, 1)

            for k in range(front_steps):
                shared.act_silu(act, k)

            def evac_xsT(i):
                act.wait_ge(e_tr, i + 1)
                act.activation(xsT[:, i % 2, :], pX[:, 0:P], ACT.Copy).then_inc(e_xsT, 1)

            def store_y(i):
                act.wait_ge(e_dn, i + 1)
                if i >= 4:
                    act.wait_ge(s_ys[i % 4], 16 * (i // 4))
                act.activation(ys[:, i % 4, :], pY[i % 2][:, 0:P], ACT.Copy).then_inc(e_y, 1)

            evac_xsT(0)
            evac_xsT(1)
            for i in range(NS):
                act.wait_ge(e_up, i + 1)
                if i >= 2:
                    act.wait_ge(e_a, i - 1)
                else:
                    act.wait_ge(shared.a_ready, front_steps)
                act.activation(sg[:, i % 2, :], pG[i % 2][:, :], ACT.Silu).then_inc(e_silu, 1)
                if i >= 2:
                    store_y(i - 2)
                if i + 2 < NS:
                    evac_xsT(i + 2)
            store_y(NS - 2)
            store_y(NS - 1)
            act.wait_ge(e_a, NS)
            for k in range(front_steps, shared.steps):
                shared.act_silu(act, k)

        @block.vector
        def _(dve):
            ch = Chain(dve, s_v)
            if first:
                C.make_consts(nc, dve)
            dve.memset(ones8[:, :], 1.0)
            dve.memset(onehot[:, NT, :], 0.0)

            def statistics(g):
                if first:
                    dve.wait_ge(s_x[g], 16)
                for t in range(CH * g, CH * g + CH):
                    last = dve.bn_stats(stats[:, t, :], x_sb[:, t, :])
                ch.link(last)
                for t in range(CH * g, CH * g + CH):
                    last = dve.bn_aggr(mv[:, t, :], stats[:, t, :])
                ch.link(last)
                dve.tensor_scalar(mv[:, CH * g:CH * g + CH, 1], mv[:, CH * g:CH * g + CH, 1], EPS, None,
                                  ALU.add).then_inc(s_vareps, 1)

            def normalize(g):
                dve.wait_ge(s_rstd, g - NORM_FROM + 1)
                for t in range(CH * g, CH * g + CH):
                    dve.tensor_scalar(h[:, t, :], x_sb[:, t, :], mv[:, t, 0:1], rstd[:, t:t + 1],
                                      ALU.subtract, ALU.mult).then_inc(s_h, 1)

            statistics(NORM_FROM)
            for g in range(NORM_FROM, NCH):
                if g + 1 < NCH:
                    statistics(g + 1)
                normalize(g)

            plog = pR[:, 0:NT * NE].rearrange("p (t e) -> p t e", e=NE)
            dve.wait_ge(s_lg, 1)
            ch.link(dve.tensor_reduce(top[:, :], plog, AX.X, ALU.max))
            dve.tensor_tensor(lg[:, :, :], plog, top[:, :].unsqueeze(2).to_broadcast([P, NT, NE]),
                              ALU.subtract).then_inc(s_ex_in, 1)
            dve.wait_ge(s_ex_in, 1)
            ch.link(dve.tensor_scalar(cnt[:, :, :].rearrange("p e t -> p (e t)"),
                                      lg[:, :, :].rearrange("p t e -> p (t e)"), 0.0, -float(NE),
                                      ALU.is_ge, ALU.mult))
            cand = cnt[:, :, :].rearrange("p e t -> p (e t)").rearrange("p (t e) -> p t e", e=NE)
            iota = C.c[:, Consts.IOTA8:Consts.IOTA8 + NE].unsqueeze(1).to_broadcast([P, NT, NE])
            ch.link(dve.tensor_tensor(cand, cand, iota, ALU.add))
            ch.link(dve.tensor_reduce(top[:, :], cand, AX.X, ALU.min))
            ch.link(dve.tensor_scalar(top[:, :], top[:, :], float(NE), None, ALU.add))
            dve.tensor_tensor(onehot[:, 0:NT, :], iota, top[:, :].unsqueeze(2).to_broadcast([P, NT, NE]),
                              ALU.is_equal).then_inc(s_oh, 1)
            dve.wait_ge(s_ex, 1)
            ch.link(dve.tensor_reduce(prob[:, :], ex[:, :, :], AX.X, ALU.add))
            ch.link(dve.reciprocal(prob[:, :], prob[:, :]))
            shared.dve_mult(dve, 0)

            ranks = pR[:, 256:256 + (NT + 1) * NE].rearrange("p (t e) -> p t e", e=NE)
            dve.wait_ge(s_rank, 1)
            ch.link(dve.tensor_copy(tiles[:, :], ranks[:, NT, :]))
            ch.link(dve.tensor_tensor(cnt[:, :, :], tiles[:, :].unsqueeze(2).to_broadcast([P, NE, NT]),
                                      C.c[:, Consts.KTILE:Consts.KTILE + NT].unsqueeze(1).to_broadcast([P, NE, NT]),
                                      ALU.is_gt))
            ch.link(dve.tensor_reduce(tiles[:, :], cnt[:, :, :], AX.X, ALU.add))
            ch.link(dve.tensor_tensor_scan(ends[:, :], ones8[:, :], tiles[:, :], 0.0, ALU.mult, ALU.add))
            ch.link(dve.tensor_tensor(base[:, :], ends[:, :], tiles[:, :], ALU.subtract))
            ch.link(dve.tensor_scalar(base[:, :], base[:, :], float(P), None, ALU.mult))
            ch.link(dve.memset(base[:, NX:NE], float(PAST)))
            ch.link(dve.tensor_tensor(ex[:, :, :], ranks[:, 0:NT, :],
                                      base[:, :].unsqueeze(1).to_broadcast([P, NT, NE]), ALU.add))
            ch.link(dve.tensor_tensor(ex[:, :, :], ex[:, :, :], onehot[:, 0:NT, :], ALU.mult))
            ch.link(dve.tensor_reduce(slot[:, :], ex[:, :, :], AX.X, ALU.add))
            dve.tensor_copy(put_at[:, :], slot[:, :]).then_inc(s_put_at, 1)
            ch.link(dve.tensor_tensor(past[:, :, :],
                                      C.c[0:1, Consts.ITILE:Consts.HALF].rearrange("p (i e) -> p i e", e=NX - 1),
                                      ends[0:1, 0:NX - 1].unsqueeze(1).to_broadcast([1, NS, NX - 1]), ALU.is_ge))
            ch.link(dve.tensor_reduce(eidf[:, :], past[:, :, :], AX.X, ALU.add))
            dve.tensor_copy(eid[:, :], eidf[:, :]).then_inc(s_eid, 1)

            for k in range(1, front_steps):
                shared.dve_mult(dve, k)
                if k % HC == 2 and k > HC:
                    shared.dve_add(dve, k // HC - 1)
            if front_steps <= HC * FRONT + 2:
                shared.dve_add(dve, FRONT - 1)

            def evac_eT(i):
                dve.wait_ge(e_at, i + 1)
                dve.tensor_copy(eT[:, i % 2, :, :], pAT[:, :].rearrange("p (c r) -> p c r", r=P)).then_inc(e_eT, 1)

            for i in range(NS):
                if i >= 2:
                    evac_eT(i - 2)
                dve.wait_ge(e_silu, i + 1)
                dve.tensor_tensor(a[:, i % 2, :], pU[i % 2][:, :], sg[:, i % 2, :], ALU.mult).then_inc(e_a, 1)
            evac_eT(NS - 2)
            evac_eT(NS - 1)

            def combine(g):
                dve.wait_ge(gathered[g], 16)
                for t in range(CH * g, CH * g + CH):
                    dve.scalar_tensor_tensor(x_sb[:, t, :], z[:, t, :], prob[:, t:t + 1], x_sb[:, t, :],
                                             ALU.mult, ALU.add).then_inc(combined, 1)

            for k in range(front_steps, shared.steps):
                shared.dve_mult(dve, k)
                if k == HC * NCH - 3:
                    combine(0)
                    combine(1)
                if k == HC * NCH - 2:
                    shared.dve_add(dve, 2)
            if not first:
                dve.wait_ge(shared.added, 3)
                combine(2)
                combine(3)
                dve.wait_ge(combined, NT)
                shared.dve_add(dve, 3)

        @block.tensor
        def _(pe):
            ident = C.c[:, Consts.IDENT:Consts.IDENT + P]
            if first:
                pe.wait_ge(C.s_const, 16)
                pe.wait_ge(C.s_bits, 3)

            def turn(n):
                g = NORM_FROM + n
                pe.wait_ge(s_h, CH * n + CH)
                if n >= 2:
                    pe.wait_ge(s_hT, n - 1)
                for j in range(CH):
                    last = pe.transpose([pX, pAT][g % 2][:, P * j:P * j + P], h[:, CH * g + j, :], ident)
                last.then_inc(s_tr, 1)

            def logits(g):
                if g >= NORM_FROM:
                    pe.wait_ge(s_hT, g - NORM_FROM + 1)
                for t in range(CH * g, CH * g + CH):
                    last = pe.matmul(pR[:, NE * t:NE * t + NE], hT[:, P * t:P * t + P], W.Wr[:, :],
                                     start=True, stop=True)
                if g == NCH - 1:
                    last.then_inc(s_lg, 1)

            if first:
                turn(0)
                turn(1)
                pe.wait_ge(C.s_w[0], 16)
                logits(0)
                turn(2)
                logits(1)
                turn(3)
            else:
                logits(0)
                logits(1)
                turn(0)
            logits(2)
            logits(3)
            if first:
                pe.wait_ge(C.s_w[1], 16 * 3)
            shared.pe_up(pe, 0)

            def rank():
                pe.wait_ge(s_oh, 1)
                R = pR[:, 256:256 + (NT + 1) * NE]
                pe.matmul(R, C.before[:, :], onehot[:, :, :].rearrange("p t e -> p (t e)"), start=True, stop=False)
                for s in range(NT):
                    last = pe.matmul(R[:, NE * (s + 1):].rearrange("p (t e) -> p t e", e=NE), C.ones[:, :],
                                     onehot[:, s, :].unsqueeze(1).to_broadcast([P, NT - s, NE]),
                                     start=False, stop=s == NT - 1)
                last.then_inc(s_rank, 1)

            rank()
            for k in range(1, front_steps):
                shared.pe_up(pe, k)
                if k % HC == 1 and k > HC:
                    shared.pe_down(pe, k // HC - 1)
            if front_steps == HC * FRONT:
                shared.pe_down(pe, FRONT - 1)

            def expert_transpose(i):
                for k, (lo, hi) in enumerate(load_parts):
                    if i == lo:
                        pe.wait_ge(s_xs[k], 16)
                if i >= 1:
                    pe.wait_ge(e_xsT, i)
                pe.transpose(pX[:, 0:P], xs[:, i, 0:D], ident).then_inc(e_tr, 1)

            expert = []

            def load_experts():
                regs = [pe.alloc_register(f"{tag}_expert{i}") for i in range(NS)]
                pe.load(regs, eid[0:1, 0:NS])
                expert.extend(pe.snap(x, donate=True, min_val=0, max_val=NX - 1) for x in regs)

            def expert_up(i):
                e = expert[i]
                pe.wait_ge(e_xsT, i + 1)
                if i >= 2:
                    pe.wait_ge(e_a, i - 1)
                else:
                    pe.wait_ge(shared.a_ready, front_steps - 1 + i)
                pe.matmul(pG[i % 2][:, :], xsT[:, i % 2, :], W.Wg[:, bass.ds(e * HID, HID)], start=True, stop=True)
                pe.matmul(pU[i % 2][:, :], xsT[:, i % 2, :], W.Wu[:, bass.ds(e * HID, HID)], start=True,
                          stop=True).then_inc(e_up, 1)

            def expert_aT(i):
                pe.wait_ge(e_a, i + 1)
                if i >= 1:
                    pe.wait_ge(e_eT, i)
                for c in range(HC):
                    last = pe.transpose(pAT[:, P * c:P * c + P], a[:, i % 2, P * c:P * c + P], ident)
                last.then_inc(e_at, 1)

            def expert_down(i):
                e = expert[i]
                pe.wait_ge(e_eT, i + 1)
                if i >= 2:
                    pe.wait_ge(e_y, i - 1)
                for c in range(HC):
                    last = pe.matmul(pY[i % 2][:, 0:P], eT[:, i % 2, c, :], W.Wd[:, bass.ds(e * HID + c * P, P)],
                                     start=c == 0, stop=c == HC - 1)
                last.then_inc(e_dn, 1)

            pe.wait_ge(s_eid, 1)
            load_experts()
            pe.wait_ge(shared.added, FRONT)
            if first:
                pe.wait_ge(C.s_w[2], 16 * 3)
            expert_transpose(0)
            expert_transpose(1)
            expert_up(0)
            for i in range(NS):
                if i + 1 < NS:
                    expert_up(i + 1)
                if i + 2 < NS:
                    expert_transpose(i + 2)
                expert_aT(i)
                if i >= 1:
                    expert_down(i - 1)
            expert_down(NS - 1)

            for k in range(front_steps, shared.steps):
                shared.pe_up(pe, k)
                if k % HC == 1:
                    pe.wait_ge(e_y, NS)
                    shared.pe_down(pe, k // HC - 1)
            if front_steps < shared.steps:
                pe.wait_ge(e_y, NS)
                shared.pe_down(pe, shared.n - 1)


def layer_norm(dve, ch, src, stats, mv, dst, s_var, s_rstd, rstd, lo, hi, nth, s_done):
    for t in range(lo, hi):
        last = dve.bn_stats(stats[:, t, :], src[:, t, :])
    ch.link(last)
    for t in range(lo, hi):
        last = dve.bn_aggr(mv[:, t, :], stats[:, t, :])
    ch.link(last)
    dve.tensor_scalar(mv[:, lo:hi, 1], mv[:, lo:hi, 1], EPS, None, ALU.add).then_inc(s_var, 1)
    dve.wait_ge(s_rstd, nth + 1)
    for t in range(lo, hi):
        last = dve.tensor_scalar(dst[:, t, :], src[:, t, :], mv[:, t, 0:1], rstd[:, t:t + 1],
                                 ALU.subtract, ALU.mult)
        last.then_inc(s_done, 1)


SH = 2
SPT = HEADS // SH
NK = NT * SPT
LAG = 16
VALUES_AFTER = 2
FIRST_LATER = 0.9
MAX_AT, V_AT = 10.5, 17.0
OUT_AT = (1, 2, 3.5)
NORM2_AT = (4.5, 8.5, 12.0)
NORM_AT = ((-3, -2, -1), (-15, -14, -10), (-14, -4, -1), (-14, -2, 0))
TURN_AT = (0, -4, 1.0, 2.5)
PROJ_AT = ((6, 7, 14, 15), (-1, 1.5, 9, 10), (6, 7, 14, 14), (6, 7, 14, 15))
SPLIT_AT = ((9.2, 17.2, 0), (4.7, 12.2, 2), (9.2, 17.2, 0), (9.2, 17.2, 0))
MROW = HD * 6
Q_PARTS = (0, 0, 1, 1, 0, 2)
K_PARTS = (0, 1, 0, 1, 2, 0)


def attention_timeline():
    ev = []
    for k in range(NK):
        ev.append((k, 0, ("scores", k)))
        ev.append((k + LAG, 1, ("turned", k)))
        ev.append((k + LAG + VALUES_AFTER + (FIRST_LATER if k % SPT == 0 else 0), 2, ("values", k)))
    for t in range(NT):
        k = SPT * t
        ev.append((k + 9, 0, ("max_split", t)))
        ev.append((k + MAX_AT, 3, ("max_turn", t)))
        ev.append((k + MAX_AT + 0.2, 3, ("max_rows", t)))
        ev.append((k + V_AT, 3, ("v", t)))
        done = k + LAG + VALUES_AFTER + SPT
        ev.append((done - 0.9, 3, ("drain", t)))
        for s in range(3):
            ev.append((done + OUT_AT[s], 3, ("out", t, s)))
        if t % CH == CH - 1 and t < NT - 1:
            c = t // CH
            for s in range(2):
                ev.append((done + NORM2_AT[s], 3, ("norm", c, 3 + s)))
            ev.append((done + NORM2_AT[2], 3, ("turn2", c)))
    for c in range(NCH):
        base = SPT * CH * (c - 1)
        for s in range(3):
            ev.append((base + NORM_AT[c][s], 3, ("norm", c, s)))
        ev.append((base + TURN_AT[c], 3, ("turn", c)))
        for s, at in enumerate(PROJ_AT[c]):
            ev.append((base + at, 3, ("proj", c, s)))
        for which in range(2):
            at, pace = SPLIT_AT[c][which], SPLIT_AT[c][2]
            for i in range(5):
                ev.append((base + at + pace * i, 3, ("split", c, which, i)))
            ready = base + at + 5 * pace + 1
            free = base + LAG + 1 + SPT * which
            ev.append((max(ready, free) if c else base + 27 - 0.1 * which, 3, ("stack", c, which)))
    ev.sort(key=lambda e: e[:2])
    return [e[2] for e in ev]


def attention(nc, A, C, W, x_sb, z):
    ctx = ExitStack()
    with ctx:
        def sb(name, shape, dt=fp32):
            return ctx.enter_context(nc.sbuf_tensor(f"att_{name}", shape, dt))

        def sem(name):
            return ctx.enter_context(nc.semaphore(f"att_{name}"))

        pS = [ctx.enter_context(nc.psum_tensor(f"att_scores{k}", [P, SH, 2 * P], fp32)) for k in range(3)]
        pT = [ctx.enter_context(nc.psum_tensor(f"att_turned{k}", [P, SH, 2, P], fp32)) for k in range(3)]
        pO = ctx.enter_context(nc.psum_tensor("att_out", [P, 512], fp32))
        pM = ctx.enter_context(nc.psum_tensor("att_jobs", [P, 512], fp32))

        def flat_bank(p):
            return p[:, :, :].rearrange("p i k -> p (i k)") if len(p.shape) == 3 else \
                p[:, :, :, :].rearrange("p i s k -> p (i s k)")

        sg = sb("shared_sg", [P, 2, HID])
        shared = SharedExpert(nc, ctx, "att", W, C.hT, x_sb, BACK, NCH, [flat_bank(pS[0]), flat_bank(pS[1])],
                              [flat_bank(pT[0]), flat_bank(pT[1])], flat_bank(pS[2]), sg)
        proj_bank = {("proj", 0, 1): flat_bank(pT[2]), ("proj", 0, 2): pO[:, :]}

        stats = sb("stats", [P, NT, 6])
        mv = sb("mv", [P, NT, 2])
        rstd = sb("rstd", [P, NT])
        h, hT = C.h, C.hT
        part = sb("rope", [P, 2, 2, 512])
        rot = sb("rotary", [P, 2, 2, 512])
        split = [sb(f"split{k}", [P, 3, 512], bf16) for k in range(2)]
        qs = sb("q_stack", [P, 2, HEADS, 512], bf16)
        ks = sb("k_stack", [P, HEADS, 2, 512], bf16)
        va = sb("v_ones", [P, 3, HEADS, 2 * HD])
        mx = sb("mx", [P, 4, HEADS])
        mrest = sb("mx_rest", [P, HEADS])
        mparts = sb("mx_parts", [P, 2, 3 * HEADS], bf16)
        mrows = sb("mx_rows", [3 * HEADS, 2, P], bf16)
        pt = shared.aT[:, 0:HC, :].rearrange("p a (h s q) -> p a h s q", h=SH, s=2)
        oT = sg[:, 0, :].rearrange("p (s q) -> p s q", q=P)
        junk = sg[:, 1, :].bitcast(bf16).rearrange("p (n k) -> p n k", n=4)
        den = sb("den", [P, HEADS])
        o = shared.aT[:, HC, 0:D]
        oo = shared.aT[:, HC, D:2 * D]

        s_v = sem("dve_chain")
        s_p = sem("pool_chain")
        s_var = sem("var_ready")
        s_rstd = sem("rstd_ready")
        s_h = sem("h_ready")
        s_hT = sem("hT_ready")
        s_fill = [sem(f"stack_rows_filled{k}") for k in range(2)]
        s_va = sem("v_ones_set")
        s_comb = sem("combined")
        s_full = sem("job_bank_full")
        s_free = sem("job_bank_free")
        s_rope = sem("rope_terms_ready")
        s_split = [sem(f"{k}_parts_ready") for k in "qk"]
        s_rot = [sem(f"rotary_loaded{k}") for k in range(2)]
        s_stack = [sem(f"{k}_stacked") for k in "qk"]
        s_S = sem("scores_done")
        s_max = sem("max_ready")
        s_ms = sem("max_parts_ready")
        s_mr = [sem(f"max_rows_ready{k}") for k in range(2)]
        s_T = sem("turned_done")
        s_exp = sem("exp_done")
        s_PV = sem("values_done")
        s_oe = sem("out_copied")

        timeline = attention_timeline()
        in_pM = ("max_turn", "v", "out", "turn", "proj", "turn2")
        job = {e: n for n, e in enumerate(e for e in timeline if e[0] in in_pM)}
        splits = {e: n for n, e in enumerate(e for e in timeline if e[0] == "split")}
        first = timeline.index(("scores", 0))
        early, main = timeline[:first], timeline[first:]
        STACKED = 16 * len(Q_PARTS)

        def split_part(eng, ch, c, which, i):
            a, b = part[:, which, 0, :], part[:, which, 1, :]
            p1, p2, p3 = (split[which][:, k, :] for k in range(3))
            if i == 0:
                eng.wait_ge(s_rope, 4 * c + 2 * which + 2)
                if c >= 1:
                    eng.wait_ge(s_stack[which], STACKED * c)
                eng.tensor_tensor(p1, a, b, ALU.add)
            if i == 1:
                ch.link(eng.tensor_tensor(a, a, b, ALU.add))
            if i == 2:
                eng.tensor_tensor(p2, a, p1, ALU.subtract)
            if i == 3:
                ch.link(eng.tensor_tensor(b, a, p1, ALU.subtract))
            if i == 4:
                eng.tensor_tensor(p3, b, p2, ALU.subtract).then_inc(s_split[which], 1)

        def walk(events, does):
            for e in events:
                if e[0] in does:
                    does[e[0]](*e[1:])

        block = ctx.enter_context(nc.Block())

        @block.sync
        def _(sp):
            def load_rotary(c):
                for k, name in enumerate(("cos_table", "sin_table")):
                    sp.dma_start(rot[:, c % 2, k, :], A[name][:, 512 * c:512 * c + 512]).then_inc(s_rot[c % 2], 16)

            stack_fill = A["stack_fill"].bitcast(bf16)

            def fill(k):
                zero = stack_fill[0:1, :].rearrange("a (h n) -> a h n", n=512)
                ones = stack_fill[1:2, :].rearrange("a (h n) -> a h n", n=512)
                rest = P - MROW - 3
                sp.dma_start(qs[MROW:P, k, :, :], zero.to_broadcast([P - MROW, HEADS, 512])).then_inc(s_fill[k], 16)
                sp.dma_start(ks[MROW:MROW + 3, :, k, :], ones.to_broadcast([3, HEADS, 512])).then_inc(s_fill[k], 16)
                sp.dma_start(ks[MROW + 3:P, :, k, :], zero.to_broadcast([rest, HEADS, 512])).then_inc(s_fill[k], 16)

            def stack(c, which):
                sp.wait_ge(s_split[which], c + 1)
                if c >= 2 and which == 0:
                    sp.wait_ge(s_T, SPT * CH * (c - 1))
                    zero = stack_fill[0:1, :].rearrange("a (h n) -> a h n", n=512)
                    sp.dma_start(qs[MROW:MROW + 3, c % 2, :, :], zero.to_broadcast([3, HEADS, 512])
                                 ).then_inc(s_fill[c % 2], 16)
                if c >= 2 and which == 1:
                    sp.wait_ge(s_T, SPT * (CH * (c - 1) + 1))
                to = qs[:, c % 2, :, :] if which == 0 else ks[:, :, c % 2, :]
                for m, k in enumerate((Q_PARTS, K_PARTS)[which]):
                    sp.dma_start(to[HD * m:HD * m + HD, :, :], split[which][:, k, :]).then_inc(s_stack[which], 16)
                if which == (c > 0) and c + 2 < NCH:
                    load_rotary(c + 2)

            def max_rows(t):
                c, j = divmod(t, CH)
                sp.wait_ge(s_free, job[("max_turn", t)] + 1)
                for k in range(3):
                    sp.dma_start(qs[MROW + k:MROW + k + 1, c % 2, :, P * j:P * j + P],
                                 mrows[HEADS * k:HEADS * k + HEADS, t % 2, :]).then_inc(s_mr[t % 2], 16)

            load_rotary(0)
            load_rotary(1)
            load_results(sp, C, z, "m1")
            fill(0)
            fill(1)
            walk(timeline, {"stack": stack, "max_rows": max_rows})

        @block.gpsimd
        def _(pool):
            ch = Chain(pool, s_p)
            norms = [0]

            def norm(c, s):
                if s in (2, 4):
                    return
                norms[0] += 1
                pool.wait_ge(s_var, norms[0])
                pool.tensor_tensor(rstd[:, CH * c:CH * c + CH], mv[:, CH * c:CH * c + CH, 1],
                                   C.c[:, Consts.HALF:Consts.HALF + CH], ALU.pow).then_inc(s_rstd, 1)

            def do_split(c, which, i):
                if (c, which) != (0, 1):
                    split_part(pool, ch, c, which, i)

            def max_split(t):
                pool.wait_ge(s_max, HEADS * (t + 1))
                m, (p1, p2, p3) = mx[:, t % 4, :], (mparts[:, t % 2, HEADS * k:HEADS * k + HEADS] for k in range(3))
                ch.link(pool.tensor_copy(p1, m))
                ch.link(pool.tensor_tensor(mrest[:, :], m, p1, ALU.subtract))
                ch.link(pool.tensor_copy(p2, mrest[:, :]))
                pool.tensor_tensor(p3, mrest[:, :], p2, ALU.subtract).then_inc(s_ms, 1)

            for i in range(NS - LEFT, NS):
                scatter_result(pool, C, "m1", i)
            walk(early, {"norm": norm, "split": do_split})
            walk(main, {"norm": norm, "split": do_split, "max_split": max_split})

        @block.scalar
        def _(act):
            def turn(c):
                act.wait_ge(s_full, job[("turn", c)] + 1)
                act.activation(hT[:, 512 * c:512 * c + 512], pM[:, :], ACT.Identity,
                               scale=W.n1w[:, 0:1], bias=W.n1b[:, 0:1]).then_inc(s_free, 1)

            def v(t):
                act.wait_ge(s_full, job[("v", t)] + 1)
                if t >= 3:
                    act.wait_ge(s_PV, SPT * (t - 1))
                act.activation(va[:, t % 3, :, 0:HD], pM[:, 0:P].rearrange("p (h d) -> p h d", d=HD),
                               ACT.Copy).then_inc(s_free, 1)

            def max_turn(t):
                act.wait_ge(s_full, job[("max_turn", t)] + 1)
                if t >= 2:
                    act.wait_ge(s_mr[t % 2], 48 * (t // 2))
                act.activation(mrows[:, t % 2, :], pM[:, 0:P // 2].bitcast(bf16)[0:3 * HEADS, :], ACT.Copy
                               ).then_inc(s_free, 1)

            def out(t, s):
                if s == 1:
                    act.wait_ge(s_full, job[("out", t, 1)] + 1)
                    act.activation(oo, pM[:, 0:P], ACT.Copy).then_inc(s_free, 1)

            def drain(t):
                act.wait_ge(s_PV, SPT * (t + 1))
                if t >= 1:
                    act.wait_ge(s_full, job[("out", t - 1, 0)] + 1)
                act.activation(oT[:, :, :], pO[:, :].rearrange("p (s q) -> p s q", q=P), ACT.Copy).then_inc(s_oe, 1)

            def turned(k):
                act.wait_ge(s_T, k + 1)
                if k >= 4:
                    act.wait_ge(s_PV, k - 3)
                if k < SPT:
                    src, dst = pT[k % 3][:, :, 1, :], pt[:, k % 4, :, 1, :]
                else:
                    src, dst = pT[k % 3][:, :, :, :], pt[:, k % 4, :, :, :]
                act.activation(dst, src, ACT.Exp).then_inc(s_exp, 1)

            def turn2(c):
                act.wait_ge(s_full, job[("turn2", c)] + 1)
                act.activation(hT[:, 512 * c:512 * c + 512], pM[:, :], ACT.Identity,
                               scale=W.n2w[:, 0:1], bias=W.n2b[:, 0:1]).then_inc(s_free, 1)

            for k in range(shared.steps - 1):
                shared.act_silu(act, k)
            turn(0)
            shared.act_silu(act, shared.steps - 1)
            walk(early[early.index(("turn", 0)) + 1:], {"turn": turn})
            act.wait_ge(s_va, 1)
            walk(main, {"turn": turn, "v": v, "max_turn": max_turn, "out": out, "turned": turned,
                        "turn2": turn2, "drain": drain})

        @block.vector
        def _(dve):
            ch = Chain(dve, s_v)
            norms = [0]

            def norm(c, s):
                lo, hi = CH * c, CH * c + CH
                if s == 0:
                    dve.wait_ge(C.gathered["m1"][c], 16)
                    if c >= BACK:
                        dve.wait_ge(shared.added, c - BACK + 1)
                    for t in range(lo, hi):
                        dve.scalar_tensor_tensor(x_sb[:, t, :], z[:, t, :], C.prob[:, t:t + 1], x_sb[:, t, :],
                                                 ALU.mult, ALU.add).then_inc(s_comb, 1)
                    dve.wait_ge(s_comb, hi)
                if s in (1, 2, 4):
                    dve.wait_ge(s_rstd, norms[0])
                    for t in range(lo, hi):
                        src, dst = (x_sb[:, t, :], z[:, t, :]) if s == 1 else (z[:, t, :], h[:, t, :])
                        last = dve.tensor_scalar(dst, src, mv[:, t, 0:1], rstd[:, t:t + 1],
                                                 ALU.subtract, ALU.mult)
                    if s != 1:
                        last.then_inc(s_h, 1)
                        return
                    ch.link(last)
                if s == 3:
                    dve.wait_ge(s_free, job[("out", c * CH + CH - 1, 2)] + 1)
                src = x_sb if s == 0 else z
                for t in range(lo, hi):
                    last = dve.bn_stats(stats[:, t, :], src[:, t, :])
                ch.link(last)
                for t in range(lo, hi):
                    last = dve.bn_aggr(mv[:, t, :], stats[:, t, :])
                ch.link(last)
                dve.tensor_scalar(mv[:, lo:hi, 1], mv[:, lo:hi, 1], EPS, None, ALU.add).then_inc(s_var, 1)
                norms[0] += 1

            def proj(c, s):
                dve.wait_ge(s_full, job[("proj", c, s)] + 1)
                dve.wait_ge(s_rot[c % 2], 32 * (c // 2 + 1))
                if c >= 1:
                    dve.wait_ge(s_split[s // 2], c)
                src = proj_bank.get(("proj", c, s), pM[:, :])
                dve.scalar_tensor_tensor(part[:, s // 2, s % 2, :], src, HD ** -0.5 if s < 2 else 1.0,
                                         rot[:, c % 2, s % 2, :], ALU.mult, ALU.mult).then_inc(s_rope, 1)
                dve.wait_ge(s_rope, 4 * c + s + 1)
                dve.sem_inc(s_free, 1)

            def out(t, s):
                if s == 0:
                    dve.wait_ge(s_full, job[("out", t, 0)] + 1)
                    rows = pM[:, :].rearrange("p (h w) -> p h w", w=32)
                    ch.link(dve.reciprocal(den[:, :].unsqueeze(2), rows[:, :, HD:HD + 1]))
                    if t >= 1:
                        dve.wait_ge(s_full, job[("out", t - 1, 1)] + 1)
                    dve.tensor_tensor(o.rearrange("p (h d) -> p h d", d=HD), rows[:, :, 0:HD],
                                      den[:, :].unsqueeze(2).to_broadcast([P, HEADS, HD]), ALU.mult
                                      ).then_inc(s_free, 1)
                if s == 2:
                    dve.wait_ge(s_full, job[("out", t, 2)] + 1)
                    dve.tensor_tensor(z[:, t, :], pM[:, 0:P], z[:, t, :], ALU.add).then_inc(s_free, 1)

            def scores(k):
                t = k // SPT
                dve.wait_ge(s_S, k + 1)
                for i in range(SH):
                    n = SH * k + i
                    head = n % HEADS
                    if n >= 4:
                        dve.wait_ge(s_max, n - 3)
                    if t >= 4 and head == 0:
                        dve.wait_ge(s_ms, t - 3)
                    keys = slice(0, 2 * P) if t else slice(P, 2 * P)
                    dve.tensor_tensor_reduce(junk[:, n % 4, keys], pS[k % 3][:, i, keys],
                                             C.masks32[:, keys], 1.0, -3e38, ALU.add, ALU.max,
                                             mx[:, t % 4, head:head + 1]).then_inc(s_max, 1)

            def do_split(c, which, i):
                if (c, which) == (0, 1):
                    split_part(dve, ch, c, which, i)

            does = {"norm": norm, "proj": proj, "out": out, "scores": scores, "split": do_split}
            ch.link(dve.memset(va[:, :, :, :], 1.0))
            dve.wait_ge(C.s_w2, 16 * C.N_W2)
            ch.link(dve.tensor_tensor(W.woT[:, :], W.woT[:, :], W.ls1[:, :], ALU.mult))
            for k in range(4):
                shared.dve_mult(dve, k)
            norm(0, 0)
            norm(0, 1)
            shared.dve_mult(dve, 4)
            shared.dve_add(dve, 0)
            norm(0, 2)
            shared.dve_mult(dve, 5)
            shared.dve_mult(dve, 6)
            shared.dve_mult(dve, 7)
            rest = early[early.index(("norm", 0, 2)) + 1:]
            added = rest.index(("split", 0, 1, 4)) + 1
            walk(rest[:added], does)
            shared.dve_add(dve, 1)
            walk(rest[added:], does)
            dve.memset(pO[:, :], 0.0).then_inc(s_va, 1)
            walk(main, does)

        @block.tensor
        def _(pe):
            ident = C.c[:, Consts.IDENT:Consts.IDENT + P]

            nth_norm = {}
            for e in timeline:
                if e[0] == "norm" and e[2] in (2, 4):
                    nth_norm[e[1], e[2]] = len(nth_norm) + 1

            def start(e):
                if e in proj_bank:
                    return
                if e == ("proj", 0, 3):
                    pe.wait_ge(s_free, job[("proj", 0, 0)] + 1)
                elif job[e] >= 1:
                    pe.wait_ge(s_free, job[e])

            def turn(c):
                start(("turn", c))
                pe.wait_ge(s_h, nth_norm[c, 2])
                for j in range(CH):
                    last = pe.transpose(pM[:, P * j:P * j + P], h[:, CH * c + j, :], ident)
                last.then_inc(s_full, 1)

            def turn2(c):
                start(("turn2", c))
                pe.wait_ge(s_h, nth_norm[c, 4])
                for j in range(CH):
                    last = pe.transpose(pM[:, P * j:P * j + P], h[:, CH * c + j, :], ident)
                last.then_inc(s_full, 1)

            def proj(c, s):
                start(("proj", c, s))
                pe.matmul(proj_bank.get(("proj", c, s), pM[:, :]), (W.wqT, W.wqrT, W.wkT, W.wkrT)[s][:, :],
                          hT[:, 512 * c:512 * c + 512], start=True, stop=True).then_inc(s_full, 1)

            def v(t):
                start(("v", t))
                pe.matmul(pM[:, 0:P], hT[:, P * t:P * t + P], W.wvT[:, :], start=True, stop=True
                          ).then_inc(s_full, 1)

            def max_turn(t):
                start(("max_turn", t))
                pe.wait_ge(s_ms, t + 1)
                pe.transpose(pM[:, 0:P // 2].bitcast(bf16)[0:3 * HEADS, :], mparts[:, t % 2, :], C.identb[:, :]
                             ).then_inc(s_full, 1)

            def out(t, s):
                start(("out", t, s))
                if s == 0:
                    pe.wait_ge(s_oe, t + 1)
                    for j in range(HEADS // 4):
                        last = pe.transpose(pM[:, P * j:P * j + P], oT[:, j, :], ident)
                    last.then_inc(s_full, 1)
                if s == 1:
                    pe.transpose(pM[:, 0:P], o, ident).then_inc(s_full, 1)
                if s == 2:
                    pe.matmul(pM[:, 0:P], oo, W.woT[:, :], start=True, stop=True).then_inc(s_full, 1)

            def key_tile(t):
                return slice(P * (t % (2 * CH)), P * (t % (2 * CH)) + P)

            def scores(k):
                t = k // SPT
                c, j = divmod(t, CH)
                if k % (SPT * CH) == 0:
                    for which in range(2):
                        pe.wait_ge(s_stack[which], STACKED * (c + 1))
                    pe.wait_ge(s_fill[c % 2], 16 * (3 + (c >= 2)))
                if k >= 3:
                    pe.wait_ge(s_max, SH * (k - 2))
                for i in range(SH):
                    head = (SH * k + i) % HEADS
                    q = qs[:, c % 2, head, P * j:P * j + P]
                    keys = ks[:, head, :, :].rearrange("p c n -> p (c n)")
                    dst = pS[k % 3][:, i, :]
                    if t % (2 * CH):
                        last = pe.matmul(dst, q, keys[:, key_tile(t - 1).start:key_tile(t).stop], start=True, stop=True)
                    else:
                        if t:
                            pe.matmul(dst[:, 0:P], q, keys[:, key_tile(t - 1)], start=True, stop=True)
                        last = pe.matmul(dst[:, P:], q, keys[:, key_tile(t)], start=True, stop=True)
                last.then_inc(s_S, 1)

            def turned(k):
                t = k // SPT
                c, j = divmod(t, CH)
                if k % SPT == 0:
                    pe.wait_ge(s_mr[t % 2], 48 * (t // 2 + 1))
                if k >= 3:
                    pe.wait_ge(s_exp, k - 2)
                sides = (0, 1) if t else (1,)
                dst = pT[k % 3]
                mask = C.masksT[:, :].rearrange("p (s q) -> p s q", q=P)[:, sides[0]:, :]
                pe.matmul(dst[:, :, sides[0]:, :], C.identb[:, :],
                          mask.unsqueeze(1).to_broadcast([P, SH, len(sides), P]), start=True, stop=False)
                for i in range(SH):
                    head = (SH * k + i) % HEADS
                    keys = ks[:, head, :, :].rearrange("p c n -> p (c n)")
                    for s in sides:
                        last = pe.matmul(dst[:, i, s, :], keys[:, key_tile(t - 1 + s)],
                                         qs[:, c % 2, head, P * j:P * j + P], start=False,
                                         stop=i == SH - 1 and s == 1)
                last.then_inc(s_T, 1)

            def values(k):
                t = k // SPT
                if k == 0:
                    pe.wait_ge(s_free, job[("v", 0)] + 1)
                if k % SPT == 0 and t >= 1:
                    pe.wait_ge(s_free, job[("v", t)] + 1)
                    pe.wait_ge(s_oe, t)
                pe.wait_ge(s_exp, k + 1)
                for i in range(SH):
                    head = (SH * k + i) % HEADS
                    s, g = divmod(head, 4)
                    dst = pO[32 * g:32 * g + 2 * HD, P * s:P * s + P]
                    if t:
                        pe.matmul(dst, va[:, (t - 1) % 3, head, :], pt[:, k % 4, i, 0, :], start=True, stop=False)
                    last = pe.matmul(dst, va[:, t % 3, head, :], pt[:, k % 4, i, 1, :], start=t == 0, stop=True)
                last.then_inc(s_PV, 1)

            does = {"turn": turn, "proj": proj, "v": v, "max_turn": max_turn, "out": out,
                    "scores": scores, "turned": turned, "values": values, "turn2": turn2}
            for k in range(HC):
                shared.pe_up(pe, k)
            shared.pe_down(pe, 0)
            for k in range(HC, shared.steps - 1):
                shared.pe_up(pe, k)
            turn(0)
            shared.pe_up(pe, shared.steps - 1)
            pe.wait_ge(C.s_w2, 16 * C.N_W2)
            projected = early.index(("proj", 0, 3)) + 1
            walk(early[early.index(("turn", 0)) + 1:projected], does)
            shared.pe_down(pe, 1)
            walk(early[projected:], does)
            pe.wait_ge(shared.added, 2)
            walk(main, does)


def ffn(nc, C, W, x_sb, z):
    ctx = ExitStack()
    with ctx:
        def sb(name, shape, dt=fp32):
            return ctx.enter_context(nc.sbuf_tensor(f"ffn_{name}", shape, dt))

        def sem(name):
            return ctx.enter_context(nc.semaphore(f"ffn_{name}"))

        bank = [ctx.enter_context(nc.psum_tensor(f"ffn_bank{k}", [P, 512], fp32)) for k in range(8)]
        pT, pF, pY = bank[0:2], bank[2:6], bank[6:8]
        stats = sb("stats", [P, NT, 6])
        mv = sb("mv", [P, NT, 2])
        rstd = sb("rstd", [P, NT])
        h, hT = C.h, C.hT
        fT = sb("fT", [P, 2, HC, 512])
        s_v = sem("dve_chain")
        s_p = sem("pool_chain")
        s_var = sem("var_ready")
        s_rstd = sem("rstd_ready")
        s_h = sem("h_ready")
        s_tr = sem("h_transposed")
        s_hT = sem("hT_ready")
        s_w = sem("w2_scaled")
        s_xz = sem("residual_ready")
        s_up = sem("up_done")
        s_g = sem("gelu_done")
        s_dn = sem("down_done")
        s_add = sem("added")
        NK = NCH * HC
        norms = [NCH - 1] + list(range(NCH - 1))
        block = ctx.enter_context(nc.Block())

        @block.gpsimd
        def _(pool):
            ch = Chain(pool, s_p)

            def pow(n):
                lo = CH * norms[n]
                pool.wait_ge(s_var, n + 1)
                pool.tensor_tensor(rstd[:, lo:lo + CH], mv[:, lo:lo + CH, 1],
                                   C.c[:, Consts.HALF:Consts.HALF + CH], ALU.pow).then_inc(s_rstd, 1)

            def residual(g):
                xg = x_sb[:, CH * g:CH * g + CH, :]
                ch.link(pool.tensor_tensor(xg, xg, z[:, CH * g:CH * g + CH, :], ALU.add))
                pool.tensor_tensor(xg, xg, W.b2[:, :].unsqueeze(1).to_broadcast([P, CH, D]), ALU.add).then_inc(s_xz, 1)

            pow(0)
            ch.link(pool.tensor_tensor(W.b2[:, :], W.b2[:, :], W.ls2[:, :], ALU.mult))
            residual(0)
            residual(1)
            pow(1)
            residual(2)
            pow(2)
            residual(3)
            pow(3)

        @block.vector
        def _(dve):
            ch = Chain(dve, s_v)

            def norm(n, src):
                layer_norm(dve, ch, src, stats, mv, h, s_var, s_rstd, rstd, CH * norms[n], CH * norms[n] + CH, n, s_h)

            norm(0, z)
            dve.tensor_tensor(W.w2T[:, :, :], W.w2T[:, :, :], W.ls2[:, :].unsqueeze(1).to_broadcast([P, HC, D]),
                              ALU.mult).then_inc(s_w, 1)
            for g in range(NCH):
                dve.wait_ge(s_dn, g + 1)
                dve.wait_ge(s_xz, g + 1)
                xg = x_sb[:, CH * g:CH * g + CH, :]
                dve.tensor_tensor(xg, pY[g % 2][:, :].rearrange("p (t d) -> p t d", d=D), xg, ALU.add).then_inc(s_add, 1)
                if g < NCH - 1:
                    dve.wait_ge(s_add, g + 1)
                    norm(g + 1, x_sb)

        @block.scalar
        def _(act):
            def turned(n):
                g = norms[n]
                act.wait_ge(s_tr, n + 1)
                if n == 0:
                    act.activation(hT[:, 512 * g:512 * g + 512], pT[n % 2][:, :], ACT.Identity,
                                   scale=W.n2w[:, 0:1], bias=W.n2b[:, 0:1]).then_inc(s_hT, 1)
                else:
                    act.activation(hT[:, 512 * g:512 * g + 512], pT[n % 2][:, :], ACT.Copy).then_inc(s_hT, 1)

            for k in range(NK):
                g, c = divmod(k, HC)
                act.wait_ge(s_up, k + 1)
                if g >= 2:
                    act.wait_ge(s_dn, g - 1)
                act.activation(fT[:, g % 2, c, :], pF[c][:, :], ACT.Gelu, bias=W.b1[:, c:c + 1]).then_inc(s_g, 1)
                if k == HC + 1:
                    turned(0)
                if g >= 2 and c == HC - 1:
                    turned(g - 1)
            turned(NCH - 1)

        @block.tensor
        def _(pe):
            ident = C.c[:, Consts.IDENT:Consts.IDENT + P]

            def turn(n):
                pe.wait_ge(s_h, CH * n + CH)
                if n >= 2:
                    pe.wait_ge(s_hT, n - 1)
                for j in range(CH):
                    last = pe.transpose(pT[n % 2][:, P * j:P * j + P], h[:, CH * norms[n] + j, :], ident)
                last.then_inc(s_tr, 1)

            def down(g):
                pe.wait_ge(s_g, HC * g + HC)
                if g == 0:
                    pe.wait_ge(s_w, 1)
                if g >= 2:
                    pe.wait_ge(s_add, g - 1)
                for j in range(CH):
                    for c in range(HC):
                        last = pe.matmul(pY[g % 2][:, P * j:P * j + P], fT[:, g % 2, c, P * j:P * j + P],
                                         W.w2T[:, c, :], start=c == 0, stop=c == HC - 1)
                last.then_inc(s_dn, 1)

            for g in range(NCH):
                if g == NCH - 1:
                    pe.wait_ge(s_hT, 1)
                for c in range(HC):
                    if g >= 1:
                        pe.wait_ge(s_g, HC * (g - 1) + c + 1)
                    pe.matmul(pF[c][:, :], W.w1T[:, P * c:P * c + P], hT[:, 512 * g:512 * g + 512],
                              start=True, stop=True).then_inc(s_up, 1)
                    if g == 1 and c == 1:
                        turn(0)
                if g >= 2:
                    turn(g - 1)
                if g >= 1:
                    down(g - 1)
            down(NCH - 1)
            turn(NCH - 1)


class Shared:
    pass


def program(nc, A, out):
    ctx = ExitStack()
    with ctx:
        def sb(name, shape, dt=fp32):
            return ctx.enter_context(nc.sbuf_tensor(name, shape, dt))

        def sem(name):
            return ctx.enter_context(nc.semaphore(name))

        C, W = Shared(), Shared()
        stages = ("m1", "m2")
        C.hs_dram = {tag: nc.dram_tensor(f"{tag}_sorted_rows", [PAST + SEQ, D + 1], fp32).ap() for tag in stages}
        C.y_dram = {tag: nc.dram_tensor(f"{tag}_results", [SEQ + PAST, D], fp32).ap() for tag in stages}
        C.c = sb("consts", [P, Consts.WIDTH])
        C.before = sb("before", [P, P], bf16)
        C.ones = sb("ones", [P, P], bf16)
        C.s_const = sem("consts_loaded")
        C.s_w = [sem(f"{k}_weights_loaded") for k in ("router", "shared", "expert")]
        C.s_zero = sem("zeros_written")
        C.s_blanked = sem("blank_slots_written")
        C.s_zeroed = {tag: sem(f"{tag}_results_zeroed") for tag in stages}
        C.s_bits = sem("bf16_consts_ready")
        x_sb = sb("x_rows", [P, NT, D])
        C.h_numbered = sb("h_rows", [P, NT, D + 1])
        C.h = C.h_numbered[:, :, 0:D]
        C.ys = sb("expert_results", [P, 4, D])
        C.row_of = sb("row_of_slot", [P, NS], u32)
        C.y_ready = {tag: sem(f"{tag}_expert_y_ready") for tag in stages}
        C.y_stored = {tag: [sem(f"{tag}_y_stored{k}") for k in range(4)] for tag in ("m1", "m2")}
        C.gathered = {tag: [sem(f"{tag}_gathered{g}") for g in range(NCH)] for tag in ("m1", "m2")}
        C.hT = sb("moe_hT", [P, SEQ])
        C.prob = sb("prob", [P, NT])
        W.Wr = sb("Wr", [D, NE])
        W.Wus = sb("Wu_s", [D, HID])
        W.Wgs = sb("Wg_s", [D, HID])
        W.Wds = sb("Wd_s", [P, HC, D])
        W.Wu = sb("Wu", [D, NX * HID])
        W.Wg = sb("Wg", [D, NX * HID])
        W.Wd = sb("Wd", [P, NX * HID])

        def load_consts(eng):
            eng.dma_start(C.c[:, :], A["const_table"]).then_inc(C.s_const, 16)
            eng.dma_start(C.masks32[:, :], A["mask_table"]).then_inc(C.s_mask, 16)

        def load_moe_weights(eng, upto):
            for kind, dst, src in (
                (0, W.Wr[:, :], A["L0_ffn_Wr"]),
                (1, W.Wus[:, :], A["L0_ffn_Wu_s"]),
                (1, W.Wgs[:, :], A["L0_ffn_Wg_s"]),
                (1, W.Wds[:, :, :], A["L0_ffn_Wd_s"].rearrange("(c p) d -> p c d", p=P)),
                (2, W.Wg[:, :].rearrange("p (e n) -> p e n", e=NX), A["L0_ffn_Wg"].rearrange("e p n -> p e n")),
                (2, W.Wu[:, :].rearrange("p (e n) -> p e n", e=NX), A["L0_ffn_Wu"].rearrange("e p n -> p e n")),
                (2, W.Wd[:, :].rearrange("p (e c d) -> p e c d", e=NX, c=HC),
                 A["L0_ffn_Wd"].rearrange("e (c p) d -> p e c d", p=P)),
            ):
                if (kind == 2) == (upto == 3):
                    eng.dma_start(dst, src).then_inc(C.s_w[kind], 16)

        def load_block_weights(eng):
            def row(name):
                return A[name].rearrange("(a n) -> a n", a=1).to_broadcast([P, D])

            def column(name):
                return A[name].rearrange("(p a) -> p a", a=1)

            for dst, src in (
                (W.wqT[:, :], A["wqT"]), (W.wqrT[:, :], A["wqrT"]), (W.wkT[:, :], A["wkT"]),
                (W.wkrT[:, :], A["wkrT"]), (W.wvT[:, :], A["wvT"]), (W.woT[:, :], A["woT"]),
                (W.w1T[:, :], A["w1T"]), (W.w2T[:, :, :], A["w2T"].rearrange("(c p) d -> p c d", p=P)),
                (W.b1[:, :], A["b1_columns"]),
                (W.b2[:, :], row("L0_attn_b2")), (W.ls1[:, :], row("L0_attn_ls1")), (W.ls2[:, :], row("L0_attn_ls2")),
                (W.n1w[:, :], column("L0_attn_norm1_w")), (W.n1b[:, :], column("L0_attn_norm1_b")),
                (W.n2w[:, :], column("L0_attn_norm2_w")), (W.n2b[:, :], column("L0_attn_norm2_b")),
            ):
                eng.dma_start(dst, src).then_inc(C.s_w2, 16)
        def make_consts(nc, dve):
            dve.memset(C.zeros[:, :, :], 0.0).then_inc(C.s_zero, 1)
            dve.wait_ge(C.s_const, 16)
            dve.tensor_copy(C.h_numbered[:, :, D:D + 1].bitcast(u32),
                            C.c[:, Consts.ROW:Consts.ROW + NT].unsqueeze(2))
            dve.tensor_copy(C.before[:, :], C.c[:, Consts.BEFORE:Consts.BEFORE + P]).then_inc(C.s_bits, 1)
            dve.memset(C.ones[:, :], 1.0).then_inc(C.s_bits, 1)
            dve.tensor_copy(C.identb[:, :], C.c[:, Consts.IDENT:Consts.IDENT + P])
            dve.wait_ge(C.s_mask, 16)
            dve.tensor_copy(C.masksT[:, :], C.masks32[:, 2 * P:4 * P]).then_inc(C.s_bits, 1)

        C.zeros = sb("zeros", [P, 1, D])
        C.s_mask = sem("masks_loaded")
        C.s_w2 = sem("block_weights_loaded")
        C.masks32 = sb("masks32", [P, 4 * P])
        C.masksT = sb("masksT", [P, 2 * P], bf16)
        C.identb = sb("identb", [P, P], bf16)
        W.wqT, W.wqrT, W.wkT, W.wkrT, W.wvT, W.woT = (
            sb(n + "_sb", [D, D]) for n in ("wqT", "wqrT", "wkT", "wkrT", "wvT", "woT"))
        W.w1T = sb("w1T_sb", [D, HID])
        W.w2T = sb("w2T_sb", [P, HC, D])
        W.b1 = sb("b1_sb", [P, HC])
        W.b2, W.ls1, W.ls2 = (sb(n + "_rows", [P, D]) for n in ("b2", "ls1", "ls2"))
        W.n1w, W.n1b, W.n2w, W.n2b = (sb(n + "_col", [D, 1]) for n in ("n1w", "n1b", "n2w", "n2b"))
        C.N_W2 = 16
        z = sb("z_rows", [P, NT, D])
        C.load_consts, C.load_moe_weights, C.load_block_weights, C.make_consts = (
            load_consts, load_moe_weights, load_block_weights, make_consts)

        x_in = A["L0_attn_x"].rearrange("b s d -> (b s) d")
        x_out = out.rearrange("b s d -> (b s) d")
        moe(nc, C, W, x_sb, z, "m1", x_in, None)
        attention(nc, A, C, W, x_sb, z)
        ffn(nc, C, W, x_sb, z)
        moe(nc, C, W, x_sb, z, "m2", None, x_out)


_INS = ["L0_attn_x", "L0_attn_norm1_w", "L0_attn_norm1_b", "L0_attn_norm2_w", "L0_attn_norm2_b",
        "L0_attn_b2", "L0_attn_ls1", "L0_attn_ls2",
        "L0_ffn_Wr", "L0_ffn_Wu", "L0_ffn_Wg", "L0_ffn_Wd", "L0_ffn_Wu_s", "L0_ffn_Wg_s", "L0_ffn_Wd_s"]


def inputs_for_launch(inputs):
    a = {n: np.ascontiguousarray(inputs[n]) for n in _INS}
    turned = np.concatenate([np.arange(HD // 2, HD), np.arange(HD // 2)])
    plain = (np.arange(HEADS)[None, :] * HD + np.arange(HD)[:, None]).reshape(-1)
    rows = (np.arange(HEADS)[None, :] * HD + turned[:, None]).reshape(-1)
    wq, wk = np.asarray(inputs["L0_attn_wq"]), np.asarray(inputs["L0_attn_wk"])
    for n, w in (("wqT", wq[plain]), ("wqrT", wq[rows]), ("wkT", wk[plain]), ("wkrT", wk[rows]),
                 ("wvT", np.asarray(inputs["L0_attn_wv"])), ("woT", np.asarray(inputs["L0_attn_wo"])),
                 ("w1T", np.asarray(inputs["L0_attn_w1"])), ("w2T", np.asarray(inputs["L0_attn_w2"]))):
        a[n] = np.ascontiguousarray(w.T)
    a["b1_columns"] = np.ascontiguousarray(np.asarray(inputs["L0_attn_b1"]).reshape(HC, P).T)
    a["stack_fill"] = np.repeat(np.array([[0x0000], [0xBF80]], np.uint16), HEADS * 512, axis=1)
    a["const_table"], a["cos_table"], a["sin_table"], a["mask_table"] = const_tables()
    return a


def kernel(**inputs):
    import concourse.bacc as bacc
    from concourse.bass_utils import run_bass_kernel_spmd

    nc = bacc.Bacc("TRN2", target_bir_lowering=False, num_devices=1)
    arrays = inputs_for_launch(inputs)
    args = {n: nc.dram_tensor(n, a.shape, mybir.dt.from_np(a.dtype), kind="ExternalInput").ap()
            for n, a in arrays.items()}
    out = nc.dram_tensor("out", (1, SEQ, D), fp32, kind="ExternalOutput").ap()
    program(nc, args, out)
    r = run_bass_kernel_spmd(nc, [arrays], core_ids=[0])
    return r.results[0]["out"]
```
